# Optimizing a Trainium2 kernel written in Bass

```python
import numpy as np
import jax
import jax.numpy as jnp

def _softmax(x, axis=-1):
    return jax.nn.softmax(x, axis=axis)

def _gelu(x):
    return jax.nn.gelu(x, approximate=True)

def _silu(x):
    return jax.nn.silu(x)

def _sigmoid(x):
    return jax.nn.sigmoid(x)

def _layernorm(x, axis=-1, eps=1e-05):
    m = jnp.mean(x, axis=axis, keepdims=True)
    v = jnp.var(x, axis=axis, keepdims=True)
    return (x - m) / jnp.sqrt(v + eps)

def _scatter_add(tgt, idx, src, axis=0):
    return tgt.at[idx].add(src)

def _segment_sum(src, seg, n):
    return jax.ops.segment_sum(src, seg, n)
kernel_name = 'mk_adaln_d1_jaxref_r4_5f8761'

def setup_inputs(seed: int=0):
    np.random.seed(seed)
    _w = jnp.asarray

    def _L0_attn_setup():
        import jax, jax.numpy as jnp
        import numpy as np
        D_MODEL = 256
        N_HEADS = 32
        HEAD_DIM = D_MODEL // N_HEADS
        EPS = 1e-05
        key = jax.random.key(seed)
        ks = jax.random.split(key, 6)
        B, S = (2, 512)
        scale = 1.0 / np.sqrt(D_MODEL)
        return {'x': jax.random.normal(ks[0], (B, S, D_MODEL), dtype=jnp.float32), 'Wqkv_w': jax.random.normal(ks[1], (3 * D_MODEL, D_MODEL), dtype=jnp.float32) * scale, 'Wqkv_b': jax.random.normal(ks[2], (3 * D_MODEL,), dtype=jnp.float32) * 0.01, 'gn_w': jnp.ones((D_MODEL,), dtype=jnp.float32), 'gn_b': jnp.zeros((D_MODEL,), dtype=jnp.float32), 'out_w': jax.random.normal(ks[3], (D_MODEL, D_MODEL), dtype=jnp.float32) * scale, 'out_b': jax.random.normal(ks[4], (D_MODEL,), dtype=jnp.float32) * 0.01}
    _L0_attn_in = _L0_attn_setup()

    def _L0_ffn_setup():
        import jax, jax.numpy as jnp
        import numpy as np
        E, K, H, F, R = (8, 2, 256, 512, 64)
        B, S = (2, 512)
        key = jax.random.key(seed)
        k0, k1, k2, k3, k4 = jax.random.split(key, 5)
        return {'hidden_states': jax.random.normal(k0, (B, S, H), dtype=jnp.float32), 'W_A': jax.random.normal(k1, (E, R, H), dtype=jnp.float32) * 0.02, 'W_B': jax.random.normal(k2, (E, F, R), dtype=jnp.float32) * 0.02, 'W_up': jax.random.normal(k3, (E, F, H), dtype=jnp.float32) * 0.02, 'W_down': jax.random.normal(k4, (E, H, F), dtype=jnp.float32) * 0.02}
    _L0_ffn_in = _L0_ffn_setup()
    _L0_c = _w((lambda *s: np.random.randn(*s).astype(np.float32) * 0.05)(4, 256))
    _L0_wmod = _w((lambda *s: np.random.randn(*s).astype(np.float32) * 0.05)(256, 6 * 256) * 256 ** (-0.5))
    _d = {'L0_attn_x': _L0_attn_in['x'], 'L0_attn_Wqkv_w': _L0_attn_in['Wqkv_w'], 'L0_attn_Wqkv_b': _L0_attn_in['Wqkv_b'], 'L0_attn_gn_w': _L0_attn_in['gn_w'], 'L0_attn_gn_b': _L0_attn_in['gn_b'], 'L0_attn_out_w': _L0_attn_in['out_w'], 'L0_attn_out_b': _L0_attn_in['out_b'], 'L0_ffn_W_A': _L0_ffn_in['W_A'], 'L0_ffn_W_B': _L0_ffn_in['W_B'], 'L0_ffn_W_up': _L0_ffn_in['W_up'], 'L0_ffn_W_down': _L0_ffn_in['W_down'], 'L0_c': _L0_c, 'L0_wmod': _L0_wmod}
    _x0 = _d['L0_attn_x']
    _d['L0_attn_x'] = jax.random.normal(jax.random.fold_in(jax.random.key(seed), 1), (4, 1024, 256), dtype=_x0.dtype)
    del _x0
    return _d

def reference(L0_attn_x, L0_attn_Wqkv_w, L0_attn_Wqkv_b, L0_attn_gn_w, L0_attn_gn_b, L0_attn_out_w, L0_attn_out_b, L0_ffn_W_A, L0_ffn_W_B, L0_ffn_W_up, L0_ffn_W_down, L0_c, L0_wmod):

    def _L0_attn_ref(x, Wqkv_w, Wqkv_b, gn_w, gn_b, out_w, out_b):
        import jax, jax.numpy as jnp
        import numpy as np
        D_MODEL = 256
        N_HEADS = 32
        HEAD_DIM = D_MODEL // N_HEADS
        EPS = 1e-05
        B, S, Dm = x.shape
        H, Dh = (N_HEADS, HEAD_DIM)
        qkv = x @ Wqkv_w.T + Wqkv_b
        qkv = qkv.reshape(B, S, 3, H, Dh)
        q, k, v = (qkv[:, :, 0], qkv[:, :, 1], qkv[:, :, 2])
        a = jnp.einsum('bthd,bshd->bhts', q, k)
        ctx = jnp.einsum('bhts,bshd->bthd', a, v)
        g = ctx.transpose(0, 2, 3, 1)
        mean = g.mean(axis=(2, 3), keepdims=True)
        var = ((g - mean) ** 2).mean(axis=(2, 3), keepdims=True)
        gh = (g - mean) * jax.lax.rsqrt(var + EPS)
        gh = gh * gn_w.reshape(H, Dh, 1) + gn_b.reshape(H, Dh, 1)
        ctx = gh.transpose(0, 3, 1, 2).reshape(B, S, Dm)
        return ctx @ out_w.T + out_b

    def _L0_ffn_ref(hidden_states, W_A, W_B, W_up, W_down):
        import jax, jax.numpy as jnp
        import numpy as np
        E, K, H, F, R = (8, 2, 256, 512, 64)
        B, S = (2, 512)
        orig_shape = hidden_states.shape
        x = hidden_states.reshape(-1, orig_shape[-1])
        num_experts = W_A.shape[0]
        gate_hidden = jnp.einsum('nh,erh->ner', x, W_A)
        scores = jnp.sqrt(jnp.sum(gate_hidden * gate_hidden, axis=-1))
        topk_scores, topk_idx = jax.lax.top_k(scores, K)
        topk_w = jax.nn.softmax(topk_scores, axis=-1)
        w_full = jnp.sum(jax.nn.one_hot(topk_idx, num_experts, dtype=topk_w.dtype) * topk_w[..., None], axis=1)
        g = jnp.einsum('ner,efr->nef', gate_hidden, W_B)
        up = jnp.einsum('nh,efh->nef', x, W_up)
        y = jnp.einsum('nef,ehf->neh', jax.nn.silu(g) * up, W_down)
        out = jnp.einsum('neh,ne->nh', y, w_full)
        return out.reshape(orig_shape)
    x = L0_attn_x
    mod = (_silu(L0_c) @ L0_wmod).reshape(L0_c.shape[0], 6, 1, -1)
    sa, ca, ga, sb, cb, gb = (mod[:, 0], mod[:, 1], mod[:, 2], mod[:, 3], mod[:, 4], mod[:, 5])
    ga = (2 * (ga >= 0) - 1) * jnp.maximum(jnp.abs(ga), 0.25)
    gb = (2 * (gb >= 0) - 1) * jnp.maximum(jnp.abs(gb), 0.25)
    h = _layernorm(x, axis=-1) * (1 + ca) + sa
    x = x + ga * _L0_attn_ref(h, L0_attn_Wqkv_w, L0_attn_Wqkv_b, L0_attn_gn_w, L0_attn_gn_b, L0_attn_out_w, L0_attn_out_b)
    h = _layernorm(x, axis=-1) * (1 + cb) + sb
    x = x + gb * _L0_ffn_ref(h, L0_ffn_W_A, L0_ffn_W_B, L0_ffn_W_up, L0_ffn_W_down)
    return x

_drawn_inputs = setup_inputs


def setup_inputs(seed=0):
    import zlib

    import numpy as np

    out = dict(_drawn_inputs(seed))
    spreads = {'L0_attn_gn_w': (1.0, 0.2), 'L0_attn_gn_b': (0.0, 0.32)}
    factors = {'L0_attn_Wqkv_b': 8.0,
     'L0_attn_out_b': 8.0,
     'L0_ffn_W_A': 8.0,
     'L0_ffn_W_B': 8.0,
     'L0_ffn_W_up': 8.0,
     'L0_ffn_W_down': 8.0}
    for name, (base, spread) in spreads.items():
        noise = np.random.default_rng([zlib.crc32(name.encode()), seed]).standard_normal(out[name].shape)
        drawn = base * np.exp(spread * noise) if base else spread * noise
        out[name] = jnp.asarray(drawn.astype(out[name].dtype))
    for name, factor in factors.items():
        out[name] = (out[name] * factor).astype(out[name].dtype)
    return out
```

```python
from contextlib import ExitStack

import concourse.bass as bass
from concourse import mybir


P = 128
ALU = mybir.AluOpType
ACT = mybir.ActivationFunctionType
F32 = mybir.dt.float32
F32R = mybir.dt.float32r
I32 = mybir.dt.int32
U32 = mybir.dt.uint32
AX_X = mybir.AxisListType.X

BATCH, SEQ, D = 4, 1024, 256
HEADS = 32
HEAD = D // HEADS
EXPERTS, TOPK, RANK, FF = 8, 2, 64, 512
EPS = 1e-5
GATE_MIN = 0.25

HC = D // P
FC = FF // P
TB = SEQ // P
TILES = BATCH * TB
TOKENS = BATCH * SEQ
ETILES = (TOPK * TOKENS + EXPERTS * (P - 1)) // P
XBUFS = 4

A_W = HC * FF
B_W = EXPERTS * FF
UP_W = EXPERTS * HC * FF
G_W = A_W + B_W + UP_W
D_W = EXPERTS * FC * D
G_CHUNK = G_W // TILES
D_CHUNK = D_W // TILES
QUAD = 4
LOG_P = P.bit_length() - 1
VALUE_PAD = TOPK * TILES

POOL_CONSTS = 8
ZEROS_SET = 4
MOD_STEPS = 11
STAT_MU, STAT_SQ, STAT_SCALE, STAT_SHIFT = 2, 8, 10, 12
ROUTE_CONSTS = 7


class Region:

    def __init__(self, nc, base, end):
        self.nc, self.at, self.end = nc, base, end

    def take(self, name, shape, dt=F32):
        size = 4
        for n in shape[1:]:
            size *= n
        t = self.nc.alloc_sbuf_tensor_at(name, shape, dt, offset=self.at)
        self.at += -(-size // 64) * 64
        assert self.at <= self.end, (name, self.at, self.end)
        return t

    def rewind(self, at):
        self.at = at


def build(nc, x, c_t, wmod, wqkv_t, wq, bq_cols, bkv_row, gn_cols, wo_t, out_b, wg, wd, out):
    h2_dram = nc.dram_tensor("h2_rows", [TOKENS, D], F32).ap()
    x2_dram = nc.dram_tensor("x2_rows", [BATCH, P, TB, D], F32).ap()
    y_dram = nc.dram_tensor("y_rows", [TOPK * TOKENS + P, D], F32).ap()
    mod_dram = nc.dram_tensor("mod_rows", [BATCH, 4, D], F32).ap()

    x_v = x.rearrange("b (p k) d -> p b k d", p=P)
    out_v = out.rearrange("b (p k) d -> p b k d", p=P)
    x2_v = x2_dram.rearrange("b p k d -> p b k d")
    h2_v = h2_dram.rearrange("(b p k) d -> p b k d", b=BATCH, p=P)
    y_v = y_dram[0:TOPK * TOKENS, :].rearrange("(c b p k) d -> p c b k d", c=TOPK, b=BATCH, p=P)

    with ExitStack() as ctx:
        def sem(name):
            return ctx.enter_context(nc.semaphore(name))

        ps = ctx.enter_context(nc.psum_tensor("ps", [P, 8, 512], F32))
        bank = [ps[:, i, :] for i in range(8)]

        base = -(-nc.sbuf_base // 64) * 64
        end = nc.sbuf_usable_end // 64 * 64
        r1 = Region(nc, base, base + 2 * 4 * D_W)
        gram = r1.take("gram", [P, BATCH, HC, D + 1])
        p1 = r1.take("p1", [P, BATCH, HC, D])
        kv = r1.take("kv", [P, BATCH, HC, P])
        a_cn = r1.take("a_cn", [P, BATCH, HC, D])
        a_nc = r1.take("a_nc", [P, BATCH, HC, D])
        bkv = r1.take("bkv", [1, BATCH, 2 * D])
        wqkv_sb = r1.take("wqkv_sb", [P, HC, 3 * D])
        wq_sb = r1.take("wq_sb", [P, HC, D])
        wo_sb = r1.take("wo_sb", [P, HC, D])
        ga_bc = r1.take("ga_bc", [P, BATCH, D])
        r1.rewind(base)
        wd_hi = r1.take("wd_hi", [P, D_W], F32R)
        wd_lo = r1.take("wd_lo", [P, D_W], F32R)
        r1.rewind(base)
        fin_y0 = r1.take("fin_y0", [P, 2, QUAD, D])
        fin_y1 = r1.take("fin_y1", [P, 2, QUAD, D])
        fin_x2 = r1.take("fin_x2", [P, 2, QUAD, D])
        fin_u = r1.take("fin_u", [P, 2, QUAD, D])
        fin_v = r1.take("fin_v", [P, 2, QUAD, D])
        gb_bc = r1.take("gb_bc", [P, BATCH, D])

        r2 = Region(nc, base + 2 * 4 * D_W, end)
        wg_hi = r2.take("wg_hi", [P, G_W], F32R)
        wg_lo = r2.take("wg_lo", [P, G_W], F32R)
        ident = r2.take("ident", [P, P])
        ones_col = r2.take("ones_col", [P, 1])
        eps_col = r2.take("eps_col", [P, 1])
        weight = r2.take("weight", [P, TOPK, TILES])
        ssum = r2.take("ssum", [P, TILES, EXPERTS])
        regional = r2.at

        wmod_sb = r2.take("wmod_sb", [P, HC, 6 * D])
        r2.rewind(regional)
        c_mat = r2.take("c_mat", [P, BATCH, HC, D])
        c0_bc = r2.take("c0_bc", [P, BATCH, D])
        rstd1 = r2.take("rstd1", [P, TILES])
        nmr1 = r2.take("nmr1", [P, TILES])
        bn = r2.take("bn", [P, 2, 6])
        mv = r2.take("mv", [P, 2, 2])
        std = r2.take("std", [P, 2])
        xbuf = r2.take("xbuf", [P, XBUFS, D])
        xhat = r2.take("xhat", [P, 2, D + 1])
        per_pass = r2.at
        stage_g = r2.take("stage_g", [P, 2, G_CHUNK])
        headmask = r2.take("headmask", [P, P])
        headavg = r2.take("headavg", [P, P])
        sc_cols = r2.take("sc_cols", [P, 2 * HC, BATCH])
        bq_c = r2.take("bq_c", [P, HC])
        bq_all = r2.take("bq_all", [P, HC, BATCH])
        gn_c = r2.take("gn_c", [P, 2, HC])
        outb_bc = r2.take("outb_bc", [P, D])
        xs_raw = r2.take("xs_raw", [P, BATCH, HC])
        g12 = r2.take("g12", [P, BATCH, P])
        cols = r2.take("cols", [P, BATCH, 6])
        stat = r2.take("stat", [P, 8, BATCH, HC])
        t_ones = r2.take("t_ones", [P, 2, HC, P])
        mod_start = r2.at
        c_sb = r2.take("c_sb", [P, HC, BATCH])
        cs_sb = r2.take("cs_sb", [P, HC, BATCH])
        mod_sb = r2.take("mod_sb", [BATCH, 4 * D])
        mod_sign = r2.take("mod_sign", [BATCH, D])
        mod_abs = r2.take("mod_abs", [BATCH, D])
        brow = r2.take("brow", [1, 2 * D])
        r2.rewind(mod_start)
        xs_row = r2.take("xs_row", [1, BATCH, D])
        rv_row = r2.take("rv_row", [1, BATCH, D])
        r2.rewind(per_pass)
        stage_d = r2.take("stage_d", [P, 2, D_CHUNK])
        sb_bc = r2.take("sb_bc", [P, BATCH, D])
        cb_bc = r2.take("cb_bc", [P, BATCH, D])
        xt = r2.take("xt", [P, HC, P])
        xn2 = r2.take("xn2", [P, 2, D])
        h2 = r2.take("h2", [P, 2, D])
        hd_hi = r2.take("hd_hi", [P, 2, HC, P], F32R)
        hd_lo = r2.take("hd_lo", [P, 2, HC, P], F32R)
        bn2 = r2.take("bn2", [P, 2, 6])
        mv2 = r2.take("mv2", [P, 2, 2])
        std2 = r2.take("std2", [P, 2])
        rstd2 = r2.take("rstd2", [P, 2])
        nmr2 = r2.take("nmr2", [P, 2])
        r2.rewind(regional)
        top = r2.take("top", [P, TILES, 8])
        topi = r2.take("topi", [P, TILES, 8], U32)
        topf = r2.take("topf", [P, TOPK, TILES])
        table = r2.take("table", [P, ETILES])
        dest = r2.take("dest", [P, ETILES], I32)
        token = r2.take("token", [P, ETILES], I32)
        tile_expert = r2.take("tile_expert", [1, ETILES + 4], I32)
        experts_start = r2.at
        pick = r2.take("pick", [P, TOPK, TILES, EXPERTS])
        both = r2.take("both", [P, TILES, EXPERTS])
        total = r2.take("total", [P, EXPERTS, TILES])
        cum = r2.take("cum", [P, EXPERTS, TILES])
        zeros = r2.take("zeros", [P, EXPERTS * TILES])
        slot_m = r2.take("slot_m", [P, TILES, EXPERTS])
        slot_k = r2.take("slot_k", [P, TOPK, TILES, EXPERTS])
        slot = r2.take("slot", [P, TOPK * TILES])
        slot_i = r2.take("slot_i", [P, 3, TOPK * TILES], I32)
        slot_f = r2.take("slot_f", [P, 2, TOPK * TILES])
        small = r2.take("small", [P, 8, EXPERTS])
        small_i = r2.take("small_i", [P, 2, EXPERTS], I32)
        upper = r2.take("upper", [P, P])
        iota_row = r2.take("iota_row", [P, P])
        ones_m = r2.take("ones_m", [P, P])
        value = r2.take("value", [P, TOPK * TILES + 1])
        in_row = r2.take("in_row", [P, 4, P])
        in_col = r2.take("in_col", [P, 4, ETILES])
        expert_f = r2.take("expert_f", [P, 2, ETILES + 1])
        pad = r2.take("pad", [P, 2, ETILES])
        r2.rewind(experts_start)
        tok_ix = r2.take("tok_ix", [P, 2], I32)
        dst_ix = r2.take("dst_ix", [P, 2], I32)
        rows = r2.take("rows", [P, 2, D])
        h_hi = r2.take("h_hi", [P, 2, HC, P], F32R)
        h_lo = r2.take("h_lo", [P, 2, HC, P], F32R)
        gh = r2.take("gh", [P, 2, 2, RANK])
        gt = r2.take("gt", [P, 2, P], F32R)
        silu = r2.take("silu", [P, FF])
        act_ = r2.take("act_", [P, 2, FF])
        act_hi = r2.take("act_hi", [P, FC, P], F32R)
        act_lo = r2.take("act_lo", [P, FC, P], F32R)
        y = r2.take("y", [P, 2, D])

        pool_past = sem("pool_past")
        const_set = sem("const_set")
        zero_set = sem("zero_set")
        cond_in = sem("cond_in")
        attw_in = sem("attw_in")
        cond_act = sem("cond_act")
        mod_prod = sem("mod_prod")
        mod_cols = sem("mod_cols")
        mod_step = sem("mod_step")
        mod_out = sem("mod_out")
        ga_in = sem("ga_in")
        bias_prod = sem("bias_prod")
        bias_set = sem("bias_set")
        x1_in = [sem(f"x1_in{i}") for i in range(XBUFS)]
        wg_in = [sem(f"wg_in{i}") for i in range(2)]
        bn_done = sem("bn_done")
        mv_done = sem("mv_done")
        std_done = sem("std_done")
        rstd_done = sem("rstd_done")
        nmr_done = sem("nmr_done")
        xhat_done = sem("xhat_done")
        wghi_done = sem("wghi_done")
        wglo_done = sem("wglo_done")
        gram_done = sem("gram_done")
        att_pe = {n: sem(f"pe_{n}") for n in ("g21", "p1", "rv", "kv", "acn", "anc", "prod", "cols", "c", "c0")}
        att_ev = {n: sem(f"ev_{n}") for n in ("gram_a", "gram_v", "g21", "p1", "rv", "kv", "acn", "anc", "prod",
                                              "cols", "scaled", "ones", "c", "c0a", "c0")}
        stat_step = sem("stat_step")
        stat_pe = sem("stat_pe")
        stat_std = sem("stat_std")
        x2_in = [sem(f"x2_in{i}") for i in range(XBUFS)]
        wd_in = [sem(f"wd_in{i}") for i in range(2)]
        scb_in = sem("scb_in")
        x2_out = [sem(f"x2_out{i}") for i in range(XBUFS)]
        h2_out = [sem(f"h2_out{i}") for i in range(2)]
        d_xhat = sem("d_xhat")
        d_xc = sem("d_xc")
        d_tx = sem("d_tx")
        d_xt = sem("d_xt")
        d_c = sem("d_c")
        d_x2 = sem("d_x2")
        d_bn = sem("d_bn")
        d_mv = sem("d_mv")
        d_std = sem("d_std")
        d_rstd = sem("d_rstd")
        d_nmr = sem("d_nmr")
        d_xn = sem("d_xn")
        d_h2m = sem("d_h2m")
        d_h2 = sem("d_h2")
        d_th = sem("d_th")
        d_hi = sem("d_hi")
        d_lo = sem("d_lo")
        d_gate = sem("d_gate")
        d_sq = sem("d_sq")
        d_sum = sem("d_sum")
        d_whi = sem("d_whi")
        d_wlo = sem("d_wlo")
        scores_done = sem("scores_done")
        route_pool = sem("route_pool")
        route_step = sem("route_step")
        pick_done = sem("pick_done")
        diff_done = sem("diff_done")
        exp_done = sem("exp_done")
        count_pe = sem("count_pe")
        onehot_done = sem("onehot_done")
        table_pe = sem("table_pe")
        route_done = sem("route_done")
        e_tix = sem("e_tix")
        e_dix = sem("e_dix")
        e_rows = [sem(f"e_rows{i}") for i in range(2)]
        e_out = [sem(f"e_out{i}") for i in range(2)]
        e_th = sem("e_th")
        e_hi = sem("e_hi")
        e_lo = sem("e_lo")
        e_up = sem("e_up")
        e_gh = sem("e_gh")
        e_ghs = sem("e_ghs")
        e_tg = sem("e_tg")
        e_gthi = sem("e_gthi")
        e_gtlo = sem("e_gtlo")
        e_g = sem("e_g")
        e_silu = sem("e_silu")
        e_act = sem("e_act")
        e_ta = sem("e_ta")
        e_ahi = sem("e_ahi")
        e_alo = sem("e_alo")
        e_y = sem("e_y")
        e_ys = sem("e_ys")
        gb_in = sem("gb_in")
        f_in = [sem(f"f_in{i}") for i in range(2)]
        f_u = sem("f_u")
        f_v = sem("f_v")
        f_w = sem("f_w")
        f_o = sem("f_o")
        f_out = [sem(f"f_out{i}") for i in range(2)]

        def gram_copies(b):
            g = ps[:, 2 * b:2 * b + 2, :]
            return ((g12[:, b, :], g[:, 0, P:D]), (xs_raw[:, b, 0:1], g[:, 0, D:D + 1]),
                    (xs_raw[:, b, 1:2], g[:, 1, P:P + 1]))

        def gram_scalings(b):
            g = ps[:, 2 * b:2 * b + 2, :]
            return ((gram[:, b, 0, :], g[:, 0, 0:D + 1], sc_cols[:, HC, b:b + 1]),
                    (gram[:, b, 1, P:D + 1], g[:, 1, 0:P + 1], sc_cols[:, HC + 1, b:b + 1]))

        def token_steps(eng, step, lag):
            for k in range(TB):
                step(0, k, lambda n, k=k: k >= n)
            with eng.Fori(1, BATCH) as b:
                for k in range(TB):
                    step(b, k, lambda n: True)
            for k in range(lag):
                step(BATCH, k, lambda n, k=k: n > k)

        PEEL = 5
        assert (ETILES - PEEL) % 2 == 0

        def expert_steps(eng, step, lag):
            for s in range(PEEL):
                step(s, s % 2, lambda n, s=s: s >= n, lambda n, s=s: (s - n) // 2)
            with eng.Fori(0, (ETILES - PEEL) // 2) as m:
                for j in range(2):
                    step(m * 2 + (PEEL + j), (PEEL + j) % 2, lambda n: True,
                         lambda n, j=j: m + (PEEL + j - n) // 2)
            for s in range(ETILES, ETILES + lag):
                step(s, s % 2, lambda n, s=s: s - n < ETILES, lambda n, s=s: (s - n) // 2)

        block = ctx.enter_context(nc.Block())

        @block.sync
        def _(sp):
            def first_pass(b, k, have):
                t = b * TB + k
                if have(XBUFS):
                    sp.wait_ge(xhat_done, t - XBUFS + 1)
                sp.dma_start(xbuf[:, k % XBUFS:k % XBUFS + 1, :], x_v[:, bass.ds(b, 1), k, :])\
                  .then_inc(x1_in[k % XBUFS], 16)
                if have(2):
                    sp.wait_ge(wglo_done, t - 1)
                sp.dma_start(stage_g[:, k % 2, :], wg[:, bass.ds(t * G_CHUNK, G_CHUNK)])\
                  .then_inc(wg_in[k % 2], 16)

            token_steps(sp, first_pass, 0)

            sp.wait_ge(att_ev["c0"], BATCH)
            sp.dma_start(sb_bc[:], mod_dram[:, 1, :].partition_broadcast(P)).then_inc(scb_in, 16)
            sp.dma_start(cb_bc[:], mod_dram[:, 2, :].partition_broadcast(P)).then_inc(scb_in, 16)

            def second_pass(b, k, have):
                t = b * TB + k
                if have(0):
                    if have(XBUFS):
                        sp.wait_ge(x2_out[k % XBUFS], 16 * (TB // XBUFS * b + k // XBUFS))
                    sp.dma_start(xbuf[:, k % XBUFS:k % XBUFS + 1, :], x_v[:, bass.ds(b, 1), k, :])\
                      .then_inc(x2_in[k % XBUFS], 16)
                    if have(2):
                        sp.wait_ge(d_wlo, t - 1)
                    sp.dma_start(stage_d[:, k % 2, :], wd[:, bass.ds(t * D_CHUNK, D_CHUNK)])\
                      .then_inc(wd_in[k % 2], 16)
                if have(2):
                    o = (k - 2) % XBUFS
                    bo, ko = (b, k - 2) if k >= 2 else (b - 1, k - 2 + TB)
                    sp.wait_ge(d_x2, t - 1)
                    sp.dma_start(x2_v[:, bass.ds(bo, 1), ko, :], xbuf[:, o:o + 1, :]).then_inc(x2_out[o], 16)
                if have(3):
                    o = (k - 3) % 2
                    bo, ko = (b, k - 3) if k >= 3 else (b - 1, k - 3 + TB)
                    sp.wait_ge(d_h2, t - 2)
                    sp.dma_start(h2_v[:, bass.ds(bo, 1), ko, :], h2[:, o:o + 1, :]).then_inc(h2_out[o], 16)

            token_steps(sp, second_pass, 3)

            sp.wait_ge(e_y, ETILES)
            sp.dma_start(gb_bc[:], mod_dram[:, 3, :].partition_broadcast(P)).then_inc(gb_in, 16)

            def last_pass(b, h, first):
                q = 2 * b + h
                if not first:
                    sp.wait_ge(f_o, q - 1)
                part = slice(QUAD * h, QUAD * h + QUAD)
                sp.dma_start(fin_x2[:, h, :, :], x2_v[:, bass.ds(b, 1), part, :].rearrange("p b k d -> p (b k) d"))\
                  .then_inc(f_in[h], 16)
                if first:
                    for i in range(2):
                        sp.wait_ge(e_out[i], 16 * ((ETILES - i + 1) // 2))
                for c, buf in ((0, fin_y0), (1, fin_y1)):
                    sp.dma_start(buf[:, h, :, :], y_v[:, c, bass.ds(b, 1), part, :].rearrange("p b k d -> p (b k) d"))\
                      .then_inc(f_in[h], 16)

            def last_store(b, h):
                q = 2 * b + h
                part = slice(QUAD * h, QUAD * h + QUAD)
                sp.wait_ge(f_o, q + 1)
                sp.dma_start(out_v[:, bass.ds(b, 1), part, :].rearrange("p b k d -> p (b k) d"), fin_v[:, h, :, :])\
                  .then_inc(f_out[h], 16)

            for h in range(2):
                last_pass(0, h, True)
            with sp.Fori(1, BATCH) as b:
                for h in range(2):
                    last_store(b - 1, h)
                    last_pass(b, h, False)
            for h in range(2):
                last_store(BATCH - 1, h)
            for h in range(2):
                sp.wait_ge(f_out[h], 16 * BATCH)
            for i in range(2):
                sp.wait_ge(e_out[i], 16 * ((ETILES - i + 1) // 2))
                sp.wait_ge(h2_out[i], 16 * (TILES // 2))
            for i in range(XBUFS):
                sp.wait_ge(x2_out[i], 16 * (TILES // XBUFS))

        @block.scalar
        def _(act):
            for dst, src in ((c_sb, c_t), (wmod_sb, wmod)):
                act.dma_start(dst[:], src).then_inc(cond_in, 16)
            for dst, src in ((wqkv_sb, wqkv_t), (brow, bkv_row), (bq_c, bq_cols), (gn_c, gn_cols),
                             (wq_sb, wq), (wo_sb, wo_t), (outb_bc, out_b.partition_broadcast(P))):
                act.dma_start(dst[:], src).then_inc(attw_in, 16)
            act.wait_ge(cond_in, 32)
            act.activation(cs_sb[:], c_sb[:], ACT.Silu).then_inc(cond_act, 1)
            act.wait_ge(mod_step, MOD_STEPS)
            act.dma_start(mod_dram.rearrange("b r d -> b (r d)"), mod_sb[:]).then_inc(mod_out, 16)
            act.wait_ge(mod_out, 16)
            act.dma_start(ga_bc[:], mod_dram[:, 0, :].partition_broadcast(P)).then_inc(ga_in, 16)
            act.wait_ge(zero_set, ZEROS_SET)

            def normalise(t, xi, i, again):
                act.wait_ge(nmr_done, t + 1)
                if again:
                    act.wait_ge(gram_done, t - 1)
                act.activation(xhat[:, i, 0:D], xbuf[:, xi, :], ACT.Identity, scale=rstd1[:, bass.ds(t, 1)],
                               bias=nmr1[:, bass.ds(t, 1)]).then_inc(xhat_done, 1)

            def first_pass(b, k, have):
                t = b * TB + k
                chunk = wg_hi[:, bass.ds(t * G_CHUNK, G_CHUNK)]
                act.wait_ge(wg_in[k % 2], 16 * (TB // 2 * b + k // 2 + 1))
                act.activation(chunk, stage_g[:, k % 2, :], ACT.Copy).then_inc(wghi_done, 1)
                act.wait_ge(mv_done, t + 1)
                act.activation(std[:, k % 2:k % 2 + 1], mv[:, k % 2, 1:2], ACT.Sqrt, bias=eps_col[:, 0:1])\
                   .then_inc(std_done, 1)
                if have(1):
                    normalise(t - 1, (k - 1) % XBUFS, 1 - k % 2, have(3))

            token_steps(act, first_pass, 0)
            normalise(TILES - 1, (TB - 1) % XBUFS, 1, True)

            act.wait_ge(mod_cols, 2)
            for b in range(0, BATCH, 2):
                act.wait_ge(gram_done, TB * (b + 1))
                for out_, in_ in gram_copies(b):
                    act.activation(out_, in_, ACT.Copy)
                for i, (out_, in_, scale) in enumerate(gram_scalings(b)):
                    ins = act.activation(out_, in_, ACT.Copy, scale=scale)
                ins.then_inc(att_ev["gram_a"], 1)
            for b in range(BATCH):
                act.wait_ge(att_pe["g21"], b + 1)
                act.activation(gram[:, b, 1, 0:P], bank[4 + b][:, 0:P], ACT.Copy, scale=sc_cols[:, HC + 1, b:b + 1])
                act.activation(xs_row[0:1, b, :], bank[4 + b][0:1, P:3 * P], ACT.Copy).then_inc(att_ev["g21"], 1)
            for b in range(BATCH):
                act.wait_ge(att_pe["p1"], b + 1)
                for i in range(HC):
                    ins = act.activation(p1[:, b, i, :], bank[b][:, i * D:(i + 1) * D], ACT.Copy,
                                         scale=sc_cols[:, HC + i, b:b + 1])
                ins.then_inc(att_ev["p1"], 1)
            for b in range(BATCH):
                act.wait_ge(att_pe["acn"], b + 1)
                act.activation(a_cn[:, b, :, :], bank[b][:, :].rearrange("p (i d) -> p i d", i=HC), ACT.Copy)\
                   .then_inc(att_ev["acn"], 1)
            for b in range(BATCH):
                act.wait_ge(att_pe["cols"], b + 1)
                act.activation(cols[:, b, :], bank[4 + b][:, 0:6], ACT.Copy).then_inc(att_ev["cols"], 1)
            act.wait_ge(stat_pe, 2)
            act.activation(stat[:, 5, :, :], bank[1][:, 0:BATCH * HC].rearrange("p (b j) -> p b j", b=BATCH),
                           ACT.Sqrt, bias=eps_col[:, 0:1]).then_inc(stat_std, 1)
            act.wait_ge(stat_step, STAT_SCALE)
            for b in range(BATCH):
                for j in range(HC):
                    ins = act.activation(a_cn[:, b, j, :], a_cn[:, b, j, :], ACT.Copy, scale=stat[:, 6, b, j:j + 1])
                ins.then_inc(att_ev["scaled"], 1)

            def second_pass(b, k, have):
                t = b * TB + k
                i = k % 2
                if have(0):
                    act.wait_ge(x2_in[k % XBUFS], 16 * (TB // XBUFS * b + k // XBUFS + 1))
                    if have(2):
                        act.wait_ge(d_tx, t - 1)
                    act.activation(xhat[:, i, 0:D], xbuf[:, k % XBUFS, :], ACT.Identity, scale=rstd1[:, bass.ds(t, 1)],
                                   bias=nmr1[:, bass.ds(t, 1)]).then_inc(d_xhat, 1)
                    act.wait_ge(d_tx, t + 1)
                    if have(1):
                        act.wait_ge(d_c, t)
                    act.activation(xt[:], bank[0][:, 0:D].rearrange("p (i q) -> p i q", i=HC), ACT.Copy)\
                       .then_inc(d_xt, 1)
                if have(4):
                    act.wait_ge(d_gate, t - 3)
                    act.activation(bank[3 + i][:, :], bank[3 + i][:, :], ACT.Square).then_inc(d_sq, 1)
                if have(0):
                    act.wait_ge(wd_in[i], 16 * (TB // 2 * b + k // 2 + 1))
                    act.activation(wd_hi[:, bass.ds(t * D_CHUNK, D_CHUNK)], stage_d[:, i, :], ACT.Copy)\
                       .then_inc(d_whi, 1)
                    act.wait_ge(d_mv, t + 1)
                    act.activation(std2[:, i:i + 1], mv2[:, i, 1:2], ACT.Sqrt, bias=eps_col[:, 0:1]).then_inc(d_std, 1)
                if have(2):
                    act.wait_ge(d_th, t - 1)
                    if have(4):
                        act.wait_ge(d_gate, t - 3)
                    act.activation(hd_hi[:, i, :, :], bank[2][:, 0:D].rearrange("p (i q) -> p i q", i=HC), ACT.Copy)\
                       .then_inc(d_hi, 1)

            token_steps(act, second_pass, 4)

            act.wait_ge(d_sum, TILES)
            act.activation(ssum[:], ssum[:], ACT.Sqrt).then_inc(scores_done, 1)
            act.wait_ge(diff_done, 1)
            act.activation(weight[:, 1, :], weight[:, 0, :], ACT.Exp).then_inc(exp_done, 1)

            def expert_step(s, par, have, uses):
                if have(2):
                    act.wait_ge(e_ta, s - 1)
                    if have(3):
                        act.wait_ge(e_y, s - 2)
                    act.activation(act_hi[:], bank[3][:, :].rearrange("p (c q) -> p c q", c=FC), ACT.Copy)\
                       .then_inc(e_ahi, 1)
                if have(0):
                    act.wait_ge(e_th, s + 1)
                    if have(2):
                        act.wait_ge(e_up, s - 1)
                    act.activation(h_hi[:, par, :, :], bank[4][:, 0:D].rearrange("p (i q) -> p i q", i=HC), ACT.Copy)\
                       .then_inc(e_hi, 1)
                if have(1):
                    act.wait_ge(e_g, s)
                    if have(2):
                        act.wait_ge(e_act, s - 1)
                    act.activation(silu[:], bank[2][:, :], ACT.Silu).then_inc(e_silu, 1)
                if have(0):
                    act.wait_ge(e_tg, s + 1)
                    if have(2):
                        act.wait_ge(e_g, s - 1)
                    act.activation(gt[:, par, :], bank[6][:, 0:P], ACT.Copy).then_inc(e_gthi, 1)
                if have(2):
                    act.wait_ge(e_y, s - 1)
                    if have(4):
                        act.wait_ge(e_out[par], 16 * uses(2))
                    act.activation(y[:, par, :], bank[7][:, 0:D], ACT.Copy).then_inc(e_ys, 1)

            expert_steps(act, expert_step, 2)

            def last_pass(b, h):
                act.wait_ge(f_in[h], 48 * (b + 1))
                for k in range(QUAD):
                    ins = act.activation(fin_u[:, h, k, :], fin_y0[:, h, k, :], ACT.Copy,
                                         scale=weight[:, 0, bass.ds(b * TB + h * QUAD + k, 1)])
                ins.then_inc(f_u, 1)

            with act.Fori(0, BATCH) as b:
                for h in range(2):
                    last_pass(b, h)

        @block.tensor
        def _(pe):
            def transpose(out_, in_):
                return pe.transpose(out_, in_, ident[0:in_.shape[0], 0:in_.shape[0]])

            pe.wait_ge(const_set, POOL_CONSTS)
            pe.wait_ge(cond_act, 1)
            pe.wait_ge(cond_in, 32)
            for n in range(2):
                for i in range(HC):
                    ins = pe.matmul(bank[n][0:BATCH, :], cs_sb[:, i, :], wmod_sb[:, i, (n + 1) * 2 * D:(n + 2) * 2 * D],
                                    start=(i == 0), stop=(i == HC - 1))
            ins.then_inc(mod_prod, 1)
            for q in range(2 * HC):
                for i in range(HC):
                    ins = pe.matmul(bank[2][:, q * BATCH:(q + 1) * BATCH], wmod_sb[:, i, q * P:(q + 1) * P], cs_sb[:, i, :],
                                    start=(i == 0), stop=(i == HC - 1))
            ins.then_inc(mod_prod, 1)
            pe.wait_ge(mod_cols, 1)
            pe.wait_ge(attw_in, 7 * 16)
            for j in range(HC):
                for i in range(HC):
                    pe.matmul(bank[3][:, j * BATCH:(j + 1) * BATCH], wqkv_sb[:, i, j * P:(j + 1) * P], sc_cols[:, i, :],
                              start=(i == 0), stop=(i == HC - 1))
            for b in range(BATCH):
                for i in range(HC):
                    ins = pe.matmul(bank[4 + b][0:1, :], sc_cols[:, i, b:b + 1], wqkv_sb[:, i, D:3 * D],
                                    start=(i == 0), stop=(i == HC - 1))
            ins.then_inc(bias_prod, 1)
            pe.wait_ge(bias_set, 1 + BATCH)
            pe.wait_ge(mod_step, 2)

            def first_pass(b, k, have):
                t = b * TB + k
                xb = xhat[:, k % 2, :]
                pe.wait_ge(xhat_done, t + 1)
                pe.matmul(ps[:, bass.ds(2 * b, 1), 0:D + 1], xb[:, 0:P], xb[:, 0:D + 1],
                          start=(k == 0), stop=(k == TB - 1))
                pe.matmul(ps[:, bass.ds(2 * b + 1, 1), 0:P + 1], xb[:, P:D], xb[:, P:D + 1],
                          start=(k == 0), stop=(k == TB - 1)).then_inc(gram_done, 1)

            token_steps(pe, first_pass, 0)

            pe.wait_ge(att_ev["gram_a"], BATCH // 2)
            pe.wait_ge(att_ev["gram_v"], BATCH // 2)
            for b in range(BATCH):
                transpose(bank[4 + b][:, 0:P], g12[:, b, :])
                for i in range(HC):
                    ins = transpose(bank[4 + b][0:1, (i + 1) * P:(i + 2) * P], xs_raw[:, b, i:i + 1])
                ins.then_inc(att_pe["g21"], 1)
            for b in range(BATCH):
                pe.wait_ge(att_ev["g21"], b + 1)
                for i in range(HC):
                    for m in range(HC):
                        pe.matmul(bank[b][:, i * D:(i + 1) * D], gram[:, b, m, i * P:(i + 1) * P],
                                  wqkv_sb[:, m, 2 * D:3 * D], start=(m == 0), stop=False)
                    ins = pe.matmul(bank[b][:, i * D:(i + 1) * D], xs_row[0:1, b, i * P:(i + 1) * P],
                                    bkv[0:1, b, D:2 * D], start=False, stop=True)
                ins.then_inc(att_pe["p1"], 1)
                for m in range(HC):
                    ins = pe.matmul(bank[4 + b][0:1, 0:D], gram[:, b, m, D:D + 1], wqkv_sb[:, m, 2 * D:3 * D],
                                    start=(m == 0), stop=(m == HC - 1))
                ins.then_inc(att_pe["rv"], 1)
            for b in range(BATCH):
                pe.wait_ge(att_ev["p1"], b + 1)
                pe.wait_ge(att_ev["rv"], b + 1)
                for j in range(HC):
                    o = bank[4 + b][:, j * P:(j + 1) * P]
                    for m in range(HC):
                        pe.matmul(o, wqkv_sb[:, m, D + j * P:D + (j + 1) * P], p1[:, b, m, j * P:(j + 1) * P],
                                  start=(m == 0), stop=False)
                    ins = pe.matmul(o, bkv[0:1, b, j * P:(j + 1) * P], rv_row[0:1, b, j * P:(j + 1) * P],
                                    start=False, stop=True)
                ins.then_inc(att_pe["kv"], 1)
            for b in range(BATCH):
                pe.wait_ge(att_ev["kv"], b + 1)
                for j in range(HC):
                    ins = pe.matmul(bank[b][:, j * D:(j + 1) * D], kv[:, b, j, :], wq_sb[:, j, :], start=True, stop=True)
                ins.then_inc(att_pe["acn"], 1)
                for i in range(HC):
                    for j in range(HC):
                        ins = pe.matmul(bank[4 + b][:, i * D + j * P:i * D + (j + 1) * P], wq_sb[:, j, i * P:(i + 1) * P],
                                        kv[:, b, j, :], start=True, stop=True)
                ins.then_inc(att_pe["anc"], 1)
            for b in range(BATCH):
                pe.wait_ge(att_ev["acn"], b + 1)
                pe.wait_ge(att_ev["anc"], b + 1)
                for i in range(HC):
                    for m in range(HC):
                        ins = pe.matmul(bank[b][:, i * D:(i + 1) * D], gram[:, b, m, i * P:(i + 1) * P], a_nc[:, b, m, :],
                                        start=(m == 0), stop=(m == HC - 1))
                ins.then_inc(att_pe["prod"], 1)
                for j in range(HC):
                    pe.matmul(bank[4 + b][:, j:j + 1], kv[:, b, j, :], bq_all[:, j, b:b + 1], start=True, stop=True)
                for j in range(HC):
                    for m in range(HC):
                        pe.matmul(bank[4 + b][:, 2 + j:3 + j], a_nc[:, b, m, j * P:(j + 1) * P], gram[:, b, m, D:D + 1],
                                  start=(m == 0), stop=(m == HC - 1))
            for b in range(BATCH):
                pe.wait_ge(att_ev["prod"], b + 1)
                for j in range(HC):
                    for m in range(HC):
                        ins = pe.matmul(bank[4 + b][:, 4 + j:5 + j], p1[:, b, m, j * P:(j + 1) * P], ones_col[:, 0:1],
                                        start=(m == 0), stop=(m == HC - 1))
                ins.then_inc(att_pe["cols"], 1)
            for n, (row, step) in enumerate(((1, STAT_MU), (4, STAT_SQ))):
                pe.wait_ge(stat_step, step)
                pe.matmul(bank[n][:, 0:BATCH * HC], headavg[:], stat[:, row, :, :].rearrange("p b j -> p (b j)"),
                          start=True, stop=True).then_inc(stat_pe, 1)
            pe.wait_ge(stat_std, 1)
            pe.wait_ge(stat_step, STAT_SHIFT)
            for b in range(BATCH):
                pe.wait_ge(att_ev["scaled"], b + 1)
                for i in range(HC):
                    for j in range(HC):
                        ins = pe.matmul(bank[b][:, i * D:(i + 1) * D], a_cn[:, b, j, i * P:(i + 1) * P], wo_sb[:, j, :],
                                        start=(j == 0), stop=(j == HC - 1))
                ins.then_inc(att_pe["c"], 1)
                pe.wait_ge(att_ev["ones"], b + 1)
                for j in range(HC):
                    ins = pe.matmul(bank[4 + b][:, 0:D], p1[:, b, j, 0:P], wo_sb[:, j, :],
                                    start=(j == 0), stop=(j == HC - 1))
                ins.then_inc(att_pe["c0"], 1)

            pe.wait_ge(att_ev["c0"], BATCH)
            pe.wait_ge(att_ev["c"], BATCH)
            pe.wait_ge(wglo_done, TILES)

            def three(out_, hi, lo, w_hi, w_lo, first, last):
                pe.matmul(out_, hi, w_hi, start=first, stop=False)
                pe.matmul(out_, hi, w_lo, start=False, stop=False)
                return pe.matmul(out_, lo, w_hi, start=False, stop=last)

            def second_pass(b, k, have):
                t = b * TB + k
                i = k % 2
                if have(0):
                    pe.wait_ge(d_xhat, t + 1)
                    if have(1):
                        pe.wait_ge(d_xt, t)
                    transpose(bank[0][:, 0:P], xhat[:, i, 0:P])
                    transpose(bank[0][:, P:D], xhat[:, i, P:D]).then_inc(d_tx, 1)
                if have(4):
                    pe.wait_ge(d_lo, t - 3)
                    if have(6):
                        pe.wait_ge(d_sum, t - 5)
                    for m in range(HC):
                        w = slice(m * FF, (m + 1) * FF)
                        ins = three(bank[3 + i][:, :], hd_hi[:, i, m, :], hd_lo[:, i, m, :], wg_hi[:, w], wg_lo[:, w],
                                    m == 0, m == HC - 1)
                    ins.then_inc(d_gate, 1)
                if have(0):
                    pe.wait_ge(d_xt, t + 1)
                    if have(1):
                        pe.wait_ge(d_x2, t)
                    for m in range(HC):
                        ins = pe.matmul(bank[1][:, 0:D], xt[:, m, :], c_mat[:, bass.ds(b, 1), m, :],
                                        start=(m == 0), stop=(m == HC - 1))
                    ins.then_inc(d_c, 1)
                if have(2):
                    pe.wait_ge(d_h2, t - 1)
                    if have(3):
                        pe.wait_ge(d_lo, t - 2)
                    transpose(bank[2][:, 0:P], h2[:, i, 0:P])
                    transpose(bank[2][:, P:D], h2[:, i, P:D]).then_inc(d_th, 1)

            token_steps(pe, second_pass, 4)

            pe.wait_ge(pick_done, 1)
            pe.wait_ge(route_pool, ROUTE_CONSTS)
            picked = both[:].rearrange("p t e -> p (t e)")
            pe.matmul(bank[5][:, 0:TILES * EXPERTS], upper[:], picked, start=True, stop=True)
            pe.matmul(bank[6][:, 0:TILES * EXPERTS], ones_m[:], picked, start=True, stop=True).then_inc(count_pe, 1)

            def table_part(n, j, first, last):
                pe.wait_ge(onehot_done, n + 1)
                pe.matmul(bank[7][:, 0:ETILES], in_row[:, j, :], in_col[:, j, :], start=first, stop=last)\
                  .then_inc(table_pe, 1)

            for j in range(4):
                table_part(j, j, j == 0, False)
            with pe.Fori(1, TOPK * TILES // 4 - 1) as m:
                for j in range(4):
                    table_part(m * 4 + j, j, False, False)
            for j in range(4):
                table_part(TOPK * TILES - 4 + j, j, False, j == 3)

            pe.wait_ge(route_done, 1)
            pe.wait_ge(d_wlo, TILES)

            def expert_step(s, par, have, uses):
                _, (e_down, e_mid, e_gate) = nc.values_load_multi_w_load_instructions(
                    tile_expert[0:1, bass.ds(s, 3)], engines=[mybir.EngineType.PE], min_val=0, max_val=EXPERTS - 1,
                    skip_runtime_bounds_check_because="counts of thresholds among EXPERTS - 1")
                if have(2):
                    pe.wait_ge(e_act, s - 1)
                    if have(3):
                        pe.wait_ge(e_alo, s - 2)
                    for c in range(FC):
                        ins = transpose(bank[3][:, c * P:(c + 1) * P], act_[:, par, c * P:(c + 1) * P])
                    ins.then_inc(e_ta, 1)
                if have(0):
                    pe.wait_ge(e_rows[par], 16 * (uses(0) + 1))
                    if have(1):
                        pe.wait_ge(e_lo, s)
                    transpose(bank[4][:, 0:P], rows[:, par, 0:P])
                    transpose(bank[4][:, P:D], rows[:, par, P:D]).then_inc(e_th, 1)
                if have(1):
                    pe.wait_ge(e_lo, s)
                    if have(3):
                        pe.wait_ge(e_act, s - 2)
                    for m in range(HC):
                        w = bass.ds(e_mid * (HC * FF) + (A_W + B_W + m * FF), FF)
                        ins = three(bank[1 - par][:, :], h_hi[:, 1 - par, m, :], h_lo[:, 1 - par, m, :],
                                    wg_hi[:, w], wg_lo[:, w], m == 0, m == HC - 1)
                    ins.then_inc(e_up, 1)
                if have(0):
                    pe.wait_ge(e_lo, s + 1)
                    if have(1):
                        pe.wait_ge(e_ghs, s)
                    for m in range(HC):
                        w = bass.ds(e_gate * RANK + m * FF, RANK)
                        ins = three(bank[5][:, 0:RANK], h_hi[:, par, m, :], h_lo[:, par, m, :],
                                    wg_hi[:, w], wg_lo[:, w], m == 0, m == HC - 1)
                    ins.then_inc(e_gh, 1)
                if have(1):
                    pe.wait_ge(e_gtlo, s)
                    if have(2):
                        pe.wait_ge(e_silu, s - 1)
                    w = bass.ds(e_mid * FF + A_W, FF)
                    pe.matmul(bank[2][:, :], gt[:, 1 - par, :], wg_hi[:, w], start=True, stop=False)
                    pe.matmul(bank[2][:, :], gt[:, 1 - par, :], wg_lo[:, w], start=False, stop=True).then_inc(e_g, 1)
                if have(0):
                    pe.wait_ge(e_ghs, s + 1)
                    if have(1):
                        pe.wait_ge(e_gtlo, s)
                    transpose(bank[6][:, 0:P], gh[:, par, :, :].rearrange("p a r -> p (a r)")).then_inc(e_tg, 1)
                if have(2):
                    pe.wait_ge(e_alo, s - 1)
                    if have(3):
                        pe.wait_ge(e_ys, s - 2)
                    for c in range(FC):
                        w = bass.ds(e_down * (FC * D) + c * D, D)
                        ins = three(bank[7][:, 0:D], act_hi[:, c, :], act_lo[:, c, :], wd_hi[:, w], wd_lo[:, w],
                                    c == 0, c == FC - 1)
                    ins.then_inc(e_y, 1)

            expert_steps(pe, expert_step, 2)

        @block.vector
        def _(dve):
            for n, (t_, v) in enumerate(((eps_col, EPS), (ones_col, 1.0))):
                dve.memset(t_[:], v).then_inc(zero_set, 1)
            for i in range(2):
                dve.memset(xhat[:, i, D:D + 1], 1.0).then_inc(zero_set, 1)

            count = {}

            def then(ins, s):
                count[s.name] = count.get(s.name, 0) + 1
                ins.then_inc(s, 1)
                dve.wait_ge(s, count[s.name])

            dve.wait_ge(mod_prod, 1)
            then(dve.tensor_copy(mod_sb[:, 0:2 * D], bank[0][0:BATCH, :]), mod_step)
            then(dve.tensor_copy(mod_sb[:, 2 * D:4 * D], bank[1][0:BATCH, :]), mod_step)
            dve.wait_ge(mod_prod, 2)
            dve.tensor_copy(sc_cols[:, 0:HC, :], bank[2][:, 0:HC * BATCH].rearrange("p (q b) -> p q b", b=BATCH))\
               .then_inc(mod_cols, 1)
            dve.tensor_scalar(sc_cols[:, HC:2 * HC, :], bank[2][:, HC * BATCH:2 * HC * BATCH].rearrange("p (q b) -> p q b", b=BATCH),
                              1.0, None, ALU.add).then_inc(mod_cols, 1)
            row_cb = mod_sb[:, 2 * D:3 * D]
            then(dve.tensor_scalar(row_cb, row_cb, 1.0, None, ALU.add), mod_step)
            for row in (mod_sb[:, 0:D], mod_sb[:, 3 * D:4 * D]):
                then(dve.tensor_scalar(mod_sign[:], row, 0.0, 2.0, ALU.is_ge, ALU.mult), mod_step)
                then(dve.scalar_tensor_tensor(out=mod_abs[:], in0=mod_sign[:], scalar=-1.0, in1=row,
                                              op0=ALU.add, op1=ALU.mult), mod_step)
                then(dve.tensor_scalar(mod_abs[:], mod_abs[:], GATE_MIN, None, ALU.max), mod_step)
                then(dve.scalar_tensor_tensor(out=row, in0=mod_sign[:], scalar=-1.0, in1=mod_abs[:],
                                              op0=ALU.add, op1=ALU.mult), mod_step)
            assert count[mod_step.name] == MOD_STEPS
            dve.wait_ge(attw_in, 7 * 16)
            dve.wait_ge(bias_prod, 1)
            dve.tensor_tensor(bq_all[:], bank[3][:, 0:HC * BATCH].rearrange("p (j b) -> p j b", b=BATCH),
                              bq_c[:].unsqueeze(2).to_broadcast([P, HC, BATCH]), ALU.add).then_inc(bias_set, 1)
            for b in range(BATCH):
                dve.tensor_tensor(bkv[0:1, b, :], bank[4 + b][0:1, :], brow[:], ALU.add).then_inc(bias_set, 1)

            def first_pass(b, k, have):
                t = b * TB + k
                i = k % 2
                if have(0):
                    dve.wait_ge(x1_in[k % XBUFS], 16 * (TB // XBUFS * b + k // XBUFS + 1))
                    dve.bn_stats(bn[:, i, :], xbuf[:, k % XBUFS, :]).then_inc(bn_done, 1)
                    dve.wait_ge(bn_done, t + 1)
                if have(1):
                    o = 1 - i
                    dve.wait_ge(std_done, t)
                    dve.reciprocal(rstd1[:, bass.ds(t - 1, 1)], std[:, o:o + 1]).then_inc(rstd_done, 1)
                if have(0):
                    dve.bn_aggr(mv[:, i, :], bn[:, i, :]).then_inc(mv_done, 1)
                if have(1):
                    dve.wait_ge(rstd_done, t)
                    dve.scalar_tensor_tensor(out=nmr1[:, bass.ds(t - 1, 1)], in0=mv[:, o, 0:1], scalar=-1.0,
                                             in1=rstd1[:, bass.ds(t - 1, 1)], op0=ALU.mult, op1=ALU.mult)\
                       .then_inc(nmr_done, 1)
                if have(0):
                    dve.wait_ge(wghi_done, t + 1)
                    chunk = bass.ds(t * G_CHUNK, G_CHUNK)
                    dve.tensor_tensor(wg_lo[:, chunk], stage_g[:, i, :], wg_hi[:, chunk].bitcast(F32), ALU.subtract)\
                       .then_inc(wglo_done, 1)

            token_steps(dve, first_pass, 1)

            for b in range(1, BATCH, 2):
                dve.wait_ge(gram_done, TB * (b + 1))
                for out_, in_ in gram_copies(b):
                    dve.tensor_copy(out_, in_)
                for out_, in_, scale in gram_scalings(b):
                    ins = dve.tensor_scalar(out_, in_, scale, None, ALU.mult)
                ins.then_inc(att_ev["gram_v"], 1)
            for b in range(BATCH):
                dve.wait_ge(att_pe["rv"], b + 1)
                dve.scalar_tensor_tensor(out=rv_row[0:1, b, :], in0=bkv[0:1, b, D:2 * D], scalar=float(SEQ),
                                         in1=bank[4 + b][0:1, 0:D], op0=ALU.mult, op1=ALU.add)\
                   .then_inc(att_ev["rv"], 1)
            for b in range(BATCH):
                dve.wait_ge(att_pe["kv"], b + 1)
                dve.tensor_tensor(kv[:, b, :, :], bank[4 + b][:, 0:D].rearrange("p (j q) -> p j q", j=HC),
                                  headmask[:].unsqueeze(1).to_broadcast([P, HC, P]), ALU.mult)\
                   .then_inc(att_ev["kv"], 1)
            for b in range(BATCH):
                dve.wait_ge(att_pe["anc"], b + 1)
                dve.tensor_copy(a_nc[:, b, :, :], bank[4 + b][:, :].rearrange("p (i d) -> p i d", i=HC))\
                   .then_inc(att_ev["anc"], 1)
            for b in range(BATCH):
                dve.wait_ge(att_pe["prod"], b + 1)
                for i in range(HC):
                    ins = dve.scalar_tensor_tensor(out=p1[:, b, i, :], in0=bank[b][:, i * D:(i + 1) * D],
                                                   scalar=sc_cols[:, HC + i, b:b + 1], in1=a_nc[:, b, i, :],
                                                   op0=ALU.mult, op1=ALU.mult)
                ins.then_inc(att_ev["prod"], 1)

            dve.wait_ge(att_ev["cols"], BATCH)
            a0, axs, sq = cols[:, :, 0:2], cols[:, :, 2:4], cols[:, :, 4:6]
            mean, mu, var, dev, dev2, std_, scale, shift = (stat[:, n, :, :] for n in range(8))

            def spread(col):
                return gn_c[:, col, :].unsqueeze(1).to_broadcast([P, BATCH, HC])

            def heads(n):
                return bank[n][:, 0:BATCH * HC].rearrange("p (b j) -> p b j", b=BATCH)

            then(dve.tensor_scalar(mean, axs, 1.0 / SEQ, None, ALU.mult), stat_step)
            then(dve.scalar_tensor_tensor(out=mu, in0=axs, scalar=1.0 / SEQ, in1=a0, op0=ALU.mult, op1=ALU.add), stat_step)
            assert count[stat_step.name] == STAT_MU
            then(dve.tensor_tensor(dev, mean, mean, ALU.mult), stat_step)
            then(dve.scalar_tensor_tensor(out=var, in0=sq, scalar=1.0 / SEQ, in1=dev, op0=ALU.mult, op1=ALU.subtract),
                 stat_step)
            dve.wait_ge(stat_pe, 1)
            then(dve.tensor_tensor(dev, mu, heads(0), ALU.subtract), stat_step)
            then(dve.tensor_tensor(mean, a0, heads(0), ALU.subtract), stat_step)
            then(dve.tensor_tensor(dev, dev, dev, ALU.mult), stat_step)
            then(dve.scalar_tensor_tensor(out=dev2, in0=var, scalar=0.0, in1=dev, op0=ALU.max, op1=ALU.add), stat_step)
            assert count[stat_step.name] == STAT_SQ
            dve.wait_ge(stat_std, 1)
            then(dve.reciprocal(scale, std_), stat_step)
            then(dve.tensor_tensor(scale, scale, spread(0), ALU.mult), stat_step)
            assert count[stat_step.name] == STAT_SCALE
            then(dve.tensor_tensor(shift, mean, scale, ALU.mult), stat_step)
            then(dve.tensor_tensor(shift, shift, spread(1), ALU.add), stat_step)
            assert count[stat_step.name] == STAT_SHIFT
            dve.wait_ge(ga_in, 16)
            for b in range(BATCH):
                dve.wait_ge(att_pe["c"], b + 1)
                for i in range(HC):
                    ins = dve.scalar_tensor_tensor(out=c_mat[:, b, i, :], in0=bank[b][:, i * D:(i + 1) * D],
                                                   scalar=sc_cols[:, HC + i, b:b + 1], in1=ga_bc[:, b, :],
                                                   op0=ALU.mult, op1=ALU.mult)
                ins.then_inc(att_ev["c"], 1)
                dve.wait_ge(att_pe["c0"], b + 1)
                dve.tensor_tensor(c0_bc[:, b, :], bank[4 + b][:, 0:D], outb_bc[:], ALU.add).then_inc(att_ev["c0a"], 1)
                dve.wait_ge(att_ev["c0a"], b + 1)
                dve.tensor_tensor(c0_bc[:, b, :], c0_bc[:, b, :], ga_bc[:, b, :], ALU.mult).then_inc(att_ev["c0"], 1)

            def second_pass(b, k, have):
                t = b * TB + k
                i = k % 2
                if have(0):
                    xk = xbuf[:, k % XBUFS, :]
                    dve.wait_ge(d_c, t + 1)
                    dve.wait_ge(d_xc, t + 1)
                    dve.tensor_tensor(xk, bank[1][:, 0:D], xk, ALU.add).then_inc(d_x2, 1)
                    dve.wait_ge(d_x2, t + 1)
                    dve.bn_stats(bn2[:, i, :], xk).then_inc(d_bn, 1)
                    dve.wait_ge(d_bn, t + 1)
                if have(4):
                    dve.wait_ge(d_sq, t - 3)
                    dve.tensor_reduce(ssum[:, bass.ds(t - 4, 1), :].rearrange("p t e -> p (t e)"),
                                      bank[3 + i][:, :].rearrange("p (e r) -> p e r", e=EXPERTS),
                                      AX_X, ALU.add).then_inc(d_sum, 1)
                if have(0):
                    dve.bn_aggr(mv2[:, i, :], bn2[:, i, :]).then_inc(d_mv, 1)
                    dve.wait_ge(d_std, t + 1)
                    dve.reciprocal(rstd2[:, i:i + 1], std2[:, i:i + 1]).then_inc(d_rstd, 1)
                    dve.wait_ge(d_rstd, t + 1)
                    dve.scalar_tensor_tensor(out=nmr2[:, i:i + 1], in0=mv2[:, i, 0:1], scalar=-1.0,
                                             in1=rstd2[:, i:i + 1], op0=ALU.mult, op1=ALU.mult).then_inc(d_nmr, 1)
                    dve.wait_ge(d_nmr, t + 1)
                    if have(2):
                        dve.wait_ge(d_h2, t - 1)
                    dve.tensor_scalar(xn2[:, i, :], xk, rstd2[:, i:i + 1], nmr2[:, i:i + 1], ALU.mult, ALU.add)\
                       .then_inc(d_xn, 1)
                if have(2):
                    dve.wait_ge(d_hi, t - 1)
                    dve.tensor_tensor(hd_lo[:, i, :, :], bank[2][:, 0:D].rearrange("p (i q) -> p i q", i=HC),
                                      hd_hi[:, i, :, :].bitcast(F32), ALU.subtract).then_inc(d_lo, 1)
                if have(0):
                    dve.wait_ge(d_whi, t + 1)
                    chunk = bass.ds(t * D_CHUNK, D_CHUNK)
                    dve.tensor_tensor(wd_lo[:, chunk], stage_d[:, i, :], wd_hi[:, chunk].bitcast(F32), ALU.subtract)\
                       .then_inc(d_wlo, 1)

            token_steps(dve, second_pass, 4)

            dve.wait_ge(scores_done, 1)
            for i in range(XBUFS):
                dve.wait_ge(x2_out[i], 16 * (TILES // XBUFS))
            for i in range(2):
                dve.wait_ge(h2_out[i], 16 * (TILES // 2))
            dve.wait_ge(d_h2, TILES)
            for t in range(TILES):
                ins = dve.max(top[:, t, :], ssum[:, t, :])
            then(ins, route_step)
            for t in range(TILES):
                ins = dve.max_index(topi[:, t, :], top[:, t, :], ssum[:, t, :])
            dve.tensor_tensor(weight[:, 0, :], top[:, :, 1], top[:, :, 0], ALU.subtract).then_inc(diff_done, 1)
            then(ins, route_step)
            dve.memset(zeros[:], 0.0)
            then(dve.tensor_copy(topf[:], topi[:, :, 0:TOPK].rearrange("p t c -> p c t")), route_step)
            dve.wait_ge(route_pool, ROUTE_CONSTS)
            for c in range(TOPK):
                ins = dve.tensor_tensor(pick[:, c, :, :], iota_row[:, 0:EXPERTS].unsqueeze(1).to_broadcast([P, TILES, EXPERTS]),
                                        topf[:, c, :].unsqueeze(2).to_broadcast([P, TILES, EXPERTS]), ALU.is_equal)
            then(ins, route_step)
            dve.tensor_tensor(both[:], pick[:, 0, :, :], pick[:, 1, :, :], ALU.add).then_inc(pick_done, 1)
            dve.wait_ge(exp_done, 1)
            then(dve.tensor_scalar(weight[:, 0, :], weight[:, 1, :], 1.0, None, ALU.add), route_step)
            then(dve.reciprocal(weight[:, 0, :], weight[:, 0, :]), route_step)
            then(dve.tensor_tensor(weight[:, 1, :], weight[:, 1, :], weight[:, 0, :], ALU.mult), route_step)
            dve.wait_ge(count_pe, 1)
            then(dve.tensor_copy(total[:], bank[6][:, 0:TILES * EXPERTS].rearrange("p (t e) -> p e t", e=EXPERTS)), route_step)
            flat = total[:].rearrange("p e t -> p (e t)")
            then(dve.tensor_tensor_scan(cum[:].rearrange("p e t -> p (e t)"), flat, zeros[:], 0.0, ALU.add, ALU.add),
                 route_step)
            start, number, tiles_f, ends, shift_e = (small[:, n, :] for n in range(5))
            dve.memset(small[:, 0, 0:1], 0.0)
            then(dve.tensor_copy(small[:, 0, 1:EXPERTS], cum[:, 0:EXPERTS - 1, TILES - 1]), route_step)
            then(dve.tensor_tensor(number, cum[:, :, TILES - 1], start, ALU.subtract), route_step)
            then(dve.tensor_scalar(small_i[:, 0, :], number, float(P - 1), None, ALU.add), route_step)
            then(dve.tensor_scalar(small_i[:, 1, :], small_i[:, 0, :], LOG_P, None, ALU.logical_shift_right), route_step)
            then(dve.tensor_copy(tiles_f, small_i[:, 1, :]), route_step)
            then(dve.tensor_tensor_scan(ends, tiles_f, zeros[:, 0:EXPERTS], 0.0, ALU.add, ALU.add), route_step)
            then(dve.tensor_tensor(shift_e, ends, tiles_f, ALU.subtract), route_step)
            then(dve.scalar_tensor_tensor(out=shift_e, in0=shift_e, scalar=float(P), in1=start, op0=ALU.mult,
                                          op1=ALU.subtract), route_step)
            then(dve.tensor_tensor(cum[:], cum[:], total[:], ALU.subtract), route_step)
            then(dve.tensor_tensor(cum[:], cum[:], shift_e.unsqueeze(2).to_broadcast([P, EXPERTS, TILES]), ALU.add), route_step)
            then(dve.tensor_tensor(slot_m[:], bank[5][:, 0:TILES * EXPERTS].rearrange("p (t e) -> p t e", e=EXPERTS),
                                   cum[:].rearrange("p e t -> p t e"), ALU.add), route_step)
            for c in range(TOPK):
                ins = dve.tensor_tensor(slot_k[:, c, :, :], pick[:, c, :, :], slot_m[:], ALU.mult)
            then(ins, route_step)
            then(dve.tensor_reduce(slot[:], slot_k[:].rearrange("p c t e -> p (c t) e"), AX_X, ALU.add), route_step)
            then(dve.tensor_copy(slot_i[:, 0, :], slot[:]), route_step)
            dve.tensor_scalar(slot_i[:, 1, :], slot_i[:, 0, :], P - 1, None, ALU.bitwise_and)
            then(dve.tensor_scalar(slot_i[:, 2, :], slot_i[:, 0, :], LOG_P, None, ALU.logical_shift_right), route_step)
            then(dve.tensor_copy(slot_f[:], slot_i[:, 1:3, :]), route_step)

            def onehots(n, j, first):
                if not first:
                    dve.wait_ge(table_pe, n - 3)
                dve.tensor_scalar(in_row[:, j, :], iota_row[:], slot_f[:, 0, bass.ds(n, 1)], None, ALU.is_equal)
                dve.tensor_scalar(in_col[:, j, :], iota_row[:, 0:ETILES], slot_f[:, 1, bass.ds(n, 1)],
                                  value[:, bass.ds(n, 1)], ALU.is_equal, ALU.mult).then_inc(onehot_done, 1)

            for j in range(4):
                onehots(j, j, True)
            with dve.Fori(1, TOPK * TILES // 4) as m:
                for j in range(4):
                    onehots(m * 4 + j, j, False)

            ef = expert_f[0:1, 0, 0:ETILES]
            then(dve.memset(tile_expert[0:1, :], 0), route_step)
            then(dve.tensor_scalar(ef, iota_row[0:1, 0:ETILES], small[0:1, 3, 0:1], None, ALU.is_ge), route_step)
            for e in range(1, EXPERTS - 1):
                then(dve.scalar_tensor_tensor(out=ef, in0=iota_row[0:1, 0:ETILES], scalar=small[0:1, 3, e:e + 1], in1=ef,
                                              op0=ALU.is_ge, op1=ALU.add), route_step)
            then(dve.tensor_copy(tile_expert[0:1, 2:2 + ETILES], ef), route_step)
            dve.wait_ge(table_pe, TOPK * TILES)
            then(dve.tensor_scalar(pad[:, 0, :], bank[7][:, 0:ETILES], 0.0, value[:, VALUE_PAD:VALUE_PAD + 1],
                                   ALU.is_equal, ALU.mult), route_step)
            then(dve.scalar_tensor_tensor(out=dest[:], in0=bank[7][:, 0:ETILES], scalar=-1.0, in1=pad[:, 0, :],
                                          op0=ALU.add, op1=ALU.add), route_step)
            then(dve.tensor_scalar(token[:], dest[:], TOKENS - 1, None, ALU.bitwise_and), route_step)
            dve.memset(pad[:, 1, :], 0.0).then_inc(route_done, 1)

            def expert_step(s, par, have, uses):
                if have(2):
                    dve.wait_ge(e_ahi, s - 1)
                    dve.tensor_tensor(act_lo[:], bank[3][:, :].rearrange("p (c q) -> p c q", c=FC),
                                      act_hi[:].bitcast(F32), ALU.subtract).then_inc(e_alo, 1)
                if have(0):
                    dve.wait_ge(e_hi, s + 1)
                    dve.tensor_tensor(h_lo[:, par, :, :], bank[4][:, 0:D].rearrange("p (i q) -> p i q", i=HC),
                                      h_hi[:, par, :, :].bitcast(F32), ALU.subtract).then_inc(e_lo, 1)
                    dve.wait_ge(e_gh, s + 1)
                    dve.tensor_copy(gh[:, par, :, :], bank[5][:, 0:RANK].unsqueeze(1).to_broadcast([P, 2, RANK]))\
                       .then_inc(e_ghs, 1)
                if have(1):
                    dve.wait_ge(e_silu, s)
                    dve.tensor_tensor(act_[:, 1 - par, :], bank[1 - par][:, :], silu[:], ALU.mult).then_inc(e_act, 1)
                if have(0):
                    dve.wait_ge(e_gthi, s + 1)
                    half = slice(RANK, 2 * RANK)
                    dve.tensor_tensor(gt[half, par, :], bank[6][half, 0:P], gt[half, par, :].bitcast(F32), ALU.subtract)\
                       .then_inc(e_gtlo, 1)

            expert_steps(dve, expert_step, 2)

            def last_pass(b, h, first):
                q = 2 * b + h
                if first:
                    pass
                else:
                    dve.wait_ge(f_out[h], 16 * b)
                dve.wait_ge(f_u, q + 1)
                for k in range(QUAD):
                    ins = dve.scalar_tensor_tensor(out=fin_v[:, h, k, :], in0=fin_y1[:, h, k, :],
                                                   scalar=weight[:, 1, bass.ds(b * TB + h * QUAD + k, 1)],
                                                   in1=fin_u[:, h, k, :], op0=ALU.mult, op1=ALU.add)
                ins.then_inc(f_v, 1)

            def last_sum(b, h):
                q = 2 * b + h
                dve.wait_ge(f_w, q + 1)
                dve.tensor_tensor(fin_v[:, h, :, :], fin_u[:, h, :, :], fin_x2[:, h, :, :], ALU.add).then_inc(f_o, 1)

            last_pass(0, 0, True)
            last_pass(0, 1, True)
            last_sum(0, 0)
            with dve.Fori(1, BATCH) as b:
                last_pass(b, 0, False)
                last_sum(b - 1, 1)
                last_pass(b, 1, False)
                last_sum(b, 0)
            last_sum(BATCH - 1, 1)

        @block.gpsimd
        def _(pool):
            n = 0
            for t_, v in ((ident, 0.0), (headmask, 1.0), (headavg, 1.0 / HEAD)):
                pool.memset(t_[:], v).then_inc(const_set, 1)
                n += 1
            pool.wait_ge(const_set, n)
            pool.affine_select(out=ident[:], in_=ident[:], compare_op=ALU.not_equal, fill=1.0, base=0,
                               pattern=[[-1, P]], channel_multiplier=1).then_inc(const_set, 1)
            for t_ in (headmask, headavg):
                v = t_[:].rearrange("p (g r) -> p g r", r=HEAD)
                pool.affine_select(out=v, in_=v, compare_op=ALU.is_ge, fill=0.0, base=0,
                                   pattern=[[-HEAD, P // HEAD], [0, HEAD]], channel_multiplier=1).then_inc(const_set, 1)
            pool.wait_ge(const_set, n + 3)
            for t_ in (headmask, headavg):
                v = t_[:].rearrange("p (g r) -> p g r", r=HEAD)
                pool.affine_select(out=v, in_=v, compare_op=ALU.is_ge, fill=0.0, base=HEAD - 1,
                                   pattern=[[HEAD, P // HEAD], [0, HEAD]], channel_multiplier=-1).then_inc(const_set, 1)
            assert n + 5 == POOL_CONSTS

            pool.wait_ge(stat_step, STAT_SHIFT)
            for b in range(BATCH):
                for j in range(HC):
                    ins = pool.tensor_scalar(p1[:, b, j, 0:P], ident[:], 0.0, stat[:, 7, b, j:j + 1], ALU.mult, ALU.add)
                ins.then_inc(att_ev["ones"], 1)

            pool.wait_ge(att_ev["c0"], BATCH)
            pool.wait_ge(scb_in, 32)

            def second_pass(b, k, have):
                t = b * TB + k
                i = k % 2
                if have(0):
                    xk = xbuf[:, k % XBUFS:k % XBUFS + 1, :]
                    pool.wait_ge(d_xhat, t + 1)
                    pool.sem_inc(pool_past, 1)
                    pool.tensor_tensor(xk, xk, c0_bc[:, bass.ds(b, 1), :], ALU.add).then_inc(d_xc, 1)
                if have(2):
                    bo = b if k >= 2 else b - 1
                    pool.wait_ge(d_xn, t - 1)
                    pool.sem_inc(pool_past, 1)
                    pool.tensor_tensor(xn2[:, i:i + 1, :], xn2[:, i:i + 1, :], cb_bc[:, bass.ds(bo, 1), :], ALU.mult)\
                        .then_inc(d_h2m, 1)
                    pool.wait_ge(d_h2m, t - 1)
                    if have(4):
                        pool.wait_ge(h2_out[i], 16 * (TB // 2 * b + k // 2 - 1))
                        pool.wait_ge(d_th, t - 3)
                    pool.sem_inc(pool_past, 1)
                    pool.tensor_tensor(h2[:, i:i + 1, :], xn2[:, i:i + 1, :], sb_bc[:, bass.ds(bo, 1), :], ALU.add)\
                        .then_inc(d_h2, 1)

            token_steps(pool, second_pass, 2)

            for i in range(XBUFS):
                pool.wait_ge(x2_out[i], 16 * (TILES // XBUFS))
            for i in range(2):
                pool.wait_ge(h2_out[i], 16 * (TILES // 2))
            pool.wait_ge(d_sum, TILES)
            pool.wait_ge(d_wlo, TILES)
            pool.memset(upper[:], 1.0).then_inc(route_pool, 1)
            pool.memset(ones_m[:], 1.0).then_inc(route_pool, 1)
            pool.iota(iota_row[:], pattern=[[1, P]], base=0, channel_multiplier=0, allow_small_or_imprecise_dtypes=True)\
                .then_inc(route_pool, 1)
            pool.wait_ge(route_pool, 3)
            pool.affine_select(out=upper[:], in_=upper[:], compare_op=ALU.is_gt, fill=0.0, base=0,
                               pattern=[[1, P]], channel_multiplier=-1).then_inc(route_pool, 1)
            for c in range(TOPK):
                pool.iota(value[:, c * TILES:(c + 1) * TILES].rearrange("p (b k) -> p b k", b=BATCH),
                          pattern=[[SEQ, BATCH], [1, TB]], base=1 + c * TOKENS, channel_multiplier=TB,
                          allow_small_or_imprecise_dtypes=True).then_inc(route_pool, 1)
            pool.iota(value[:, VALUE_PAD:VALUE_PAD + 1], pattern=[[0, 1]], base=TOPK * TOKENS + 1, channel_multiplier=1,
                      allow_small_or_imprecise_dtypes=True).then_inc(route_pool, 1)

            pool.wait_ge(route_done, 1)

            def expert_step(s, par, have, uses):
                if have(0):
                    if have(2):
                        pool.wait_ge(e_th, s - 1)
                    pool.tensor_copy(tok_ix[:, par:par + 1], token[:, bass.ds(s, 1)]).then_inc(e_tix, 1)
                    pool.wait_ge(e_tix, s + 1)
                    pool.sem_inc(pool_past, 1)
                    pool.indirect_dma_start(rows[:, par, :], None, h2_dram,
                                            bass.IndirectOffsetOnAxis(ap=tok_ix[:, par:par + 1], axis=0))\
                        .then_inc(e_rows[par], 16)
                if have(3):
                    o = 1 - par
                    pool.wait_ge(e_ys, s - 2)
                    if have(4):
                        pool.wait_ge(e_out[par], 16 * (uses(4) + 1))
                    pool.tensor_copy(dst_ix[:, o:o + 1], dest[:, bass.ds(s - 3, 1)]).then_inc(e_dix, 1)
                    pool.wait_ge(e_dix, s - 2)
                    pool.sem_inc(pool_past, 1)
                    pool.indirect_dma_start(y_dram, bass.IndirectOffsetOnAxis(ap=dst_ix[:, o:o + 1], axis=0),
                                            y[:, o, :], None).then_inc(e_out[o], 16)

            expert_steps(pool, expert_step, 3)

            pool.wait_ge(gb_in, 16)

            def last_pass(b, h):
                q = 2 * b + h
                pool.wait_ge(f_v, q + 1)
                pool.sem_inc(pool_past, 1)
                pool.tensor_tensor(fin_u[:, h, :, :], fin_v[:, h, :, :],
                                   gb_bc[:, bass.ds(b, 1), :].to_broadcast([P, QUAD, D]), ALU.mult).then_inc(f_w, 1)

            with pool.Fori(0, BATCH) as b:
                for h in range(2):
                    last_pass(b, h)


def kernel(**inputs):
    import numpy as np
    import concourse.bacc as bacc
    from concourse.bass_utils import run_bass_kernel_spmd

    a = {n.removeprefix("L0_"): np.asarray(v) for n, v in inputs.items()}

    def halves(m):
        return np.ascontiguousarray(m.reshape(-1, P, m.shape[-1]).transpose(1, 0, 2))

    w_a = halves(a["ffn_W_A"].reshape(EXPERTS * RANK, D).T).reshape(P, -1)
    w_b = a["ffn_W_B"].transpose(2, 0, 1).reshape(RANK, -1)
    w_up = a["ffn_W_up"].transpose(2, 0, 1).reshape(HC, P, EXPERTS, FF).transpose(1, 2, 0, 3).reshape(P, -1)
    w_down = a["ffn_W_down"].transpose(2, 0, 1).reshape(FC, P, EXPERTS, D).transpose(1, 2, 0, 3).reshape(P, -1)
    arrays = {
        "x": a["attn_x"],
        "c_t": halves(a["c"].T),
        "wmod": halves(a["wmod"]),
        "wqkv_t": halves(a["attn_Wqkv_w"].T),
        "wq": halves(a["attn_Wqkv_w"][0:D]),
        "bq_cols": a["attn_Wqkv_b"][0:D].reshape(HC, P).T,
        "bkv_row": a["attn_Wqkv_b"][D:].reshape(1, 2 * D),
        "gn_cols": np.stack([a["attn_gn_w"].reshape(HC, P).T, a["attn_gn_b"].reshape(HC, P).T], axis=1),
        "wo_t": halves(a["attn_out_w"].T),
        "out_b": a["attn_out_b"],
        "wg": np.concatenate([w_a, np.concatenate([w_b, w_b], axis=0), w_up], axis=1),
        "wd": w_down,
    }
    nc = bacc.Bacc("TRN2", target_bir_lowering=False, num_devices=1)
    args = {}
    for name, v in arrays.items():
        arrays[name] = v = np.ascontiguousarray(v)
        args[name] = nc.dram_tensor(f"in_{name}", v.shape, mybir.dt.from_np(v.dtype), kind="ExternalInput").ap()
    args["out"] = nc.dram_tensor("out_0", (BATCH, SEQ, D), F32, kind="ExternalOutput").ap()
    build(nc, **args)
    r = run_bass_kernel_spmd(nc, [{f"in_{n}": v for n, v in arrays.items()}], core_ids=[0])
    return r.results[0]["out_0"]
```

```python
from contextlib import ExitStack

import concourse.bass as bass
from concourse import mybir


P = 128
ALU = mybir.AluOpType
ACT = mybir.ActivationFunctionType
F32 = mybir.dt.float32
F32R = mybir.dt.float32r
I32 = mybir.dt.int32
U32 = mybir.dt.uint32
AX_X = mybir.AxisListType.X

BATCH, SEQ, D = 4, 1024, 256
HEADS = 32
HEAD = D // HEADS
EXPERTS, TOPK, RANK, FF = 8, 2, 64, 512
EPS = 1e-5
GATE_MIN = 0.25

HC = D // P
FC = FF // P
TB = SEQ // P
TILES = BATCH * TB
TOKENS = BATCH * SEQ
ETILES = (TOPK * TOKENS + EXPERTS * (P - 1)) // P
XBUFS = 4
X1BUFS = 8

A_W = HC * FF
B_W = EXPERTS * FF
UP_W = EXPERTS * HC * FF
G_W = A_W + B_W + UP_W
D_W = EXPERTS * FC * D
G_CHUNK = G_W // TILES
D_CHUNK = D_W // TILES
GBUFS = 4
QUAD = 4
E_LAG = 3
LOG_P = P.bit_length() - 1
VALUE_PAD = TOPK * TILES

POOL_CONSTS = 8
ZEROS_SET = 4
STAT_MU, STAT_SQ, STAT_SCALE, STAT_SHIFT = 2, 8, 10, 12
ROUTE_CONSTS = 7


class Region:

    def __init__(self, nc, base, end):
        self.nc, self.at, self.end = nc, base, end

    def take(self, name, shape, dt=F32):
        size = 4
        for n in shape[1:]:
            size *= n
        t = self.nc.alloc_sbuf_tensor_at(name, shape, dt, offset=self.at)
        self.at += -(-size // 64) * 64
        assert self.at <= self.end, (name, self.at, self.end)
        return t

    def rewind(self, at):
        self.at = at


def build(nc, x, c_t, wmod, wqkv_t, wq, bq_cols, bkv_row, gn_cols, wo_t, out_b, wg, wd, out):
    h2_dram = nc.dram_tensor("h2_rows", [TOKENS, D], F32).ap()
    x2_dram = nc.dram_tensor("x2_rows", [BATCH, P, TB, D], F32).ap()
    y_dram = nc.dram_tensor("y_rows", [TOPK * TOKENS + P, D], F32).ap()
    mod_dram = nc.dram_tensor("mod_rows", [BATCH, 4, D], F32).ap()

    x_v = x.rearrange("b (p k) d -> p b k d", p=P)
    out_v = out.rearrange("b (p k) d -> p b k d", p=P)
    x2_v = x2_dram.rearrange("b p k d -> p b k d")
    h2_v = h2_dram.rearrange("(b p k) d -> p b k d", b=BATCH, p=P)
    y_v = y_dram[0:TOPK * TOKENS, :].rearrange("(c b p k) d -> p c b k d", c=TOPK, b=BATCH, p=P)

    with ExitStack() as ctx:
        def sem(name):
            return ctx.enter_context(nc.semaphore(name))

        ps = ctx.enter_context(nc.psum_tensor("ps", [P, 8, 512], F32))
        bank = [ps[:, i, :] for i in range(8)]

        base = -(-nc.sbuf_base // 64) * 64
        end = nc.sbuf_usable_end // 64 * 64
        r1 = Region(nc, base, base + 2 * 4 * D_W)
        gram = r1.take("gram", [P, BATCH, HC, D + 1])
        p1 = r1.take("p1", [P, BATCH, HC, D])
        kv = r1.take("kv", [P, BATCH, HC, P])
        a_start = r1.at
        mod_sign = r1.take("mod_sign", [BATCH, 2, D])
        mod_abs = r1.take("mod_abs", [BATCH, 2, D])
        brow = r1.take("brow", [BATCH, 2 * D])
        bkv_rows = r1.take("bkv_rows", [BATCH, 2 * D])
        r1.rewind(a_start)
        a_cn = r1.take("a_cn", [P, BATCH, HC, D])
        a_nc = r1.take("a_nc", [P, BATCH, HC, D])
        bkv = r1.take("bkv", [1, BATCH, 2 * D])
        wqkv_sb = r1.take("wqkv_sb", [P, HC, 3 * D])
        wq_sb = r1.take("wq_sb", [P, HC, D])
        wo_sb = r1.take("wo_sb", [P, HC, D])
        ga_bc = r1.take("ga_bc", [P, BATCH, D])
        x1_more = r1.take("x1_more", [P, X1BUFS - XBUFS, D])
        r1.rewind(base)
        wd_hi = r1.take("wd_hi", [P, D_W], F32R)
        wd_lo = r1.take("wd_lo", [P, D_W], F32R)
        r1.rewind(base)
        fin_y0 = r1.take("fin_y0", [P, 2, QUAD, D])
        fin_y1 = r1.take("fin_y1", [P, 2, QUAD, D])
        fin_x2 = r1.take("fin_x2", [P, 2, QUAD, D])
        fin_u = r1.take("fin_u", [P, 2, QUAD, D])
        fin_v = r1.take("fin_v", [P, 2, QUAD, D])
        gb_bc = r1.take("gb_bc", [P, BATCH, D])

        r2 = Region(nc, base + 2 * 4 * D_W, end)
        wg_parts = r2.take("wg_parts", [P, 2, G_W], F32R)
        wg_hi, wg_lo = wg_parts[:, 0, :], wg_parts[:, 1, :]
        ident = r2.take("ident", [P, P])
        ones_col = r2.take("ones_col", [P, 1])
        eps_col = r2.take("eps_col", [P, 1])
        weight = r2.take("weight", [P, TOPK, TILES])
        ssum = r2.take("ssum", [P, TILES, EXPERTS])
        regional = r2.at

        wmod_sb = r2.take("wmod_sb", [P, HC, 6 * D])
        r2.rewind(regional)
        c_mat = r2.take("c_mat", [P, BATCH, HC, D])
        c0_bc = r2.take("c0_bc", [P, BATCH, D])
        rstd1 = r2.take("rstd1", [P, TILES])
        nmr1 = r2.take("nmr1", [P, TILES])
        bn = r2.take("bn", [P, 2, 6])
        mv = r2.take("mv", [P, 2, 2])
        std = r2.take("std", [P, 2])
        xbuf = r2.take("xbuf", [P, XBUFS, D])
        xhat = r2.take("xhat", [P, 2, D + 1])
        x1_bufs = [xbuf[:, i:i + 1, :] for i in range(XBUFS)] + [x1_more[:, i:i + 1, :] for i in range(X1BUFS - XBUFS)]
        per_pass = r2.at
        stage_g = r2.take("stage_g", [P, GBUFS, G_CHUNK])
        headmask = r2.take("headmask", [P, P])
        headavg = r2.take("headavg", [P, P])
        sc_cols = r2.take("sc_cols", [P, 2 * HC, BATCH])
        bq_c = r2.take("bq_c", [P, HC])
        bq_all = r2.take("bq_all", [P, HC, BATCH])
        gn_c = r2.take("gn_c", [P, 2, HC])
        outb_bc = r2.take("outb_bc", [P, D])
        xs_raw = r2.take("xs_raw", [P, BATCH, HC])
        g12 = r2.take("g12", [P, BATCH, P])
        cols = r2.take("cols", [P, BATCH, 6])
        stat = r2.take("stat", [P, 8, BATCH, HC])
        mod_start = r2.at
        c_sb = r2.take("c_sb", [P, HC, BATCH])
        cs_sb = r2.take("cs_sb", [P, HC, BATCH])
        mod_sb = r2.take("mod_sb", [BATCH, 4 * D])
        r2.rewind(mod_start)
        xs_row = r2.take("xs_row", [1, BATCH, D])
        rv_row = r2.take("rv_row", [1, BATCH, D])
        r2.rewind(per_pass)
        stage_d = r2.take("stage_d", [P, 2, D_CHUNK])
        sb_bc = r2.take("sb_bc", [P, BATCH, D])
        cb_bc = r2.take("cb_bc", [P, BATCH, D])
        xt = r2.take("xt", [P, HC, P])
        x2buf = r2.take("x2buf", [P, 2, D])
        h2 = r2.take("h2", [P, 2, D])
        hd_hi = r2.take("hd_hi", [P, 2, HC, P], F32R)
        hd_lo = r2.take("hd_lo", [P, 2, HC, P], F32R)
        bn2 = r2.take("bn2", [P, 2, 6])
        mv2 = r2.take("mv2", [P, 2, 2])
        std2 = r2.take("std2", [P, 2])
        rstd2 = r2.take("rstd2", [P, 2])
        nmr2 = r2.take("nmr2", [P, 2])
        r2.rewind(regional)
        top = r2.take("top", [P, TILES, 8])
        topi = r2.take("topi", [P, TILES, 8], U32)
        topf = r2.take("topf", [P, TOPK, TILES])
        table = r2.take("table", [P, ETILES])
        dest = r2.take("dest", [P, ETILES], I32)
        token = r2.take("token", [P, ETILES], I32)
        tile_expert = r2.take("tile_expert", [1, ETILES + 2 * E_LAG], I32)
        experts_start = r2.at
        pick = r2.take("pick", [P, TOPK, TILES, EXPERTS])
        both = r2.take("both", [P, TILES, EXPERTS])
        total = r2.take("total", [P, EXPERTS, TILES])
        cum = r2.take("cum", [P, EXPERTS, TILES])
        zeros = r2.take("zeros", [P, EXPERTS * TILES])
        slot_m = r2.take("slot_m", [P, TILES, EXPERTS])
        slot_k = r2.take("slot_k", [P, TOPK, TILES, EXPERTS])
        slot = r2.take("slot", [P, TOPK * TILES])
        slot_i = r2.take("slot_i", [P, 3, TOPK * TILES], I32)
        slot_f = r2.take("slot_f", [P, 2, TOPK * TILES])
        small = r2.take("small", [P, 8, EXPERTS])
        small_i = r2.take("small_i", [P, 2, EXPERTS], I32)
        upper = r2.take("upper", [P, P])
        iota_row = r2.take("iota_row", [P, P])
        ones_m = r2.take("ones_m", [P, P])
        value = r2.take("value", [P, TOPK * TILES + 1])
        in_row = r2.take("in_row", [P, 4, P])
        in_col = r2.take("in_col", [P, 4, ETILES])
        expert_f = r2.take("expert_f", [P, 2, ETILES + 1])
        pad = r2.take("pad", [P, 2, ETILES])
        r2.rewind(experts_start)
        tok_ix = r2.take("tok_ix", [P, 2], I32)
        dst_ix = r2.take("dst_ix", [P, 2], I32)
        rows = r2.take("rows", [P, 2, D])
        h_hi = r2.take("h_hi", [P, 2, HC, P], F32R)
        h_lo = r2.take("h_lo", [P, 2, HC, P], F32R)
        gh = r2.take("gh", [P, 2, 2, RANK])
        gt = r2.take("gt", [P, 2, P], F32R)
        silu = r2.take("silu", [P, FF])
        act_ = r2.take("act_", [P, 2, FF])
        act_hi = r2.take("act_hi", [P, FC, P], F32R)
        act_lo = r2.take("act_lo", [P, FC, P], F32R)
        y = r2.take("y", [P, 2, D])

        pool_past = sem("pool_past")
        const_set = sem("const_set")
        zero_set = sem("zero_set")
        c_in = sem("c_in")
        wmod_in = sem("wmod_in")
        attw_in = sem("attw_in")
        cond_act = sem("cond_act")
        mod_prod = sem("mod_prod")
        mod_cols = sem("mod_cols")
        mod_rows = sem("mod_rows")
        mod_step = sem("mod_step")
        mod_out = sem("mod_out")
        ga_in = sem("ga_in")
        bias_prod = sem("bias_prod")
        bias_set = sem("bias_set")
        bkv_in = sem("bkv_in")
        x1_in = [sem(f"x1_in{i}") for i in range(X1BUFS)]
        wg_in = [sem(f"wg_in{i}") for i in range(GBUFS)]
        bn_done = sem("bn_done")
        mv_done = sem("mv_done")
        std_done = sem("std_done")
        rstd_done = sem("rstd_done")
        nmr_done = sem("nmr_done")
        xhat_done = sem("xhat_done")
        wghi_done = sem("wghi_done")
        wglo_done = sem("wglo_done")
        gram_done = sem("gram_done")
        att_pe = {n: sem(f"pe_{n}") for n in ("g21", "p1", "rv", "kv", "acn", "anc", "prod", "cols", "c", "c0")}
        att_ev = {n: sem(f"ev_{n}") for n in ("gram_a", "gram_v", "g21", "p1", "rv", "kv", "acn", "anc", "prod",
                                              "cols", "scaled", "ones", "c", "c0a", "c0")}
        stat_step = sem("stat_step")
        stat_pe = sem("stat_pe")
        stat_std = sem("stat_std")
        x2_in = [sem(f"x2_in{i}") for i in range(XBUFS)]
        wd_in = [sem(f"wd_in{i}") for i in range(2)]
        scb_in = sem("scb_in")
        x2_out = [sem(f"x2_out{i}") for i in range(2)]
        h2_out = [sem(f"h2_out{i}") for i in range(2)]
        d_xhat = sem("d_xhat")
        d_xc = sem("d_xc")
        d_tx = sem("d_tx")
        d_xt = sem("d_xt")
        d_c = sem("d_c")
        d_x2 = sem("d_x2")
        d_bn = sem("d_bn")
        d_mv = sem("d_mv")
        d_std = sem("d_std")
        d_rstd = sem("d_rstd")
        d_nmr = sem("d_nmr")
        d_xn = sem("d_xn")
        d_h2m = sem("d_h2m")
        d_h2 = sem("d_h2")
        d_th = sem("d_th")
        d_hi = sem("d_hi")
        d_lo = sem("d_lo")
        d_gate = sem("d_gate")
        d_sq = sem("d_sq")
        d_sum = sem("d_sum")
        d_whi = sem("d_whi")
        d_wlo = sem("d_wlo")
        scores_done = sem("scores_done")
        route_pool = sem("route_pool")
        route_step = sem("route_step")
        pick_done = sem("pick_done")
        diff_done = sem("diff_done")
        exp_done = sem("exp_done")
        count_pe = sem("count_pe")
        onehot_done = sem("onehot_done")
        table_pe = sem("table_pe")
        route_done = sem("route_done")
        e_tix = sem("e_tix")
        e_dix = sem("e_dix")
        e_rows = [sem(f"e_rows{i}") for i in range(2)]
        e_out = [sem(f"e_out{i}") for i in range(2)]
        e_th = sem("e_th")
        e_hi = sem("e_hi")
        e_lo = sem("e_lo")
        e_up = sem("e_up")
        e_gh = sem("e_gh")
        e_ghs = sem("e_ghs")
        e_tg = sem("e_tg")
        e_gthi = sem("e_gthi")
        e_gtlo = sem("e_gtlo")
        e_g = sem("e_g")
        e_silu = sem("e_silu")
        e_act = sem("e_act")
        e_ta = sem("e_ta")
        e_ahi = sem("e_ahi")
        e_alo = sem("e_alo")
        e_y = sem("e_y")
        e_ys = sem("e_ys")
        gb_in = sem("gb_in")
        f_in = [sem(f"f_in{i}") for i in range(2)]
        f_u = sem("f_u")
        f_v = sem("f_v")
        f_w = sem("f_w")
        f_o = sem("f_o")
        f_out = [sem(f"f_out{i}") for i in range(2)]

        def gram_copies(b):
            g = ps[:, 2 * b:2 * b + 2, :]
            return ((g12[:, b, :], g[:, 0, P:D]), (xs_raw[:, b, 0:1], g[:, 0, D:D + 1]),
                    (xs_raw[:, b, 1:2], g[:, 1, P:P + 1]))

        def gram_scalings(b):
            g = ps[:, 2 * b:2 * b + 2, :]
            return ((gram[:, b, 0, :], g[:, 0, 0:D + 1], sc_cols[:, HC, b:b + 1]),
                    (gram[:, b, 1, P:D + 1], g[:, 1, 0:P + 1], sc_cols[:, HC + 1, b:b + 1]))

        def token_steps(eng, step, lag, alone=1, between={}):
            for t in range(alone * TB):
                step(t // TB, t % TB, lambda n, t=t: t >= n)
                if t in between:
                    between[t]()
            with eng.Fori(alone, BATCH) as b:
                for k in range(TB):
                    step(b, k, lambda n: True)
            for k in range(lag):
                step(BATCH, k, lambda n, k=k: n > k)

        def back(b, k, n):
            return (b, k - n) if k >= n else (b - 1, k - n + TB)

        PEEL = 5
        assert (ETILES - PEEL) % 2 == 0

        def expert_steps(eng, step, lag):
            for s in range(PEEL):
                step(s, s % 2, lambda n, s=s: s >= n, lambda n, s=s: (s - n) // 2)
            with eng.Fori(0, (ETILES - PEEL) // 2) as m:
                for j in range(2):
                    step(m * 2 + (PEEL + j), (PEEL + j) % 2, lambda n: True,
                         lambda n, j=j: m + (PEEL + j - n) // 2)
            for s in range(ETILES, ETILES + lag):
                step(s, s % 2, lambda n, s=s: s - n < ETILES, lambda n, s=s: (s - n) // 2)

        block = ctx.enter_context(nc.Block())

        @block.sync
        def _(sp):
            def first_pass(b, k, have):
                t = b * TB + k
                if have(X1BUFS):
                    sp.wait_ge(xhat_done, t - X1BUFS + 1)
                sp.dma_start(x1_bufs[k % X1BUFS], x_v[:, bass.ds(b, 1), k, :]).then_inc(x1_in[k % X1BUFS], 16)
                if have(GBUFS):
                    sp.wait_ge(wglo_done, t - GBUFS + 1)
                sp.dma_start(stage_g[:, k % GBUFS, :], wg[:, bass.ds(t * G_CHUNK, G_CHUNK)])\
                  .then_inc(wg_in[k % GBUFS], 16)

            def modulation_weights():
                sp.dma_start(wmod_sb[:], wmod).then_inc(wmod_in, 16)

            def attention_weights():
                for dst, src in ((wqkv_sb, wqkv_t), (brow, bkv_row.partition_broadcast(BATCH)), (bq_c, bq_cols),
                                 (gn_c, gn_cols), (wq_sb, wq), (wo_sb, wo_t), (outb_bc, out_b.partition_broadcast(P))):
                    sp.dma_start(dst[:], src).then_inc(attw_in, 16)

            token_steps(sp, first_pass, 0, 2, {GBUFS - 1: modulation_weights, GBUFS + 2: attention_weights})

            sp.wait_ge(att_ev["c0"], BATCH)
            sp.dma_start(sb_bc[:], mod_dram[:, 1, :].partition_broadcast(P)).then_inc(scb_in, 16)
            sp.dma_start(cb_bc[:], mod_dram[:, 2, :].partition_broadcast(P)).then_inc(scb_in, 16)

            def second_pass(b, k, have):
                t = b * TB + k
                if have(1):
                    if have(3):
                        sp.wait_ge(d_wlo, t - 2)
                    sp.dma_start(stage_d[:, (k - 1) % 2, :], wd[:, bass.ds((t - 1) * D_CHUNK, D_CHUNK)])\
                      .then_inc(wd_in[(k - 1) % 2], 16)
                if have(6):
                    bo, ko = back(b, k, 6)
                    sp.wait_ge(d_h2, t - 5)
                    sp.dma_start(h2_v[:, bass.ds(bo, 1), ko, :], h2[:, k % 2:k % 2 + 1, :]).then_inc(h2_out[k % 2], 16)
                if have(4):
                    bo, ko = back(b, k, 4)
                    sp.wait_ge(d_x2, t - 3)
                    sp.dma_start(x2_v[:, bass.ds(bo, 1), ko, :], x2buf[:, k % 2:k % 2 + 1, :]).then_inc(x2_out[k % 2], 16)
                if have(0):
                    sp.dma_start(xbuf[:, k % XBUFS:k % XBUFS + 1, :], x_v[:, bass.ds(b, 1), k, :])\
                      .then_inc(x2_in[k % XBUFS], 16)

            token_steps(sp, second_pass, 6)

            sp.wait_ge(e_y, ETILES)
            sp.dma_start(gb_bc[:], mod_dram[:, 3, :].partition_broadcast(P)).then_inc(gb_in, 16)

            def last_pass(b, h, first):
                q = 2 * b + h
                if not first:
                    sp.wait_ge(f_o, q - 1)
                part = slice(QUAD * h, QUAD * h + QUAD)
                sp.dma_start(fin_x2[:, h, :, :], x2_v[:, bass.ds(b, 1), part, :].rearrange("p b k d -> p (b k) d"))\
                  .then_inc(f_in[h], 16)
                if first:
                    for i in range(2):
                        sp.wait_ge(e_out[i], 16 * ((ETILES - i + 1) // 2))
                for c, buf in ((0, fin_y0), (1, fin_y1)):
                    sp.dma_start(buf[:, h, :, :], y_v[:, c, bass.ds(b, 1), part, :].rearrange("p b k d -> p (b k) d"))\
                      .then_inc(f_in[h], 16)

            def last_store(b, h):
                q = 2 * b + h
                part = slice(QUAD * h, QUAD * h + QUAD)
                sp.wait_ge(f_o, q + 1)
                sp.dma_start(out_v[:, bass.ds(b, 1), part, :].rearrange("p b k d -> p (b k) d"), fin_v[:, h, :, :])\
                  .then_inc(f_out[h], 16)

            for h in range(2):
                last_pass(0, h, True)
            with sp.Fori(1, BATCH) as b:
                for h in range(2):
                    last_store(b - 1, h)
                    last_pass(b, h, False)
            for h in range(2):
                last_store(BATCH - 1, h)
            for h in range(2):
                sp.wait_ge(f_out[h], 16 * BATCH)
            for i in range(2):
                sp.wait_ge(e_out[i], 16 * ((ETILES - i + 1) // 2))
                sp.wait_ge(h2_out[i], 16 * (TILES // 2))
            for i in range(2):
                sp.wait_ge(x2_out[i], 16 * (TILES // 2))

        @block.scalar
        def _(act):
            act.dma_start(c_sb[:], c_t).then_inc(c_in, 16)
            act.wait_ge(c_in, 16)
            act.activation(cs_sb[:], c_sb[:], ACT.Silu).then_inc(cond_act, 1)
            act.wait_ge(zero_set, ZEROS_SET)

            def modulation_rows():
                act.wait_ge(mod_prod, 2)
                for n in range(2):
                    act.activation(mod_sb[:, n * 2 * D:(n + 1) * 2 * D], bank[4 + n][0:BATCH, :], ACT.Copy)\
                       .then_inc(mod_rows, 1)

            def first_pass(b, k, have):
                t = b * TB + k
                i, o = k % 2, 1 - k % 2
                if have(1):
                    act.wait_ge(mv_done, t)
                    act.activation(std[:, o:o + 1], mv[:, o, 1:2], ACT.Sqrt, bias=eps_col[:, 0:1]).then_inc(std_done, 1)
                if have(2):
                    act.wait_ge(nmr_done, t - 1)
                    if have(4):
                        act.wait_ge(gram_done, t - 3)
                    act.activation(xhat[:, i, 0:D], x1_bufs[(k - 2) % X1BUFS][:, 0, :], ACT.Identity,
                                   scale=rstd1[:, bass.ds(t - 2, 1)], bias=nmr1[:, bass.ds(t - 2, 1)])\
                       .then_inc(xhat_done, 1)
                if have(0):
                    act.wait_ge(wg_in[k % GBUFS], 16 * (TB // GBUFS * b + k // GBUFS + 1))
                    act.activation(wg_hi[:, bass.ds(t * G_CHUNK, G_CHUNK)], stage_g[:, k % GBUFS, :], ACT.Copy)\
                       .then_inc(wghi_done, 1)

            token_steps(act, first_pass, 2, 2, {11: modulation_rows})

            act.wait_ge(mod_cols, 2)
            for b in range(0, BATCH, 2):
                act.wait_ge(gram_done, TB * (b + 1))
                for out_, in_ in gram_copies(b):
                    act.activation(out_, in_, ACT.Copy)
                for i, (out_, in_, scale) in enumerate(gram_scalings(b)):
                    ins = act.activation(out_, in_, ACT.Copy, scale=scale)
                ins.then_inc(att_ev["gram_a"], 1)
            act.wait_ge(mod_out, 16)
            act.wait_ge(bkv_in, 16 * BATCH)
            for b in range(BATCH):
                act.wait_ge(att_pe["g21"], b + 1)
                act.activation(gram[:, b, 1, 0:P], bank[4 + b][:, 0:P], ACT.Copy, scale=sc_cols[:, HC + 1, b:b + 1])
                act.activation(xs_row[0:1, b, :], bank[4 + b][0:1, P:3 * P], ACT.Copy).then_inc(att_ev["g21"], 1)
            for b in range(BATCH):
                act.wait_ge(att_pe["p1"], b + 1)
                for i in range(HC):
                    ins = act.activation(p1[:, b, i, :], bank[b][:, i * D:(i + 1) * D], ACT.Copy,
                                         scale=sc_cols[:, HC + i, b:b + 1])
                ins.then_inc(att_ev["p1"], 1)
            for b in range(BATCH):
                act.wait_ge(att_pe["acn"], b + 1)
                act.activation(a_cn[:, b, :, :], bank[b][:, :].rearrange("p (i d) -> p i d", i=HC), ACT.Copy)\
                   .then_inc(att_ev["acn"], 1)
            for b in range(BATCH):
                act.wait_ge(att_pe["cols"], b + 1)
                act.activation(cols[:, b, :], bank[4 + b][:, 0:6], ACT.Copy).then_inc(att_ev["cols"], 1)
            act.wait_ge(stat_pe, 2)
            act.activation(stat[:, 5, :, :], bank[1][:, 0:BATCH * HC].rearrange("p (b j) -> p b j", b=BATCH),
                           ACT.Sqrt, bias=eps_col[:, 0:1]).then_inc(stat_std, 1)
            act.wait_ge(stat_step, STAT_SCALE)
            for b in range(BATCH):
                for j in range(HC):
                    ins = act.activation(a_cn[:, b, j, :], a_cn[:, b, j, :], ACT.Copy, scale=stat[:, 6, b, j:j + 1])
                ins.then_inc(att_ev["scaled"], 1)

            def second_pass(b, k, have):
                t = b * TB + k
                i, o = k % 2, 1 - k % 2
                if have(5):
                    act.wait_ge(d_th, t - 4)
                    if have(7):
                        act.wait_ge(d_gate, t - 6)
                    act.activation(hd_hi[:, o, :, :], bank[2][:, 0:D].rearrange("p (i q) -> p i q", i=HC), ACT.Copy)\
                       .then_inc(d_hi, 1)
                if have(6):
                    act.wait_ge(d_gate, t - 5)
                    act.activation(bank[3 + i][:, :], bank[3 + i][:, :], ACT.Square).then_inc(d_sq, 1)
                if have(3):
                    act.wait_ge(d_mv, t - 2)
                    act.activation(std2[:, o:o + 1], mv2[:, o, 1:2], ACT.Sqrt, bias=eps_col[:, 0:1]).then_inc(d_std, 1)
                if have(0):
                    act.wait_ge(x2_in[k % XBUFS], 16 * (TB // XBUFS * b + k // XBUFS + 1))
                    if have(2):
                        act.wait_ge(d_tx, t - 1)
                    act.activation(xhat[:, i, 0:D], xbuf[:, k % XBUFS, :], ACT.Identity, scale=rstd1[:, bass.ds(t, 1)],
                                   bias=nmr1[:, bass.ds(t, 1)]).then_inc(d_xhat, 1)
                if have(1):
                    act.wait_ge(d_tx, t)
                    if have(2):
                        act.wait_ge(d_c, t - 1)
                    act.activation(xt[:], bank[0][:, 0:D].rearrange("p (i q) -> p i q", i=HC), ACT.Copy)\
                       .then_inc(d_xt, 1)
                if have(0):
                    act.wait_ge(wd_in[i], 16 * (TB // 2 * b + k // 2 + 1))
                    act.activation(wd_hi[:, bass.ds(t * D_CHUNK, D_CHUNK)], stage_d[:, i, :], ACT.Copy)\
                       .then_inc(d_whi, 1)

            token_steps(act, second_pass, 6)

            act.wait_ge(d_sum, TILES)
            act.activation(ssum[:], ssum[:], ACT.Sqrt).then_inc(scores_done, 1)
            act.wait_ge(diff_done, 1)
            act.activation(weight[:, 1, :], weight[:, 0, :], ACT.Exp).then_inc(exp_done, 1)

            def expert_step(s, par, have, uses):
                o = 1 - par
                if have(2):
                    act.wait_ge(e_g, s - 1)
                    if have(3):
                        act.wait_ge(e_act, s - 2)
                    act.activation(silu[:], bank[2][:, :], ACT.Silu).then_inc(e_silu, 1)
                if have(0):
                    act.wait_ge(e_th, s + 1)
                    if have(2):
                        act.wait_ge(e_gh, s - 1)
                    act.activation(h_hi[:, par, :, :], bank[4][:, 0:D].rearrange("p (i q) -> p i q", i=HC), ACT.Copy)\
                       .then_inc(e_hi, 1)
                if have(3):
                    act.wait_ge(e_y, s - 2)
                    if have(5):
                        act.wait_ge(e_out[o], 16 * uses(3))
                    act.activation(y[:, o, :], bank[7][:, 0:D], ACT.Copy).then_inc(e_ys, 1)
                if have(1):
                    act.wait_ge(e_tg, s)
                    if have(3):
                        act.wait_ge(e_g, s - 2)
                    act.activation(gt[:, o, :], bank[6][:, 0:P], ACT.Copy).then_inc(e_gthi, 1)
                if have(2):
                    act.wait_ge(e_ta, s - 1)
                    if have(3):
                        act.wait_ge(e_y, s - 2)
                    act.activation(act_hi[:], bank[3][:, :].rearrange("p (c q) -> p c q", c=FC), ACT.Copy)\
                       .then_inc(e_ahi, 1)

            expert_steps(act, expert_step, E_LAG)

            def last_pass(b, h):
                act.wait_ge(f_in[h], 48 * (b + 1))
                for k in range(QUAD):
                    ins = act.activation(fin_u[:, h, k, :], fin_y0[:, h, k, :], ACT.Copy,
                                         scale=weight[:, 0, bass.ds(b * TB + h * QUAD + k, 1)])
                ins.then_inc(f_u, 1)

            with act.Fori(0, BATCH) as b:
                for h in range(2):
                    last_pass(b, h)

        @block.tensor
        def _(pe):
            def transpose(out_, in_):
                return pe.transpose(out_, in_, ident[0:in_.shape[0], 0:in_.shape[0]])

            def modulation_rows(n, i):
                if n + i == 0:
                    pe.wait_ge(cond_act, 1)
                    pe.wait_ge(wmod_in, 16)
                ins = pe.matmul(bank[4 + n][0:BATCH, :], cs_sb[:, i, :],
                                wmod_sb[:, i, (n + 1) * 2 * D:(n + 2) * 2 * D], start=(i == 0), stop=(i == HC - 1))
                if i == HC - 1:
                    ins.then_inc(mod_prod, 1)

            def modulation_columns():
                for q in range(2 * HC):
                    for i in range(HC):
                        ins = pe.matmul(bank[6][:, q * BATCH:(q + 1) * BATCH], wmod_sb[:, i, q * P:(q + 1) * P],
                                        cs_sb[:, i, :], start=(i == 0), stop=(i == HC - 1))
                ins.then_inc(mod_prod, 1)

            def biases_q():
                pe.wait_ge(mod_rows, 2)
                pe.wait_ge(mod_cols, 1)
                pe.wait_ge(attw_in, 7 * 16)
                for j in range(HC):
                    for i in range(HC):
                        ins = pe.matmul(bank[5][:, j * BATCH:(j + 1) * BATCH], wqkv_sb[:, i, j * P:(j + 1) * P],
                                        sc_cols[:, i, :], start=(i == 0), stop=(i == HC - 1))
                ins.then_inc(bias_prod, 1)

            def biases_kv(i):
                ins = pe.matmul(bank[7][0:BATCH, :], sc_cols[:, i, :], wqkv_sb[:, i, D:3 * D],
                                start=(i == 0), stop=(i == HC - 1))
                if i == HC - 1:
                    ins.then_inc(bias_prod, 1)

            def banks_free():
                pe.wait_ge(mod_rows, 2)
                pe.wait_ge(mod_cols, 2)
                pe.wait_ge(bias_set, 2)

            def first_pass(b, k, have):
                t = b * TB + k
                xb = xhat[:, k % 2, :]
                pe.wait_ge(xhat_done, t + 1)
                pe.matmul(ps[:, bass.ds(2 * b, 1), 0:D + 1], xb[:, 0:P], xb[:, 0:D + 1],
                          start=(k == 0), stop=(k == TB - 1))
                pe.matmul(ps[:, bass.ds(2 * b + 1, 1), 0:P + 1], xb[:, P:D], xb[:, P:D + 1],
                          start=(k == 0), stop=(k == TB - 1)).then_inc(gram_done, 1)

            token_steps(pe, first_pass, 0, 2, {
                5: lambda: modulation_rows(0, 0), 6: lambda: modulation_rows(0, 1), 7: lambda: modulation_rows(1, 0),
                8: lambda: modulation_rows(1, 1), 9: modulation_columns, 11: biases_q, 12: lambda: biases_kv(0),
                13: lambda: biases_kv(1), 15: banks_free})
            pe.wait_ge(const_set, POOL_CONSTS)

            pe.wait_ge(att_ev["gram_a"], BATCH // 2)
            pe.wait_ge(att_ev["gram_v"], BATCH // 2)
            for b in range(BATCH):
                transpose(bank[4 + b][:, 0:P], g12[:, b, :])
                for i in range(HC):
                    ins = transpose(bank[4 + b][0:1, (i + 1) * P:(i + 2) * P], xs_raw[:, b, i:i + 1])
                ins.then_inc(att_pe["g21"], 1)
            pe.wait_ge(bkv_in, 16 * BATCH)
            for b in range(BATCH):
                pe.wait_ge(att_ev["g21"], b + 1)
                for i in range(HC):
                    for m in range(HC):
                        pe.matmul(bank[b][:, i * D:(i + 1) * D], gram[:, b, m, i * P:(i + 1) * P],
                                  wqkv_sb[:, m, 2 * D:3 * D], start=(m == 0), stop=False)
                    ins = pe.matmul(bank[b][:, i * D:(i + 1) * D], xs_row[0:1, b, i * P:(i + 1) * P],
                                    bkv[0:1, b, D:2 * D], start=False, stop=True)
                ins.then_inc(att_pe["p1"], 1)
                for m in range(HC):
                    ins = pe.matmul(bank[4 + b][0:1, 0:D], gram[:, b, m, D:D + 1], wqkv_sb[:, m, 2 * D:3 * D],
                                    start=(m == 0), stop=(m == HC - 1))
                ins.then_inc(att_pe["rv"], 1)
            for b in range(BATCH):
                pe.wait_ge(att_ev["p1"], b + 1)
                pe.wait_ge(att_ev["rv"], b + 1)
                for j in range(HC):
                    o = bank[4 + b][:, j * P:(j + 1) * P]
                    for m in range(HC):
                        pe.matmul(o, wqkv_sb[:, m, D + j * P:D + (j + 1) * P], p1[:, b, m, j * P:(j + 1) * P],
                                  start=(m == 0), stop=False)
                    ins = pe.matmul(o, bkv[0:1, b, j * P:(j + 1) * P], rv_row[0:1, b, j * P:(j + 1) * P],
                                    start=False, stop=True)
                ins.then_inc(att_pe["kv"], 1)
            for b in range(BATCH):
                pe.wait_ge(att_ev["kv"], b + 1)
                for j in range(HC):
                    ins = pe.matmul(bank[b][:, j * D:(j + 1) * D], kv[:, b, j, :], wq_sb[:, j, :], start=True, stop=True)
                ins.then_inc(att_pe["acn"], 1)
                for i in range(HC):
                    for j in range(HC):
                        ins = pe.matmul(bank[4 + b][:, i * D + j * P:i * D + (j + 1) * P], wq_sb[:, j, i * P:(i + 1) * P],
                                        kv[:, b, j, :], start=True, stop=True)
                ins.then_inc(att_pe["anc"], 1)
            for b in range(BATCH):
                pe.wait_ge(att_ev["acn"], b + 1)
                pe.wait_ge(att_ev["anc"], b + 1)
                for i in range(HC):
                    for m in range(HC):
                        ins = pe.matmul(bank[b][:, i * D:(i + 1) * D], gram[:, b, m, i * P:(i + 1) * P], a_nc[:, b, m, :],
                                        start=(m == 0), stop=(m == HC - 1))
                ins.then_inc(att_pe["prod"], 1)
                for j in range(HC):
                    pe.matmul(bank[4 + b][:, j:j + 1], kv[:, b, j, :], bq_all[:, j, b:b + 1], start=True, stop=True)
                for j in range(HC):
                    for m in range(HC):
                        pe.matmul(bank[4 + b][:, 2 + j:3 + j], a_nc[:, b, m, j * P:(j + 1) * P], gram[:, b, m, D:D + 1],
                                  start=(m == 0), stop=(m == HC - 1))
            for b in range(BATCH):
                pe.wait_ge(att_ev["prod"], b + 1)
                for j in range(HC):
                    for m in range(HC):
                        ins = pe.matmul(bank[4 + b][:, 4 + j:5 + j], p1[:, b, m, j * P:(j + 1) * P], ones_col[:, 0:1],
                                        start=(m == 0), stop=(m == HC - 1))
                ins.then_inc(att_pe["cols"], 1)
            for n, (row, step) in enumerate(((1, STAT_MU), (4, STAT_SQ))):
                pe.wait_ge(stat_step, step)
                pe.matmul(bank[n][:, 0:BATCH * HC], headavg[:], stat[:, row, :, :].rearrange("p b j -> p (b j)"),
                          start=True, stop=True).then_inc(stat_pe, 1)
            pe.wait_ge(stat_std, 1)
            pe.wait_ge(stat_step, STAT_SHIFT)
            for b in range(BATCH):
                pe.wait_ge(att_ev["scaled"], b + 1)
                for i in range(HC):
                    for j in range(HC):
                        ins = pe.matmul(bank[b][:, i * D:(i + 1) * D], a_cn[:, b, j, i * P:(i + 1) * P], wo_sb[:, j, :],
                                        start=(j == 0), stop=(j == HC - 1))
                ins.then_inc(att_pe["c"], 1)
                pe.wait_ge(att_ev["ones"], b + 1)
                for j in range(HC):
                    ins = pe.matmul(bank[4 + b][:, 0:D], p1[:, b, j, 0:P], wo_sb[:, j, :],
                                    start=(j == 0), stop=(j == HC - 1))
                ins.then_inc(att_pe["c0"], 1)

            pe.wait_ge(att_ev["c0"], BATCH)
            pe.wait_ge(att_ev["c"], BATCH)
            pe.wait_ge(wglo_done, TILES)

            def three(out_, hi, lo, w_hi, w_lo, first, last):
                pe.matmul(out_, hi, w_hi, start=first, stop=False)
                pe.matmul(out_, hi, w_lo, start=False, stop=False)
                return pe.matmul(out_, lo, w_hi, start=False, stop=last)

            def second_pass(b, k, have):
                t = b * TB + k
                i, o = k % 2, 1 - k % 2
                if have(1):
                    pe.wait_ge(d_xhat, t)
                    if have(2):
                        pe.wait_ge(d_xt, t - 1)
                    transpose(bank[0][:, 0:P], xhat[:, o, 0:P])
                    transpose(bank[0][:, P:D], xhat[:, o, P:D]).then_inc(d_tx, 1)
                if have(2):
                    bo, _ = back(b, k, 2)
                    pe.wait_ge(d_xt, t - 1)
                    if have(3):
                        pe.wait_ge(d_x2, t - 2)
                    for m in range(HC):
                        ins = pe.matmul(bank[1][:, 0:D], xt[:, m, :], c_mat[:, bass.ds(bo, 1), m, :],
                                        start=(m == 0), stop=(m == HC - 1))
                    ins.then_inc(d_c, 1)
                if have(5):
                    pe.wait_ge(d_lo, t - 4)
                    if have(7):
                        pe.wait_ge(d_sum, t - 6)
                    for m in range(HC):
                        w = slice(m * FF, (m + 1) * FF)
                        ins = three(bank[3 + o][:, :], hd_hi[:, o, m, :], hd_lo[:, o, m, :], wg_hi[:, w], wg_lo[:, w],
                                    m == 0, m == HC - 1)
                    ins.then_inc(d_gate, 1)
                if have(4):
                    pe.wait_ge(d_h2, t - 3)
                    if have(5):
                        pe.wait_ge(d_lo, t - 4)
                    transpose(bank[2][:, 0:P], h2[:, i, 0:P])
                    transpose(bank[2][:, P:D], h2[:, i, P:D]).then_inc(d_th, 1)

            token_steps(pe, second_pass, 5)

            pe.wait_ge(pick_done, 1)
            pe.wait_ge(route_pool, ROUTE_CONSTS)
            picked = both[:].rearrange("p t e -> p (t e)")
            pe.matmul(bank[5][:, 0:TILES * EXPERTS], upper[:], picked, start=True, stop=True)
            pe.matmul(bank[6][:, 0:TILES * EXPERTS], ones_m[:], picked, start=True, stop=True).then_inc(count_pe, 1)

            def table_part(n, j, first, last):
                pe.wait_ge(onehot_done, n + 1)
                pe.matmul(bank[7][:, 0:ETILES], in_row[:, j, :], in_col[:, j, :], start=first, stop=last)\
                  .then_inc(table_pe, 1)

            for j in range(4):
                table_part(j, j, j == 0, False)
            with pe.Fori(1, TOPK * TILES // 4 - 1) as m:
                for j in range(4):
                    table_part(m * 4 + j, j, False, False)
            for j in range(4):
                table_part(TOPK * TILES - 4 + j, j, False, j == 3)

            pe.wait_ge(route_done, 1)
            pe.wait_ge(d_wlo, TILES)

            def expert_step(s, par, have, uses):
                _, (e_down, e_g_, e_gate, e_up_) = nc.values_load_multi_w_load_instructions(
                    tile_expert[0:1, bass.ds(s, E_LAG + 1)], engines=[mybir.EngineType.PE], min_val=0,
                    max_val=EXPERTS - 1, skip_runtime_bounds_check_because="counts of thresholds among EXPERTS - 1")
                o = 1 - par
                if have(2):
                    pe.wait_ge(e_gtlo, s - 1)
                    if have(3):
                        pe.wait_ge(e_silu, s - 2)
                    w = bass.ds(e_g_ * FF + A_W, FF)
                    pe.matmul(bank[2][:, :], gt[:, par, :], wg_hi[:, w], start=True, stop=False)
                    pe.matmul(bank[2][:, :], gt[:, par, :], wg_lo[:, w], start=False, stop=True).then_inc(e_g, 1)
                if have(1):
                    pe.wait_ge(e_lo, s)
                    if have(2):
                        pe.wait_ge(e_ghs, s - 1)
                    for m in range(HC):
                        w = wg_parts[:, :, bass.ds(e_gate * RANK + m * FF, RANK)]
                        pe.matmul(bank[5][:, 0:2 * RANK], h_hi[:, o, m, :], w, start=(m == 0), stop=False)
                        ins = pe.matmul(bank[5][:, 0:2 * RANK], h_lo[:, o, m, :], w, start=False, stop=(m == HC - 1))
                    ins.then_inc(e_gh, 1)
                if have(0):
                    pe.wait_ge(e_rows[par], 16 * (uses(0) + 1))
                    if have(1):
                        pe.wait_ge(e_lo, s)
                    transpose(bank[4][:, 0:P], rows[:, par, 0:P])
                    transpose(bank[4][:, P:D], rows[:, par, P:D]).then_inc(e_th, 1)
                if have(3):
                    pe.wait_ge(e_alo, s - 2)
                    if have(4):
                        pe.wait_ge(e_ys, s - 3)
                    for c in range(FC):
                        w = bass.ds(e_down * (FC * D) + c * D, D)
                        ins = three(bank[7][:, 0:D], act_hi[:, c, :], act_lo[:, c, :], wd_hi[:, w], wd_lo[:, w],
                                    c == 0, c == FC - 1)
                    ins.then_inc(e_y, 1)
                if have(1):
                    pe.wait_ge(e_ghs, s)
                    if have(2):
                        pe.wait_ge(e_gtlo, s - 1)
                    transpose(bank[6][:, 0:P], gh[:, o, :, :].rearrange("p a r -> p (a r)")).then_inc(e_tg, 1)
                if have(2):
                    pe.wait_ge(e_act, s - 1)
                    if have(3):
                        pe.wait_ge(e_alo, s - 2)
                    for c in range(FC):
                        ins = transpose(bank[3][:, c * P:(c + 1) * P], act_[:, par, c * P:(c + 1) * P])
                    ins.then_inc(e_ta, 1)
                if have(0):
                    pe.wait_ge(e_lo, s + 1)
                    if have(2):
                        pe.wait_ge(e_act, s - 1)
                    for m in range(HC):
                        w = bass.ds(e_up_ * (HC * FF) + (A_W + B_W + m * FF), FF)
                        ins = three(bank[par][:, :], h_hi[:, par, m, :], h_lo[:, par, m, :],
                                    wg_hi[:, w], wg_lo[:, w], m == 0, m == HC - 1)
                    ins.then_inc(e_up, 1)

            expert_steps(pe, expert_step, E_LAG)

        @block.vector
        def _(dve):
            for n, (t_, v) in enumerate(((eps_col, EPS), (ones_col, 1.0))):
                dve.memset(t_[:], v).then_inc(zero_set, 1)
            for i in range(2):
                dve.memset(xhat[:, i, D:D + 1], 1.0).then_inc(zero_set, 1)

            count = {}

            def then(ins, s):
                count[s.name] = count.get(s.name, 0) + 1
                ins.then_inc(s, 1)
                dve.wait_ge(s, count[s.name])


            def modulation_columns():
                dve.wait_ge(mod_prod, 3)
                v = bank[6][:, 0:2 * HC * BATCH].rearrange("p (q b) -> p q b", b=BATCH)
                dve.tensor_copy(sc_cols[:, 0:HC, :], v[:, 0:HC, :]).then_inc(mod_cols, 1)
                dve.tensor_scalar(sc_cols[:, HC:2 * HC, :], v[:, HC:2 * HC, :], 1.0, None, ALU.add).then_inc(mod_cols, 1)

            def biases():
                dve.wait_ge(attw_in, 7 * 16)
                dve.wait_ge(bias_prod, 2)
                dve.tensor_tensor(bq_all[:], bank[5][:, 0:HC * BATCH].rearrange("p (j b) -> p j b", b=BATCH),
                                  bq_c[:].unsqueeze(2).to_broadcast([P, HC, BATCH]), ALU.add).then_inc(bias_set, 1)
                dve.tensor_tensor(bkv_rows[:], bank[7][0:BATCH, :], brow[:], ALU.add).then_inc(bias_set, 1)

            def first_pass(b, k, have):
                t = b * TB + k
                i, o = k % 2, 1 - k % 2
                if have(0):
                    dve.wait_ge(x1_in[k % X1BUFS], 16 * (TB // X1BUFS * b + k // X1BUFS + 1))
                    dve.bn_stats(bn[:, i, :], x1_bufs[k % X1BUFS][:, 0, :]).then_inc(bn_done, 1)
                if have(1):
                    dve.wait_ge(std_done, t)
                    dve.reciprocal(rstd1[:, bass.ds(t - 1, 1)], std[:, o:o + 1]).then_inc(rstd_done, 1)
                if have(1):
                    dve.wait_ge(wghi_done, t)
                    chunk = bass.ds((t - 1) * G_CHUNK, G_CHUNK)
                    dve.tensor_tensor(wg_lo[:, chunk], stage_g[:, (k - 1) % GBUFS, :], wg_hi[:, chunk].bitcast(F32),
                                      ALU.subtract).then_inc(wglo_done, 1)
                if have(0):
                    dve.wait_ge(bn_done, t + 1)
                if have(1):
                    dve.wait_ge(rstd_done, t)
                    dve.scalar_tensor_tensor(out=nmr1[:, bass.ds(t - 1, 1)], in0=mv[:, o, 0:1], scalar=-1.0,
                                             in1=rstd1[:, bass.ds(t - 1, 1)], op0=ALU.mult, op1=ALU.mult)\
                       .then_inc(nmr_done, 1)
                if have(0):
                    dve.bn_aggr(mv[:, i, :], bn[:, i, :]).then_inc(mv_done, 1)

            token_steps(dve, first_pass, 1, 2, {12: modulation_columns, 15: biases})

            for b in range(1, BATCH, 2):
                dve.wait_ge(gram_done, TB * (b + 1))
                for out_, in_ in gram_copies(b):
                    dve.tensor_copy(out_, in_)
                for out_, in_, scale in gram_scalings(b):
                    ins = dve.tensor_scalar(out_, in_, scale, None, ALU.mult)
                ins.then_inc(att_ev["gram_v"], 1)
            dve.wait_ge(bkv_in, 16 * BATCH)
            for b in range(BATCH):
                dve.wait_ge(att_pe["rv"], b + 1)
                dve.scalar_tensor_tensor(out=rv_row[0:1, b, :], in0=bkv[0:1, b, D:2 * D], scalar=float(SEQ),
                                         in1=bank[4 + b][0:1, 0:D], op0=ALU.mult, op1=ALU.add)\
                   .then_inc(att_ev["rv"], 1)
            for b in range(BATCH):
                dve.wait_ge(att_pe["kv"], b + 1)
                dve.tensor_tensor(kv[:, b, :, :], bank[4 + b][:, 0:D].rearrange("p (j q) -> p j q", j=HC),
                                  headmask[:].unsqueeze(1).to_broadcast([P, HC, P]), ALU.mult)\
                   .then_inc(att_ev["kv"], 1)
            for b in range(BATCH):
                dve.wait_ge(att_pe["anc"], b + 1)
                dve.tensor_copy(a_nc[:, b, :, :], bank[4 + b][:, :].rearrange("p (i d) -> p i d", i=HC))\
                   .then_inc(att_ev["anc"], 1)
            for b in range(BATCH):
                dve.wait_ge(att_pe["prod"], b + 1)
                for i in range(HC):
                    ins = dve.scalar_tensor_tensor(out=p1[:, b, i, :], in0=bank[b][:, i * D:(i + 1) * D],
                                                   scalar=sc_cols[:, HC + i, b:b + 1], in1=a_nc[:, b, i, :],
                                                   op0=ALU.mult, op1=ALU.mult)
                ins.then_inc(att_ev["prod"], 1)

            dve.wait_ge(att_ev["cols"], BATCH)
            a0, axs, sq = cols[:, :, 0:2], cols[:, :, 2:4], cols[:, :, 4:6]
            mean, mu, var, dev, dev2, std_, scale, shift = (stat[:, n, :, :] for n in range(8))

            def spread(col):
                return gn_c[:, col, :].unsqueeze(1).to_broadcast([P, BATCH, HC])

            def heads(n):
                return bank[n][:, 0:BATCH * HC].rearrange("p (b j) -> p b j", b=BATCH)

            then(dve.tensor_scalar(mean, axs, 1.0 / SEQ, None, ALU.mult), stat_step)
            then(dve.scalar_tensor_tensor(out=mu, in0=axs, scalar=1.0 / SEQ, in1=a0, op0=ALU.mult, op1=ALU.add), stat_step)
            assert count[stat_step.name] == STAT_MU
            then(dve.tensor_tensor(dev, mean, mean, ALU.mult), stat_step)
            then(dve.scalar_tensor_tensor(out=var, in0=sq, scalar=1.0 / SEQ, in1=dev, op0=ALU.mult, op1=ALU.subtract),
                 stat_step)
            dve.wait_ge(stat_pe, 1)
            then(dve.tensor_tensor(dev, mu, heads(0), ALU.subtract), stat_step)
            then(dve.tensor_tensor(mean, a0, heads(0), ALU.subtract), stat_step)
            then(dve.tensor_tensor(dev, dev, dev, ALU.mult), stat_step)
            then(dve.scalar_tensor_tensor(out=dev2, in0=var, scalar=0.0, in1=dev, op0=ALU.max, op1=ALU.add), stat_step)
            assert count[stat_step.name] == STAT_SQ
            dve.wait_ge(stat_std, 1)
            then(dve.reciprocal(scale, std_), stat_step)
            then(dve.tensor_tensor(scale, scale, spread(0), ALU.mult), stat_step)
            assert count[stat_step.name] == STAT_SCALE
            then(dve.tensor_tensor(shift, mean, scale, ALU.mult), stat_step)
            then(dve.tensor_tensor(shift, shift, spread(1), ALU.add), stat_step)
            assert count[stat_step.name] == STAT_SHIFT
            dve.wait_ge(ga_in, 16)
            for b in range(BATCH):
                dve.wait_ge(att_pe["c"], b + 1)
                for i in range(HC):
                    ins = dve.scalar_tensor_tensor(out=c_mat[:, b, i, :], in0=bank[b][:, i * D:(i + 1) * D],
                                                   scalar=sc_cols[:, HC + i, b:b + 1], in1=ga_bc[:, b, :],
                                                   op0=ALU.mult, op1=ALU.mult)
                ins.then_inc(att_ev["c"], 1)
                dve.wait_ge(att_pe["c0"], b + 1)
                dve.tensor_tensor(c0_bc[:, b, :], bank[4 + b][:, 0:D], outb_bc[:], ALU.add).then_inc(att_ev["c0a"], 1)
                dve.wait_ge(att_ev["c0a"], b + 1)
                dve.tensor_tensor(c0_bc[:, b, :], c0_bc[:, b, :], ga_bc[:, b, :], ALU.mult).then_inc(att_ev["c0"], 1)

            def second_pass(b, k, have):
                t = b * TB + k
                i, o = k % 2, 1 - k % 2
                if have(3):
                    dve.wait_ge(d_bn, t - 2)
                if have(5):
                    dve.wait_ge(d_hi, t - 4)
                    dve.tensor_tensor(hd_lo[:, o, :, :], bank[2][:, 0:D].rearrange("p (i q) -> p i q", i=HC),
                                      hd_hi[:, o, :, :].bitcast(F32), ALU.subtract).then_inc(d_lo, 1)
                if have(3):
                    dve.bn_aggr(mv2[:, o, :], bn2[:, o, :]).then_inc(d_mv, 1)
                if have(6):
                    dve.wait_ge(d_sq, t - 5)
                    dve.tensor_reduce(ssum[:, bass.ds(t - 6, 1), :].rearrange("p t e -> p (t e)"),
                                      bank[3 + i][:, :].rearrange("p (e r) -> p e r", e=EXPERTS),
                                      AX_X, ALU.add).then_inc(d_sum, 1)
                if have(3):
                    dve.wait_ge(d_std, t - 2)
                    dve.reciprocal(rstd2[:, o:o + 1], std2[:, o:o + 1]).then_inc(d_rstd, 1)
                if have(2):
                    dve.wait_ge(d_c, t - 1)
                    dve.wait_ge(d_xc, t - 1)
                    if have(4):
                        dve.wait_ge(x2_out[i], 16 * (TB // 2 * b + (k - 2) // 2))
                    dve.tensor_tensor(x2buf[:, i, :], bank[1][:, 0:D], xbuf[:, (k - 2) % XBUFS, :], ALU.add)\
                       .then_inc(d_x2, 1)
                if have(3):
                    dve.wait_ge(d_rstd, t - 2)
                    dve.scalar_tensor_tensor(out=nmr2[:, o:o + 1], in0=mv2[:, o, 0:1], scalar=-1.0,
                                             in1=rstd2[:, o:o + 1], op0=ALU.mult, op1=ALU.mult).then_inc(d_nmr, 1)
                if have(1):
                    dve.wait_ge(d_whi, t)
                    chunk = bass.ds((t - 1) * D_CHUNK, D_CHUNK)
                    dve.tensor_tensor(wd_lo[:, chunk], stage_d[:, o, :], wd_hi[:, chunk].bitcast(F32), ALU.subtract)\
                       .then_inc(d_wlo, 1)
                if have(3):
                    dve.wait_ge(d_nmr, t - 2)
                    if have(5):
                        dve.wait_ge(h2_out[o], 16 * (TB // 2 * b + (k - 3) // 2))
                        dve.wait_ge(d_th, t - 4)
                    dve.tensor_scalar(h2[:, o, :], x2buf[:, o, :], rstd2[:, o:o + 1], nmr2[:, o:o + 1],
                                      ALU.mult, ALU.add).then_inc(d_xn, 1)
                if have(2):
                    dve.wait_ge(d_x2, t - 1)
                    dve.bn_stats(bn2[:, i, :], x2buf[:, i, :]).then_inc(d_bn, 1)

            token_steps(dve, second_pass, 6)

            dve.wait_ge(scores_done, 1)
            for i in range(2):
                dve.wait_ge(x2_out[i], 16 * (TILES // 2))
                dve.wait_ge(h2_out[i], 16 * (TILES // 2))
            dve.wait_ge(d_h2, TILES)
            for t in range(TILES):
                ins = dve.max(top[:, t, :], ssum[:, t, :])
            then(ins, route_step)
            for t in range(TILES):
                ins = dve.max_index(topi[:, t, :], top[:, t, :], ssum[:, t, :])
            dve.tensor_tensor(weight[:, 0, :], top[:, :, 1], top[:, :, 0], ALU.subtract).then_inc(diff_done, 1)
            then(ins, route_step)
            dve.memset(zeros[:], 0.0)
            then(dve.tensor_copy(topf[:], topi[:, :, 0:TOPK].rearrange("p t c -> p c t")), route_step)
            dve.wait_ge(route_pool, ROUTE_CONSTS)
            for c in range(TOPK):
                ins = dve.tensor_tensor(pick[:, c, :, :], iota_row[:, 0:EXPERTS].unsqueeze(1).to_broadcast([P, TILES, EXPERTS]),
                                        topf[:, c, :].unsqueeze(2).to_broadcast([P, TILES, EXPERTS]), ALU.is_equal)
            then(ins, route_step)
            dve.tensor_tensor(both[:], pick[:, 0, :, :], pick[:, 1, :, :], ALU.add).then_inc(pick_done, 1)
            dve.wait_ge(exp_done, 1)
            then(dve.tensor_scalar(weight[:, 0, :], weight[:, 1, :], 1.0, None, ALU.add), route_step)
            then(dve.reciprocal(weight[:, 0, :], weight[:, 0, :]), route_step)
            then(dve.tensor_tensor(weight[:, 1, :], weight[:, 1, :], weight[:, 0, :], ALU.mult), route_step)
            dve.wait_ge(count_pe, 1)
            then(dve.tensor_copy(total[:], bank[6][:, 0:TILES * EXPERTS].rearrange("p (t e) -> p e t", e=EXPERTS)), route_step)
            flat = total[:].rearrange("p e t -> p (e t)")
            then(dve.tensor_tensor_scan(cum[:].rearrange("p e t -> p (e t)"), flat, zeros[:], 0.0, ALU.add, ALU.add),
                 route_step)
            start, number, tiles_f, ends, shift_e = (small[:, n, :] for n in range(5))
            dve.memset(small[:, 0, 0:1], 0.0)
            then(dve.tensor_copy(small[:, 0, 1:EXPERTS], cum[:, 0:EXPERTS - 1, TILES - 1]), route_step)
            then(dve.tensor_tensor(number, cum[:, :, TILES - 1], start, ALU.subtract), route_step)
            then(dve.tensor_scalar(small_i[:, 0, :], number, float(P - 1), None, ALU.add), route_step)
            then(dve.tensor_scalar(small_i[:, 1, :], small_i[:, 0, :], LOG_P, None, ALU.logical_shift_right), route_step)
            then(dve.tensor_copy(tiles_f, small_i[:, 1, :]), route_step)
            then(dve.tensor_tensor_scan(ends, tiles_f, zeros[:, 0:EXPERTS], 0.0, ALU.add, ALU.add), route_step)
            then(dve.tensor_tensor(shift_e, ends, tiles_f, ALU.subtract), route_step)
            then(dve.scalar_tensor_tensor(out=shift_e, in0=shift_e, scalar=float(P), in1=start, op0=ALU.mult,
                                          op1=ALU.subtract), route_step)
            then(dve.tensor_tensor(cum[:], cum[:], total[:], ALU.subtract), route_step)
            then(dve.tensor_tensor(cum[:], cum[:], shift_e.unsqueeze(2).to_broadcast([P, EXPERTS, TILES]), ALU.add), route_step)
            then(dve.tensor_tensor(slot_m[:], bank[5][:, 0:TILES * EXPERTS].rearrange("p (t e) -> p t e", e=EXPERTS),
                                   cum[:].rearrange("p e t -> p t e"), ALU.add), route_step)
            for c in range(TOPK):
                ins = dve.tensor_tensor(slot_k[:, c, :, :], pick[:, c, :, :], slot_m[:], ALU.mult)
            then(ins, route_step)
            then(dve.tensor_reduce(slot[:], slot_k[:].rearrange("p c t e -> p (c t) e"), AX_X, ALU.add), route_step)
            then(dve.tensor_copy(slot_i[:, 0, :], slot[:]), route_step)
            dve.tensor_scalar(slot_i[:, 1, :], slot_i[:, 0, :], P - 1, None, ALU.bitwise_and)
            then(dve.tensor_scalar(slot_i[:, 2, :], slot_i[:, 0, :], LOG_P, None, ALU.logical_shift_right), route_step)
            then(dve.tensor_copy(slot_f[:], slot_i[:, 1:3, :]), route_step)

            def onehots(n, j, first):
                if not first:
                    dve.wait_ge(table_pe, n - 3)
                dve.tensor_scalar(in_row[:, j, :], iota_row[:], slot_f[:, 0, bass.ds(n, 1)], None, ALU.is_equal)
                dve.tensor_scalar(in_col[:, j, :], iota_row[:, 0:ETILES], slot_f[:, 1, bass.ds(n, 1)],
                                  value[:, bass.ds(n, 1)], ALU.is_equal, ALU.mult).then_inc(onehot_done, 1)

            for j in range(4):
                onehots(j, j, True)
            with dve.Fori(1, TOPK * TILES // 4) as m:
                for j in range(4):
                    onehots(m * 4 + j, j, False)

            ef = expert_f[0:1, 0, 0:ETILES]
            then(dve.memset(tile_expert[0:1, :], 0), route_step)
            then(dve.tensor_scalar(ef, iota_row[0:1, 0:ETILES], small[0:1, 3, 0:1], None, ALU.is_ge), route_step)
            for e in range(1, EXPERTS - 1):
                then(dve.scalar_tensor_tensor(out=ef, in0=iota_row[0:1, 0:ETILES], scalar=small[0:1, 3, e:e + 1], in1=ef,
                                              op0=ALU.is_ge, op1=ALU.add), route_step)
            then(dve.tensor_copy(tile_expert[0:1, E_LAG:E_LAG + ETILES], ef), route_step)
            dve.wait_ge(table_pe, TOPK * TILES)
            then(dve.tensor_scalar(pad[:, 0, :], bank[7][:, 0:ETILES], 0.0, value[:, VALUE_PAD:VALUE_PAD + 1],
                                   ALU.is_equal, ALU.mult), route_step)
            then(dve.scalar_tensor_tensor(out=dest[:], in0=bank[7][:, 0:ETILES], scalar=-1.0, in1=pad[:, 0, :],
                                          op0=ALU.add, op1=ALU.add), route_step)
            then(dve.tensor_scalar(token[:], dest[:], TOKENS - 1, None, ALU.bitwise_and), route_step)
            dve.memset(pad[:, 1, :], 0.0).then_inc(route_done, 1)

            def expert_step(s, par, have, uses):
                o = 1 - par
                if have(1):
                    dve.wait_ge(e_gh, s)
                    dve.tensor_reduce(gh[:, o, :, :], bank[5][:, 0:2 * RANK].rearrange("p (w r) -> p r w", w=2)
                                      .unsqueeze(1).to_broadcast([P, 2, RANK, 2]), AX_X, ALU.add).then_inc(e_ghs, 1)
                if have(2):
                    dve.wait_ge(e_silu, s - 1)
                    dve.tensor_tensor(act_[:, par, :], bank[par][:, :], silu[:], ALU.mult).then_inc(e_act, 1)
                if have(0):
                    dve.wait_ge(e_hi, s + 1)
                    dve.tensor_tensor(h_lo[:, par, :, :], bank[4][:, 0:D].rearrange("p (i q) -> p i q", i=HC),
                                      h_hi[:, par, :, :].bitcast(F32), ALU.subtract).then_inc(e_lo, 1)
                if have(1):
                    dve.wait_ge(e_gthi, s)
                    half = slice(RANK, 2 * RANK)
                    dve.tensor_tensor(gt[half, o, :], bank[6][half, 0:P], gt[half, o, :].bitcast(F32), ALU.subtract)\
                       .then_inc(e_gtlo, 1)
                if have(2):
                    dve.wait_ge(e_ahi, s - 1)
                    dve.tensor_tensor(act_lo[:], bank[3][:, :].rearrange("p (c q) -> p c q", c=FC),
                                      act_hi[:].bitcast(F32), ALU.subtract).then_inc(e_alo, 1)

            expert_steps(dve, expert_step, E_LAG)

            def last_pass(b, h, first):
                q = 2 * b + h
                if first:
                    pass
                else:
                    dve.wait_ge(f_out[h], 16 * b)
                dve.wait_ge(f_u, q + 1)
                for k in range(QUAD):
                    ins = dve.scalar_tensor_tensor(out=fin_v[:, h, k, :], in0=fin_y1[:, h, k, :],
                                                   scalar=weight[:, 1, bass.ds(b * TB + h * QUAD + k, 1)],
                                                   in1=fin_u[:, h, k, :], op0=ALU.mult, op1=ALU.add)
                ins.then_inc(f_v, 1)

            def last_sum(b, h):
                q = 2 * b + h
                dve.wait_ge(f_w, q + 1)
                dve.tensor_tensor(fin_v[:, h, :, :], fin_u[:, h, :, :], fin_x2[:, h, :, :], ALU.add).then_inc(f_o, 1)

            last_pass(0, 0, True)
            last_pass(0, 1, True)
            last_sum(0, 0)
            with dve.Fori(1, BATCH) as b:
                last_pass(b, 0, False)
                last_sum(b - 1, 1)
                last_pass(b, 1, False)
                last_sum(b, 0)
            last_sum(BATCH - 1, 1)

        @block.gpsimd
        def _(pool):
            n = 0
            for t_, v in ((ident, 0.0), (headmask, 1.0), (headavg, 1.0 / HEAD)):
                pool.memset(t_[:], v).then_inc(const_set, 1)
                n += 1
            pool.wait_ge(const_set, n)
            pool.affine_select(out=ident[:], in_=ident[:], compare_op=ALU.not_equal, fill=1.0, base=0,
                               pattern=[[-1, P]], channel_multiplier=1).then_inc(const_set, 1)
            for t_ in (headmask, headavg):
                v = t_[:].rearrange("p (g r) -> p g r", r=HEAD)
                pool.affine_select(out=v, in_=v, compare_op=ALU.is_ge, fill=0.0, base=0,
                                   pattern=[[-HEAD, P // HEAD], [0, HEAD]], channel_multiplier=1).then_inc(const_set, 1)
            pool.wait_ge(const_set, n + 3)
            for t_ in (headmask, headavg):
                v = t_[:].rearrange("p (g r) -> p g r", r=HEAD)
                pool.affine_select(out=v, in_=v, compare_op=ALU.is_ge, fill=0.0, base=HEAD - 1,
                                   pattern=[[HEAD, P // HEAD], [0, HEAD]], channel_multiplier=-1).then_inc(const_set, 1)
            assert n + 5 == POOL_CONSTS

            pool.wait_ge(mod_rows, 2)
            row_cb = mod_sb[:, 2 * D:3 * D]
            gates = mod_sb[:, :].rearrange("b (r d) -> b r d", r=4)[:, 0:4:3, :]
            pool.tensor_scalar(row_cb, row_cb, 1.0, None, ALU.add).then_inc(mod_step, 1)
            pool.tensor_scalar(mod_sign[:], gates, 0.0, 2.0, ALU.is_ge, ALU.mult).then_inc(mod_step, 1)
            pool.wait_ge(mod_step, 2)
            pool.tensor_scalar(mod_sign[:], mod_sign[:], -1.0, None, ALU.add).then_inc(mod_step, 1)
            pool.wait_ge(mod_step, 3)
            pool.tensor_tensor(mod_abs[:], mod_sign[:], gates, ALU.mult).then_inc(mod_step, 1)
            pool.wait_ge(mod_step, 4)
            pool.tensor_scalar(mod_abs[:], mod_abs[:], GATE_MIN, None, ALU.max).then_inc(mod_step, 1)
            pool.wait_ge(mod_step, 5)
            pool.tensor_tensor(gates, mod_sign[:], mod_abs[:], ALU.mult).then_inc(mod_step, 1)
            pool.wait_ge(mod_step, 6)
            pool.dma_start(mod_dram.rearrange("b r d -> b (r d)"), mod_sb[:]).then_inc(mod_out, 16)
            pool.wait_ge(bias_set, 2)
            for b in range(BATCH):
                pool.dma_start(bkv[0:1, b, :], bkv_rows[b:b + 1, :]).then_inc(bkv_in, 16)
            pool.wait_ge(mod_out, 16)
            pool.dma_start(ga_bc[:], mod_dram[:, 0, :].partition_broadcast(P)).then_inc(ga_in, 16)

            pool.wait_ge(stat_step, STAT_SHIFT)
            for b in range(BATCH):
                for j in range(HC):
                    ins = pool.tensor_scalar(p1[:, b, j, 0:P], ident[:], 0.0, stat[:, 7, b, j:j + 1], ALU.mult, ALU.add)
                ins.then_inc(att_ev["ones"], 1)

            pool.wait_ge(att_ev["c0"], BATCH)
            pool.wait_ge(scb_in, 32)

            def second_pass(b, k, have):
                t = b * TB + k
                i, o = k % 2, 1 - k % 2
                if have(4):
                    bo, _ = back(b, k, 4)
                    hk = h2[:, i:i + 1, :]
                    pool.wait_ge(d_h2m, t - 3)
                    pool.sem_inc(pool_past, 1)
                    pool.tensor_tensor(hk, hk, sb_bc[:, bass.ds(bo, 1), :], ALU.add).then_inc(d_h2, 1)
                if have(1):
                    bo, ko = back(b, k, 1)
                    xk = xbuf[:, ko % XBUFS:ko % XBUFS + 1, :]
                    pool.wait_ge(d_xhat, t)
                    pool.sem_inc(pool_past, 1)
                    pool.tensor_tensor(xk, xk, c0_bc[:, bass.ds(bo, 1), :], ALU.add).then_inc(d_xc, 1)
                if have(3):
                    bo, _ = back(b, k, 3)
                    hk = h2[:, o:o + 1, :]
                    pool.wait_ge(d_xn, t - 2)
                    pool.sem_inc(pool_past, 1)
                    pool.tensor_tensor(hk, hk, cb_bc[:, bass.ds(bo, 1), :], ALU.mult).then_inc(d_h2m, 1)

            token_steps(pool, second_pass, 4)

            for i in range(2):
                pool.wait_ge(x2_out[i], 16 * (TILES // 2))
                pool.wait_ge(h2_out[i], 16 * (TILES // 2))
            pool.wait_ge(d_sum, TILES)
            pool.wait_ge(d_wlo, TILES)
            pool.memset(upper[:], 1.0).then_inc(route_pool, 1)
            pool.memset(ones_m[:], 1.0).then_inc(route_pool, 1)
            pool.iota(iota_row[:], pattern=[[1, P]], base=0, channel_multiplier=0, allow_small_or_imprecise_dtypes=True)\
                .then_inc(route_pool, 1)
            pool.wait_ge(route_pool, 3)
            pool.affine_select(out=upper[:], in_=upper[:], compare_op=ALU.is_gt, fill=0.0, base=0,
                               pattern=[[1, P]], channel_multiplier=-1).then_inc(route_pool, 1)
            for c in range(TOPK):
                pool.iota(value[:, c * TILES:(c + 1) * TILES].rearrange("p (b k) -> p b k", b=BATCH),
                          pattern=[[SEQ, BATCH], [1, TB]], base=1 + c * TOKENS, channel_multiplier=TB,
                          allow_small_or_imprecise_dtypes=True).then_inc(route_pool, 1)
            pool.iota(value[:, VALUE_PAD:VALUE_PAD + 1], pattern=[[0, 1]], base=TOPK * TOKENS + 1, channel_multiplier=1,
                      allow_small_or_imprecise_dtypes=True).then_inc(route_pool, 1)

            pool.wait_ge(route_done, 1)

            def expert_step(s, par, have, uses):
                if have(0):
                    if have(2):
                        pool.wait_ge(e_th, s - 1)
                    pool.tensor_copy(tok_ix[:, par:par + 1], token[:, bass.ds(s, 1)]).then_inc(e_tix, 1)
                    pool.wait_ge(e_tix, s + 1)
                    pool.sem_inc(pool_past, 1)
                    pool.indirect_dma_start(rows[:, par, :], None, h2_dram,
                                            bass.IndirectOffsetOnAxis(ap=tok_ix[:, par:par + 1], axis=0))\
                        .then_inc(e_rows[par], 16)
                if have(4):
                    pool.wait_ge(e_ys, s - 3)
                    if have(5):
                        pool.wait_ge(e_out[1 - par], 16 * (uses(5) + 1))
                    pool.tensor_copy(dst_ix[:, par:par + 1], dest[:, bass.ds(s - 4, 1)]).then_inc(e_dix, 1)
                    pool.wait_ge(e_dix, s - 3)
                    pool.sem_inc(pool_past, 1)
                    pool.indirect_dma_start(y_dram, bass.IndirectOffsetOnAxis(ap=dst_ix[:, par:par + 1], axis=0),
                                            y[:, par, :], None).then_inc(e_out[par], 16)

            expert_steps(pool, expert_step, E_LAG + 1)

            pool.wait_ge(gb_in, 16)

            def last_pass(b, h):
                q = 2 * b + h
                pool.wait_ge(f_v, q + 1)
                pool.sem_inc(pool_past, 1)
                pool.tensor_tensor(fin_u[:, h, :, :], fin_v[:, h, :, :],
                                   gb_bc[:, bass.ds(b, 1), :].to_broadcast([P, QUAD, D]), ALU.mult).then_inc(f_w, 1)

            with pool.Fori(0, BATCH) as b:
                for h in range(2):
                    last_pass(b, h)


def kernel(**inputs):
    import numpy as np
    import concourse.bacc as bacc
    from concourse.bass_utils import run_bass_kernel_spmd

    a = {n.removeprefix("L0_"): np.asarray(v) for n, v in inputs.items()}

    def halves(m):
        return np.ascontiguousarray(m.reshape(-1, P, m.shape[-1]).transpose(1, 0, 2))

    w_a = halves(a["ffn_W_A"].reshape(EXPERTS * RANK, D).T).reshape(P, -1)
    w_b = a["ffn_W_B"].transpose(2, 0, 1).reshape(RANK, -1)
    w_up = a["ffn_W_up"].transpose(2, 0, 1).reshape(HC, P, EXPERTS, FF).transpose(1, 2, 0, 3).reshape(P, -1)
    w_down = a["ffn_W_down"].transpose(2, 0, 1).reshape(FC, P, EXPERTS, D).transpose(1, 2, 0, 3).reshape(P, -1)
    arrays = {
        "x": a["attn_x"],
        "c_t": halves(a["c"].T),
        "wmod": halves(a["wmod"]),
        "wqkv_t": halves(a["attn_Wqkv_w"].T),
        "wq": halves(a["attn_Wqkv_w"][0:D]),
        "bq_cols": a["attn_Wqkv_b"][0:D].reshape(HC, P).T,
        "bkv_row": a["attn_Wqkv_b"][D:].reshape(1, 2 * D),
        "gn_cols": np.stack([a["attn_gn_w"].reshape(HC, P).T, a["attn_gn_b"].reshape(HC, P).T], axis=1),
        "wo_t": halves(a["attn_out_w"].T),
        "out_b": a["attn_out_b"],
        "wg": np.concatenate([w_a, np.concatenate([w_b, w_b], axis=0), w_up], axis=1),
        "wd": w_down,
    }
    nc = bacc.Bacc("TRN2", target_bir_lowering=False, num_devices=1)
    args = {}
    for name, v in arrays.items():
        arrays[name] = v = np.ascontiguousarray(v)
        args[name] = nc.dram_tensor(f"in_{name}", v.shape, mybir.dt.from_np(v.dtype), kind="ExternalInput").ap()
    args["out"] = nc.dram_tensor("out_0", (BATCH, SEQ, D), F32, kind="ExternalOutput").ap()
    build(nc, **args)
    r = run_bass_kernel_spmd(nc, [{f"in_{n}": v for n, v in arrays.items()}], core_ids=[0])
    return r.results[0]["out_0"]
```

```python
from contextlib import ExitStack

import concourse.bass as bass
from concourse import mybir


P = 128
ALU = mybir.AluOpType
ACT = mybir.ActivationFunctionType
F32 = mybir.dt.float32
F32R = mybir.dt.float32r
I32 = mybir.dt.int32
U32 = mybir.dt.uint32
AX_X = mybir.AxisListType.X

BATCH, SEQ, D = 4, 1024, 256
HEADS = 32
HEAD = D // HEADS
EXPERTS, TOPK, RANK, FF = 8, 2, 64, 512
EPS = 1e-5
GATE_MIN = 0.25

HC = D // P
FC = FF // P
TB = SEQ // P
TILES = BATCH * TB
TOKENS = BATCH * SEQ
ETILES = (TOPK * TOKENS + EXPERTS * (P - 1)) // P
XBUFS = 4
X1BUFS = 8

HALF = (FF + RANK) // 2
UA_W = EXPERTS * HC * 2 * HALF
B_W = EXPERTS * FF
G_W = UA_W + B_W
D_W = EXPERTS * FC * D
G_CHUNKS = TILES
G_CHUNK = G_W // G_CHUNKS
G_EVERY = 2
G_FIRST = TILES // G_EVERY
G_LATER = (G_CHUNKS - G_FIRST) // (2 * BATCH)
D_CHUNK = D_W // TILES
GBUFS = 4
MVBUFS = 4
E_LAG = 3
LOG_P = P.bit_length() - 1
OUT_LAG = E_LAG + 2
EARLY = TILES - TB
GROUP = 4
GROUPS = TOPK * TILES // GROUP
TABLE_BUFS = 4
ROWBUFS = 4

POOL_CONSTS = 8
ZEROS_SET = 4
STAT_MU, STAT_SQ, STAT_SCALE, STAT_SHIFT = 2, 8, 10, 12
ROUTE_CONSTS = 6


class Region:

    def __init__(self, nc, base, end):
        self.nc, self.at, self.end = nc, base, end

    def take(self, name, shape, dt=F32):
        size = 4
        for n in shape[1:]:
            size *= n
        t = self.nc.alloc_sbuf_tensor_at(name, shape, dt, offset=self.at)
        self.at += -(-size // 64) * 64
        assert self.at <= self.end, (name, self.at, self.end)
        return t

    def rewind(self, at):
        self.at = at


def build(nc, x, c_t, wmod, wqkv_t, wq, bq_cols, bkv_row, gn_cols, wo_t, out_b, wg, wd, out):
    h2_dram = nc.dram_tensor("h2_rows", [TOKENS, 2 * D], F32).ap()
    bv_dram = nc.dram_tensor("bias_v_rows", [BATCH, D], F32).ap()
    mod_dram = nc.dram_tensor("mod_rows", [BATCH, 4, D], F32).ap()

    x_v = x.rearrange("b (p k) d -> p b k d", p=P)
    x2_v = out[0:TOKENS, :].rearrange("(b p k) d -> p b k d", b=BATCH, p=P)
    h2_v = h2_dram[:, 0:D].rearrange("(b p k) d -> p b k d", b=BATCH, p=P)

    with ExitStack() as ctx:
        def sem(name):
            return ctx.enter_context(nc.semaphore(name))

        ps = ctx.enter_context(nc.psum_tensor("ps", [P, 8, 512], F32))
        bank = [ps[:, i, :] for i in range(8)]

        base = -(-nc.sbuf_base // 64) * 64
        end = nc.sbuf_usable_end // 64 * 64
        r1 = Region(nc, base, base + 2 * 4 * D_W)
        gram = r1.take("gram", [P, BATCH, HC, D + 1])
        p1 = r1.take("p1", [P, BATCH, HC, D])
        kv = r1.take("kv", [P, BATCH, HC, P])
        a_start = r1.at
        mod_sign = r1.take("mod_sign", [BATCH, 2, D])
        mod_abs = r1.take("mod_abs", [BATCH, 2, D])
        brow = r1.take("brow", [BATCH, 2 * D])
        bkv_rows = r1.take("bkv_rows", [BATCH, 2 * D])
        mod_sb = r1.take("mod_sb", [BATCH, 4 * D])
        bv_bc = r1.take("bv_bc", [P, BATCH, D])
        r1.rewind(a_start)
        a_cn = r1.take("a_cn", [P, BATCH, HC, D])
        a_nc = r1.take("a_nc", [P, BATCH, HC, D])
        bkv = r1.take("bkv", [1, BATCH, 2 * D])
        wqkv_sb = r1.take("wqkv_sb", [P, HC, 3 * D])
        wq_sb = r1.take("wq_sb", [P, HC, D])
        wo_sb = r1.take("wo_sb", [P, HC, D])
        ga_bc = r1.take("ga_bc", [P, BATCH, D])
        c_sb = r1.take("c_sb", [P, HC, BATCH])
        cs_sb = r1.take("cs_sb", [P, HC, BATCH])
        x1_more = r1.take("x1_more", [P, X1BUFS - XBUFS, D])
        r1.rewind(base)
        wd_hi = r1.take("wd_hi", [P, D_W], F32R)
        wd_lo = r1.take("wd_lo", [P, D_W], F32R)

        r2 = Region(nc, base + 2 * 4 * D_W, end)
        wg_hi = r2.take("wg_hi", [P, G_W], F32R)
        wg_lo = r2.take("wg_lo", [P, G_W], F32R)
        ident = r2.take("ident", [P, P])
        ones_col = r2.take("ones_col", [P, 1])
        eps_col = r2.take("eps_col", [P, 1])
        weight = r2.take("weight", [P, TOPK, TILES])
        ssum = r2.take("ssum", [P, TILES, EXPERTS])
        regional = r2.at

        wmod_sb = r2.take("wmod_sb", [P, HC, 6 * D])
        r2.rewind(regional)
        c_mat = r2.take("c_mat", [P, BATCH, HC, D])
        c0_bc = r2.take("c0_bc", [P, BATCH, D])
        rstd1 = r2.take("rstd1", [P, TILES])
        nmr1 = r2.take("nmr1", [P, TILES])
        bn = r2.take("bn", [P, 2, 6])
        mv = r2.take("mv", [P, MVBUFS, 2])
        std = r2.take("std", [P, 2])
        xbuf = r2.take("xbuf", [P, XBUFS, D])
        xhat = r2.take("xhat", [P, 2, D + 1])
        x1_bufs = [xbuf[:, i:i + 1, :] for i in range(XBUFS)] + [x1_more[:, i:i + 1, :] for i in range(X1BUFS - XBUFS)]
        per_pass = r2.at
        stage_g = r2.take("stage_g", [P, GBUFS, G_CHUNK])
        headmask = r2.take("headmask", [P, P])
        headavg = r2.take("headavg", [P, P])
        sc_cols = r2.take("sc_cols", [P, 2 * HC, BATCH])
        bq_c = r2.take("bq_c", [P, HC])
        bq_all = r2.take("bq_all", [P, HC, BATCH])
        gn_c = r2.take("gn_c", [P, 2, HC])
        outb_bc = r2.take("outb_bc", [P, D])
        xs_raw = r2.take("xs_raw", [P, BATCH, HC])
        g12 = r2.take("g12", [P, BATCH, P])
        cols = r2.take("cols", [P, BATCH, 6])
        stat = r2.take("stat", [P, 8, BATCH, HC])
        rv_row = r2.take("rv_row", [1, BATCH, D])
        r2.rewind(per_pass)
        stage_d = r2.take("stage_d", [P, 2, D_CHUNK])
        sb_bc = r2.take("sb_bc", [P, BATCH, D])
        cb_bc = r2.take("cb_bc", [P, BATCH, D])
        xt = r2.take("xt", [P, HC, P])
        x2buf = r2.take("x2buf", [P, 2, D])
        h2 = r2.take("h2", [P, 2, D])
        hd_hi = r2.take("hd_hi", [P, 2, HC, P], F32R)
        hd_lo = r2.take("hd_lo", [P, 2, HC, P], F32R)
        bn2 = r2.take("bn2", [P, 2, 6])
        mv2 = r2.take("mv2", [P, 2, 2])
        std2 = r2.take("std2", [P, 2])
        rstd2 = r2.take("rstd2", [P, 2])
        r2.rewind(regional)
        top = r2.take("top", [P, TILES, 8])
        topi = r2.take("topi", [P, TILES, 8], U32)
        topf = r2.take("topf", [P, TOPK, TILES])
        dest = r2.take("dest", [P, ETILES], I32)
        token = r2.take("token", [P, ETILES], I32)
        slot_w = r2.take("slot_w", [P, ETILES])
        tile_expert = r2.take("tile_expert", [1, ETILES + 2 * E_LAG], I32)
        experts_start = r2.at
        pick = r2.take("pick", [P, TOPK, TILES, EXPERTS])
        both = r2.take("both", [P, TILES, EXPERTS])
        total = r2.take("total", [P, EXPERTS, TILES])
        cum = r2.take("cum", [P, EXPERTS, TILES])
        zeros = r2.take("zeros", [P, EXPERTS * TILES])
        slot_m = r2.take("slot_m", [P, TILES, EXPERTS])
        slot_k = r2.take("slot_k", [P, TOPK, TILES, EXPERTS])
        slot = r2.take("slot", [P, TOPK * TILES])
        slot_i = r2.take("slot_i", [P, 3, TOPK * TILES], I32)
        slot_f = r2.take("slot_f", [P, 2, TOPK * TILES])
        small = r2.take("small", [P, 8, EXPERTS])
        small_i = r2.take("small_i", [P, 2, EXPERTS], I32)
        upper = r2.take("upper", [P, P])
        iota_row = r2.take("iota_row", [P, P])
        ones_m = r2.take("ones_m", [P, P])
        value = r2.take("value", [P, TILES + 1])
        values = r2.take("values", [P, TOPK * TILES])
        in_row = r2.take("in_row", [P, TABLE_BUFS, GROUP, P])
        in_col = r2.take("in_col", [P, TABLE_BUFS, GROUP, ETILES])
        col_values = r2.take("col_values", [P, TABLE_BUFS, GROUP, 2, ETILES])
        pad = top[:].rearrange("p t e -> p (t e)")[:, 0:ETILES]
        expert_f = total[:].rearrange("p e t -> p (e t)")[:, 0:ETILES]
        r2.rewind(experts_start)
        tok_ix = r2.take("tok_ix", [P, ROWBUFS], I32)
        dst_ix = r2.take("dst_ix", [P, 2], I32)
        rows = r2.take("rows", [P, ROWBUFS, 2 * D])
        gate = r2.take("gate", [P, 2, D])
        h_hi = r2.take("h_hi", [P, 2, HC, P], F32R)
        h_lo = r2.take("h_lo", [P, 2, HC, P], F32R)
        gh = r2.take("gh", [P, 2, 2, RANK])
        gt = r2.take("gt", [P, 2, P], F32R)
        silu = r2.take("silu", [P, FF])
        hidden = r2.take("hidden", [P, 2, FF])
        act_hi = r2.take("act_hi", [P, FC, P], F32R)
        act_lo = r2.take("act_lo", [P, FC, P], F32R)
        y = r2.take("y", [P, 2, D])

        pool_past = sem("pool_past")
        const_set = sem("const_set")
        zero_set = sem("zero_set")
        c_in = sem("c_in")
        wmod_in = sem("wmod_in")
        qkv_in = sem("qkv_in")
        attw_in = sem("attw_in")
        cond_act = sem("cond_act")
        mod_prod = sem("mod_prod")
        mod_cols = sem("mod_cols")
        mod_rows = sem("mod_rows")
        mod_step = sem("mod_step")
        mod_out = sem("mod_out")
        ga_in = sem("ga_in")
        bias_prod = sem("bias_prod")
        bias_set = sem("bias_set")
        bkv_in = sem("bkv_in")
        bv_out = sem("bv_out")
        bv_in = sem("bv_in")
        p1_bias = sem("p1_bias")
        x1_in = [sem(f"x1_in{i}") for i in range(X1BUFS)]
        wg_in = [sem(f"wg_in{i}") for i in range(GBUFS)]
        bn_done = sem("bn_done")
        mv_done = sem("mv_done")
        std_done = sem("std_done")
        rstd_done = sem("rstd_done")
        nmr_done = sem("nmr_done")
        xhat_done = sem("xhat_done")
        wghi_done = sem("wghi_done")
        wglo_done = sem("wglo_done")
        gram_done = sem("gram_done")
        gb_out = sem("gb_out")
        pad_out = sem("pad_out")
        att_pe = {n: sem(f"pe_{n}") for n in ("g21", "p1", "rv", "kv", "acn", "anc", "prod", "cols", "c", "c0")}
        att_ev = {n: sem(f"ev_{n}") for n in ("gram_a", "gram_v", "g21", "p1", "rv", "kv", "acn", "anc", "prod",
                                              "cols", "scaled", "ones", "c", "c0a", "c0")}
        prod_sum = sem("prod_sum")
        stat_step = sem("stat_step")
        stat_pe = sem("stat_pe")
        stat_std = sem("stat_std")
        x2_in = [sem(f"x2_in{i}") for i in range(XBUFS)]
        wd_in = [sem(f"wd_in{i}") for i in range(2)]
        sb_in = sem("sb_in")
        cb_in = sem("cb_in")
        x2_out = [sem(f"x2_out{i}") for i in range(2)]
        h2_out = [sem(f"h2_out{i}") for i in range(2)]
        d_xhat = sem("d_xhat")
        d_xc = sem("d_xc")
        d_tx = sem("d_tx")
        d_xt = sem("d_xt")
        d_c = sem("d_c")
        d_x2 = sem("d_x2")
        d_bn = sem("d_bn")
        d_mv = sem("d_mv")
        d_std = sem("d_std")
        d_rstd = sem("d_rstd")
        d_xn = sem("d_xn")
        d_h2m = sem("d_h2m")
        d_h2 = sem("d_h2")
        d_th = sem("d_th")
        d_hi = sem("d_hi")
        d_lo = sem("d_lo")
        d_gate = sem("d_gate")
        d_sq = sem("d_sq")
        d_sum = sem("d_sum")
        d_whi = sem("d_whi")
        d_wlo = sem("d_wlo")
        scores_done = sem("scores_done")
        top_done = sem("top_done")
        route_pool = sem("route_pool")
        route_step = sem("route_step")
        pick_done = sem("pick_done")
        diff_done = sem("diff_done")
        exp_done = sem("exp_done")
        count_pe = sem("count_pe")
        rows_done = sem("rows_done")
        cols_done = sem("cols_done")
        col_value_done = sem("col_value_done")
        col_weight_done = sem("col_weight_done")
        table_pe = sem("table_pe")
        route_done = sem("route_done")
        e_tix = sem("e_tix")
        e_dix = sem("e_dix")
        e_rows = [sem(f"e_rows{i}") for i in range(ROWBUFS)]
        e_gate = sem("e_gate")
        e_out = [sem(f"e_out{i}") for i in range(2)]
        e_th = sem("e_th")
        e_hi = sem("e_hi")
        e_lo = sem("e_lo")
        e_up = sem("e_up")
        e_ghs = sem("e_ghs")
        e_tg = sem("e_tg")
        e_gthi = sem("e_gthi")
        e_gtlo = sem("e_gtlo")
        e_g = sem("e_g")
        e_silu = sem("e_silu")
        e_act = sem("e_act")
        e_ta = sem("e_ta")
        e_ahi = sem("e_ahi")
        e_alo = sem("e_alo")
        e_y = sem("e_y")
        e_ys = sem("e_ys")

        def gram_copies(b):
            g = ps[:, 2 * b:2 * b + 2, :]
            return ((g12[:, b, :], g[:, 0, P:D]), (xs_raw[:, b, 0:1], g[:, 0, D:D + 1]),
                    (xs_raw[:, b, 1:2], g[:, 1, P:P + 1]))

        def gram_scalings(b):
            g = ps[:, 2 * b:2 * b + 2, :]
            return ((gram[:, b, 0, :], g[:, 0, 0:D + 1], sc_cols[:, HC, b:b + 1]),
                    (gram[:, b, 1, P:D + 1], g[:, 1, 0:P + 1], sc_cols[:, HC + 1, b:b + 1]))

        def token_steps(eng, step, lag, alone=1, between={}):
            for t in range(alone * TB):
                step(t // TB, t % TB, lambda n, t=t: t >= n)
                if t in between:
                    between[t]()
            with eng.Fori(alone, BATCH) as b:
                for k in range(TB):
                    step(b, k, lambda n: True)
            for k in range(lag):
                step(BATCH, k, lambda n, k=k: n > k)
                if TILES + k in between:
                    between[TILES + k]()

        def chunk_of(b, k):
            return b * (TB // G_EVERY) + k // G_EVERY, k // G_EVERY % GBUFS

        def up_banks(par):
            return ps[:, 5 * par:5 * par + 2, :]

        def back(b, k, n):
            return (b, k - n) if k >= n else (b - 1, k - n + TB)

        def table_steps(eng, step):
            for g in range(TABLE_BUFS):
                step(g, g, True, False)
            with eng.Fori(1, GROUPS // TABLE_BUFS - 1) as m:
                for g in range(TABLE_BUFS):
                    step(m * TABLE_BUFS + g, g, False, False)
            for g in range(TABLE_BUFS):
                step(GROUPS - TABLE_BUFS + g, g, False, g == TABLE_BUFS - 1)

        UNROLL = 2 * ROWBUFS
        PEEL = ETILES % UNROLL
        assert PEEL > OUT_LAG

        def expert_steps(eng, step, lag, enter=lambda s, n: None):
            enter(0, PEEL)
            for s in range(PEEL):
                step(s, s % ROWBUFS, lambda n, s=s: s >= n, lambda n, bufs, s=s: (s - n) // bufs)
            with eng.Fori(0, (ETILES - PEEL) // UNROLL) as m:
                enter(m * UNROLL + PEEL, UNROLL)
                for j in range(UNROLL):
                    step(m * UNROLL + (PEEL + j), (PEEL + j) % ROWBUFS, lambda n: True,
                         lambda n, bufs, j=j: m * (UNROLL // bufs) + (PEEL + j - n) // bufs)
            enter(ETILES, lag)
            for s in range(ETILES, ETILES + lag):
                step(s, s % ROWBUFS, lambda n, s=s: s - n < ETILES, lambda n, bufs, s=s: (s - n) // bufs)

        block = ctx.enter_context(nc.Block())

        @block.sync
        def _(sp):
            def first_pass(b, k, have):
                t = b * TB + k
                if have(X1BUFS):
                    sp.wait_ge(xhat_done, t - X1BUFS + 1)
                sp.dma_start(x1_bufs[k % X1BUFS], x_v[:, bass.ds(b, 1), k, :]).then_inc(x1_in[k % X1BUFS], 16)
                if k % G_EVERY == 0:
                    n, buf = chunk_of(b, k)
                    if have(GBUFS * G_EVERY):
                        sp.wait_ge(wglo_done, n - GBUFS + 1)
                    sp.dma_start(stage_g[:, buf, :], wg[:, bass.ds(n * G_CHUNK, G_CHUNK)]).then_inc(wg_in[buf], 16)

            def modulation_weights(part):
                w = slice(0, 2 * D) if part == 0 else slice(2 * D, 6 * D)
                sp.dma_start(wmod_sb[:, :, w], wmod[:, :, w]).then_inc(wmod_in, 16)

            def load(dst, src, done):
                return lambda: sp.dma_start(dst[:], src).then_inc(done, 16)

            token_steps(sp, first_pass, 0, 2, {
                3: lambda: modulation_weights(0), 5: load(wqkv_sb, wqkv_t, qkv_in),
                6: load(brow, bkv_row.partition_broadcast(BATCH), qkv_in), 7: load(bq_c, bq_cols, qkv_in),
                8: load(gn_c, gn_cols, attw_in), 9: load(wq_sb, wq, attw_in), 10: load(wo_sb, wo_t, attw_in),
                11: load(outb_bc, out_b.partition_broadcast(P), attw_in), 13: lambda: modulation_weights(1)})

            for n in range(G_FIRST, G_CHUNKS):
                sp.wait_ge(wglo_done, n - GBUFS + 1)
                sp.dma_start(stage_g[:, n % GBUFS, :], wg[:, n * G_CHUNK:(n + 1) * G_CHUNK])\
                  .then_inc(wg_in[n % GBUFS], 16)

            sp.wait_ge(mod_out, 16)
            for b in range(BATCH):
                sp.dma_start(h2_dram[b * SEQ:(b + 1) * SEQ, D:2 * D], mod_dram[b, 3:4, :].to_broadcast([SEQ, D]))\
                  .then_inc(gb_out, 16)
            sp.dma_start(out[TOKENS:TOKENS + P, :], x[0, 0:P, :]).then_inc(pad_out, 16)

            sp.wait_ge(xhat_done, TILES)
            sp.wait_ge(wglo_done, G_CHUNKS)
            sp.dma_start(sb_bc[:], mod_dram[:, 1, :].partition_broadcast(P)).then_inc(sb_in, 16)

            def second_pass(b, k, have):
                t = b * TB + k
                if have(6):
                    bo, ko = back(b, k, 6)
                    sp.wait_ge(d_h2, t - 5)
                    sp.dma_start(h2_v[:, bass.ds(bo, 1), ko, :], h2[:, k % 2:k % 2 + 1, :]).then_inc(h2_out[k % 2], 16)
                if have(4):
                    bo, ko = back(b, k, 4)
                    sp.wait_ge(d_x2, t - 3)
                    sp.dma_start(x2_v[:, bass.ds(bo, 1), ko, :], x2buf[:, k % 2:k % 2 + 1, :]).then_inc(x2_out[k % 2], 16)
                if have(0):
                    sp.dma_start(xbuf[:, k % XBUFS:k % XBUFS + 1, :], x_v[:, bass.ds(b, 1), k, :])\
                      .then_inc(x2_in[k % XBUFS], 16)
                if have(0):
                    if have(2):
                        sp.wait_ge(d_wlo, t - 1)
                    sp.dma_start(stage_d[:, k % 2, :], wd[:, bass.ds(t * D_CHUNK, D_CHUNK)])\
                      .then_inc(wd_in[k % 2], 16)

            token_steps(sp, second_pass, 6)

            for i in range(2):
                sp.wait_ge(e_out[i], 16 * ((ETILES - i + 1) // 2))
                sp.wait_ge(h2_out[i], 16 * (TILES // 2))
            for i in range(2):
                sp.wait_ge(x2_out[i], 16 * (TILES // 2))
            sp.wait_ge(gb_out, 16 * BATCH)
            sp.wait_ge(pad_out, 16)

        @block.scalar
        def _(act):
            act.dma_start(c_sb[:], c_t).then_inc(c_in, 16)
            act.wait_ge(c_in, 16)
            act.activation(cs_sb[:], c_sb[:], ACT.Silu).then_inc(cond_act, 1)
            act.wait_ge(zero_set, ZEROS_SET)

            def split_high(n, buf, uses):
                act.wait_ge(wg_in[buf], 16 * uses)
                act.activation(wg_hi[:, bass.ds(n * G_CHUNK, G_CHUNK)], stage_g[:, buf, :], ACT.Copy)\
                   .then_inc(wghi_done, 1)

            def first_pass(b, k, have):
                t = b * TB + k
                i, o = k % 2, 1 - k % 2
                if have(1):
                    act.wait_ge(mv_done, t)
                    act.activation(std[:, o:o + 1], mv[:, (k - 1) % MVBUFS, 1:2], ACT.Sqrt, bias=eps_col[:, 0:1])\
                       .then_inc(std_done, 1)
                if have(3):
                    act.wait_ge(nmr_done, t - 2)
                    if have(5):
                        act.wait_ge(gram_done, t - 4)
                    act.activation(xhat[:, o, 0:D], x1_bufs[(k - 3) % X1BUFS][:, 0, :], ACT.Identity,
                                   scale=rstd1[:, bass.ds(t - 3, 1)], bias=nmr1[:, bass.ds(t - 3, 1)])\
                       .then_inc(xhat_done, 1)
                if have(0) and k % G_EVERY == 0:
                    n, buf = chunk_of(b, k)
                    split_high(n, buf, b * (TB // G_EVERY // GBUFS) + k // G_EVERY // GBUFS + 1)

            token_steps(act, first_pass, 3, 2)

            act.wait_ge(mod_cols, 2)
            for b in range(0, BATCH, 2):
                act.wait_ge(gram_done, TB * (b + 1))
                for out_, in_ in gram_copies(b):
                    act.activation(out_, in_, ACT.Copy)
                for i, (out_, in_, scale) in enumerate(gram_scalings(b)):
                    ins = act.activation(out_, in_, ACT.Copy, scale=scale)
                ins.then_inc(att_ev["gram_a"], 1)
            for b in range(BATCH):
                act.wait_ge(att_pe["g21"], b + 1)
                act.activation(gram[:, b, 1, 0:P], bank[4 + b][:, 0:P], ACT.Copy, scale=sc_cols[:, HC + 1, b:b + 1])\
                   .then_inc(att_ev["g21"], 1)
            for b in range(BATCH):
                for n in range(G_FIRST + G_LATER * b, G_FIRST + G_LATER * (b + 1)):
                    split_high(n, n % GBUFS, n // GBUFS + 1)
            act.wait_ge(mod_out, 16)
            act.wait_ge(bkv_in, 16 * BATCH)
            for b in range(BATCH):
                act.wait_ge(att_pe["acn"], b + 1)
                act.activation(a_cn[:, b, :, :], bank[b][:, :].rearrange("p (i d) -> p i d", i=HC), ACT.Copy)\
                   .then_inc(att_ev["acn"], 1)
            for n in range(G_FIRST + G_LATER * BATCH, G_CHUNKS):
                split_high(n, n % GBUFS, n // GBUFS + 1)
            for b in range(BATCH):
                act.wait_ge(att_pe["cols"], b + 1)
                act.activation(cols[:, b, :], bank[4 + b][:, 0:6], ACT.Copy).then_inc(att_ev["cols"], 1)
            act.wait_ge(stat_pe, 2)
            act.activation(stat[:, 5, :, :], bank[1][:, 0:BATCH * HC].rearrange("p (b j) -> p b j", b=BATCH),
                           ACT.Sqrt, bias=eps_col[:, 0:1]).then_inc(stat_std, 1)
            act.wait_ge(stat_step, STAT_SCALE)
            for b in range(BATCH):
                for j in range(HC):
                    ins = act.activation(a_cn[:, b, j, :], a_cn[:, b, j, :], ACT.Copy, scale=stat[:, 6, b, j:j + 1])
                ins.then_inc(att_ev["scaled"], 1)

            def second_pass(b, k, have):
                t = b * TB + k
                i, o = k % 2, 1 - k % 2
                if have(5):
                    act.wait_ge(d_th, t - 4)
                    if have(7):
                        act.wait_ge(d_gate, t - 6)
                    act.activation(hd_hi[:, o, :, :], bank[2][:, 0:D].rearrange("p (i q) -> p i q", i=HC), ACT.Copy)\
                       .then_inc(d_hi, 1)
                if have(6):
                    act.wait_ge(d_gate, t - 5)
                    act.activation(bank[3 + i][:, :], bank[3 + i][:, :], ACT.Square).then_inc(d_sq, 1)
                if have(3):
                    act.wait_ge(d_mv, t - 2)
                    act.activation(std2[:, o:o + 1], mv2[:, o, 1:2], ACT.Sqrt, bias=eps_col[:, 0:1]).then_inc(d_std, 1)
                if have(0):
                    act.wait_ge(x2_in[k % XBUFS], 16 * (TB // XBUFS * b + k // XBUFS + 1))
                    if have(2):
                        act.wait_ge(d_tx, t - 1)
                    act.activation(xhat[:, i, 0:D], xbuf[:, k % XBUFS, :], ACT.Identity, scale=rstd1[:, bass.ds(t, 1)],
                                   bias=nmr1[:, bass.ds(t, 1)]).then_inc(d_xhat, 1)
                if have(1):
                    act.wait_ge(d_tx, t)
                    if have(2):
                        act.wait_ge(d_c, t - 1)
                    act.activation(xt[:], bank[0][:, 0:D].rearrange("p (i q) -> p i q", i=HC), ACT.Copy)\
                       .then_inc(d_xt, 1)
                if have(0):
                    if not have(1):
                        act.wait_ge(att_ev["c0"], BATCH)
                        act.dma_start(cb_bc[:], mod_dram[:, 2, :].partition_broadcast(P)).then_inc(cb_in, 16)
                    act.wait_ge(wd_in[i], 16 * (TB // 2 * b + k // 2 + 1))
                    act.activation(wd_hi[:, bass.ds(t * D_CHUNK, D_CHUNK)], stage_d[:, i, :], ACT.Copy)\
                       .then_inc(d_whi, 1)

            def scores(first, last):
                act.wait_ge(d_sum, last)
                act.activation(ssum[:, first:last, :], ssum[:, first:last, :], ACT.Sqrt).then_inc(scores_done, 1)

            token_steps(act, second_pass, 6, 1, {TILES: lambda: scores(0, EARLY)})
            scores(EARLY, TILES)
            act.wait_ge(diff_done, 1)
            act.activation(weight[:, 1, :], weight[:, 0, :], ACT.Exp).then_inc(exp_done, 1)

            def table_values(g, buf, first, last):
                act.wait_ge(cols_done, g + 1)
                for j in range(GROUP):
                    ins = act.activation(col_values[:, buf, j, 0, :], in_col[:, buf, j, :], ACT.Copy,
                                         scale=values[:, bass.ds(g * GROUP + j, 1)])
                ins.then_inc(col_value_done, 1)

            table_steps(act, table_values)

            def expert_step(s, k, have, taken):
                par = k % 2
                o = 1 - par
                if have(2):
                    act.wait_ge(e_g, s - 1)
                    if have(3):
                        act.wait_ge(e_act, s - 2)
                    act.activation(silu[:], bank[2][:, :], ACT.Silu).then_inc(e_silu, 1)
                if have(0):
                    act.wait_ge(e_th, s + 1)
                    if have(2):
                        act.wait_ge(e_up, s - 1)
                    act.activation(h_hi[:, par, :, :], bank[4][:, 0:D].rearrange("p (i q) -> p i q", i=HC), ACT.Copy)\
                       .then_inc(e_hi, 1)
                if have(2):
                    if not have(3):
                        act.wait_ge(route_done, 3)
                    act.wait_ge(e_rows[(k - 2) % ROWBUFS], 16 * (taken(2, ROWBUFS) + 1))
                    if have(4):
                        act.wait_ge(e_ys, s - 3)
                    act.activation(gate[:, par, :], rows[:, (k - 2) % ROWBUFS, D:2 * D], ACT.Copy,
                                   scale=slot_w[:, bass.ds(s - 2, 1)]).then_inc(e_gate, 1)
                if have(1):
                    act.wait_ge(e_tg, s)
                    if have(3):
                        act.wait_ge(e_g, s - 2)
                    act.activation(gt[:, o, :], bank[4][:, D:D + P], ACT.Copy).then_inc(e_gthi, 1)
                if have(2):
                    act.wait_ge(e_ta, s - 1)
                    if have(3):
                        act.wait_ge(e_y, s - 2)
                    act.activation(act_hi[:], bank[3][:, :].rearrange("p (c q) -> p c q", c=FC), ACT.Copy)\
                       .then_inc(e_ahi, 1)

            expert_steps(act, expert_step, E_LAG)

        @block.tensor
        def _(pe):
            def transpose(out_, in_):
                return pe.transpose(out_, in_, ident[0:in_.shape[0], 0:in_.shape[0]])

            def modulation_columns():
                pe.wait_ge(cond_act, 1)
                pe.wait_ge(wmod_in, 16)
                for q in range(2 * HC):
                    for i in range(HC):
                        ins = pe.matmul(bank[6][:, q * BATCH:(q + 1) * BATCH], wmod_sb[:, i, q * P:(q + 1) * P],
                                        cs_sb[:, i, :], start=(i == 0), stop=(i == HC - 1))
                ins.then_inc(mod_prod, 1)

            def biases_q():
                pe.wait_ge(mod_cols, 1)
                pe.wait_ge(qkv_in, 3 * 16)
                for j in range(HC):
                    for i in range(HC):
                        ins = pe.matmul(bank[5][:, j * BATCH:(j + 1) * BATCH], wqkv_sb[:, i, j * P:(j + 1) * P],
                                        sc_cols[:, i, :], start=(i == 0), stop=(i == HC - 1))
                ins.then_inc(bias_prod, 1)

            def biases_kv(i):
                ins = pe.matmul(bank[7][0:BATCH, :], sc_cols[:, i, :], wqkv_sb[:, i, D:3 * D],
                                start=(i == 0), stop=(i == HC - 1))
                if i == HC - 1:
                    ins.then_inc(bias_prod, 1)

            def banks_free():
                pe.wait_ge(mod_cols, 2)
                pe.wait_ge(bias_set, 2)

            def first_pass(b, k, have):
                t = b * TB + k
                xb = xhat[:, k % 2, :]
                pe.wait_ge(xhat_done, t + 1)
                pe.matmul(ps[:, bass.ds(2 * b, 1), 0:D + 1], xb[:, 0:P], xb[:, 0:D + 1],
                          start=(k == 0), stop=(k == TB - 1))
                pe.matmul(ps[:, bass.ds(2 * b + 1, 1), 0:P + 1], xb[:, P:D], xb[:, P:D + 1],
                          start=(k == 0), stop=(k == TB - 1)).then_inc(gram_done, 1)

            token_steps(pe, first_pass, 0, 2, {4: modulation_columns, 8: biases_q, 9: lambda: biases_kv(0),
                                               11: lambda: biases_kv(1), 15: banks_free})
            pe.wait_ge(const_set, POOL_CONSTS)

            pe.wait_ge(att_ev["gram_a"], BATCH // 2)
            pe.wait_ge(att_ev["gram_v"], BATCH // 2)
            for b in range(BATCH):
                transpose(bank[4 + b][:, 0:P], g12[:, b, :]).then_inc(att_pe["g21"], 1)
            pe.wait_ge(wmod_in, 32)
            for n in range(4):
                for i in range(HC):
                    ins = pe.matmul(bank[n][0:BATCH, 0:D], cs_sb[:, i, :], wmod_sb[:, i, (n + 2) * D:(n + 3) * D],
                                    start=(i == 0), stop=(i == HC - 1))
                ins.then_inc(mod_prod, 1)
            for b in range(BATCH):
                pe.wait_ge(mod_rows, b + 1)
                pe.wait_ge(att_ev["g21"], b + 1)
                for i in range(HC):
                    for m in range(HC):
                        ins = pe.matmul(bank[b][:, i * D:(i + 1) * D], gram[:, b, m, i * P:(i + 1) * P],
                                        wqkv_sb[:, m, 2 * D:3 * D], start=(m == 0), stop=(m == HC - 1))
                ins.then_inc(att_pe["p1"], 1)
                for m in range(HC):
                    ins = pe.matmul(bank[4 + b][0:1, 0:D], gram[:, b, m, D:D + 1], wqkv_sb[:, m, 2 * D:3 * D],
                                    start=(m == 0), stop=(m == HC - 1))
                ins.then_inc(att_pe["rv"], 1)
            pe.wait_ge(bkv_in, 16 * BATCH)
            for b in range(BATCH):
                pe.wait_ge(att_ev["p1"], b + 1)
                pe.wait_ge(att_ev["rv"], b + 1)
                for j in range(HC):
                    o = bank[4 + b][:, j * P:(j + 1) * P]
                    for m in range(HC):
                        pe.matmul(o, wqkv_sb[:, m, D + j * P:D + (j + 1) * P], p1[:, b, m, j * P:(j + 1) * P],
                                  start=(m == 0), stop=False)
                    ins = pe.matmul(o, bkv[0:1, b, j * P:(j + 1) * P], rv_row[0:1, b, j * P:(j + 1) * P],
                                    start=False, stop=True)
                ins.then_inc(att_pe["kv"], 1)
            for b in range(BATCH):
                pe.wait_ge(attw_in, 4 * 16)
                pe.wait_ge(att_ev["kv"], b + 1)
                for j in range(HC):
                    ins = pe.matmul(bank[b][:, j * D:(j + 1) * D], kv[:, b, j, :], wq_sb[:, j, :], start=True, stop=True)
                ins.then_inc(att_pe["acn"], 1)
                for i in range(HC):
                    for j in range(HC):
                        ins = pe.matmul(bank[4 + b][:, i * D + j * P:i * D + (j + 1) * P], wq_sb[:, j, i * P:(i + 1) * P],
                                        kv[:, b, j, :], start=True, stop=True)
                ins.then_inc(att_pe["anc"], 1)
            for b in range(BATCH):
                pe.wait_ge(att_ev["acn"], b + 1)
                pe.wait_ge(att_ev["anc"], b + 1)
                for i in range(HC):
                    for m in range(HC):
                        ins = pe.matmul(bank[b][:, i * D:(i + 1) * D], gram[:, b, m, i * P:(i + 1) * P], a_nc[:, b, m, :],
                                        start=(m == 0), stop=(m == HC - 1))
                ins.then_inc(att_pe["prod"], 1)
                for j in range(HC):
                    pe.matmul(bank[4 + b][:, j:j + 1], kv[:, b, j, :], bq_all[:, j, b:b + 1], start=True, stop=True)
                for j in range(HC):
                    for m in range(HC):
                        pe.matmul(bank[4 + b][:, 2 + j:3 + j], a_nc[:, b, m, j * P:(j + 1) * P], gram[:, b, m, D:D + 1],
                                  start=(m == 0), stop=(m == HC - 1))
            for b in range(BATCH):
                pe.wait_ge(prod_sum, b + 1)
                for j in range(HC):
                    ins = pe.matmul(bank[4 + b][:, 4 + j:5 + j], p1[:, b, 0, j * P:(j + 1) * P], ones_col[:, 0:1],
                                    start=True, stop=True)
                ins.then_inc(att_pe["cols"], 1)
            for n, (row, step) in enumerate(((1, STAT_MU), (4, STAT_SQ))):
                pe.wait_ge(stat_step, step)
                pe.matmul(bank[n][:, 0:BATCH * HC], headavg[:], stat[:, row, :, :].rearrange("p b j -> p (b j)"),
                          start=True, stop=True).then_inc(stat_pe, 1)
            pe.wait_ge(stat_std, 1)
            pe.wait_ge(stat_step, STAT_SHIFT)
            for b in range(BATCH):
                pe.wait_ge(att_ev["scaled"], b + 1)
                for i in range(HC):
                    for j in range(HC):
                        ins = pe.matmul(bank[b][:, i * D:(i + 1) * D], a_cn[:, b, j, i * P:(i + 1) * P], wo_sb[:, j, :],
                                        start=(j == 0), stop=(j == HC - 1))
                ins.then_inc(att_pe["c"], 1)
                pe.wait_ge(att_ev["ones"], b + 1)
                for j in range(HC):
                    ins = pe.matmul(bank[4 + b][:, 0:D], p1[:, b, j, 0:P], wo_sb[:, j, :],
                                    start=(j == 0), stop=(j == HC - 1))
                ins.then_inc(att_pe["c0"], 1)

            pe.wait_ge(att_ev["c0"], BATCH)
            pe.wait_ge(att_ev["c"], BATCH)
            pe.wait_ge(wglo_done, G_CHUNKS)

            def three(out_, hi, lo, w_hi, w_lo, first, last):
                pe.matmul(out_, hi, w_hi, start=first, stop=False)
                pe.matmul(out_, hi, w_lo, start=False, stop=False)
                return pe.matmul(out_, lo, w_hi, start=False, stop=last)

            def second_pass(b, k, have):
                t = b * TB + k
                i, o = k % 2, 1 - k % 2
                if have(1):
                    pe.wait_ge(d_xhat, t)
                    if have(2):
                        pe.wait_ge(d_xt, t - 1)
                    transpose(bank[0][:, 0:P], xhat[:, o, 0:P])
                    transpose(bank[0][:, P:D], xhat[:, o, P:D]).then_inc(d_tx, 1)
                if have(2):
                    bo, _ = back(b, k, 2)
                    pe.wait_ge(d_xt, t - 1)
                    if have(3):
                        pe.wait_ge(d_x2, t - 2)
                    for m in range(HC):
                        ins = pe.matmul(bank[1][:, 0:D], xt[:, m, :], c_mat[:, bass.ds(bo, 1), m, :],
                                        start=(m == 0), stop=(m == HC - 1))
                    ins.then_inc(d_c, 1)

                def gates(m):
                    w_hi, w_lo = (w[:, 0:UA_W].rearrange("p (e m c k) -> p m e c k", e=EXPERTS, m=HC, c=2)
                                  [:, m, :, :, FF // 2:HALF] for w in (wg_hi, wg_lo))
                    return three(bank[3 + o][:, :].rearrange("p (e c r) -> p e c r", e=EXPERTS, c=2),
                                 hd_hi[:, o, m, :], hd_lo[:, o, m, :], w_hi, w_lo, m == 0, m == HC - 1)

                if have(5):
                    pe.wait_ge(d_lo, t - 4)
                    if have(7):
                        pe.wait_ge(d_sum, t - 6)
                    gates(0)
                if have(4):
                    pe.wait_ge(d_h2, t - 3)
                    if have(5):
                        pe.wait_ge(d_lo, t - 4)
                    transpose(bank[2][:, 0:P], h2[:, i, 0:P])
                    transpose(bank[2][:, P:D], h2[:, i, P:D]).then_inc(d_th, 1)
                if have(5):
                    gates(1).then_inc(d_gate, 1)

            token_steps(pe, second_pass, 5)

            pe.wait_ge(pick_done, 1)
            pe.wait_ge(route_pool, ROUTE_CONSTS)
            picked = both[:].rearrange("p t e -> p (t e)")
            pe.matmul(bank[5][:, 0:TILES * EXPERTS], upper[:], picked, start=True, stop=True)
            pe.matmul(bank[6][:, 0:TILES * EXPERTS], ones_m[:], picked, start=True, stop=True).then_inc(count_pe, 1)

            def table_products(g, buf, first, last):
                pe.wait_ge(rows_done, g + 1)
                pe.wait_ge(col_value_done, g + 1)
                pe.wait_ge(col_weight_done, g + 1)
                for j in range(GROUP):
                    ins = pe.matmul(bank[7][:, 0:2 * ETILES], in_row[:, buf, j, :],
                                    col_values[:, buf, j, :, :].rearrange("p v t -> p (v t)"),
                                    start=(first and buf == 0 and j == 0), stop=(last and j == GROUP - 1))
                ins.then_inc(table_pe, 1)

            table_steps(pe, table_products)

            pe.wait_ge(route_done, 1)
            pe.wait_ge(d_wlo, TILES)

            experts = []

            def load_experts(s, n):
                experts[:] = nc.values_load_multi_w_load_instructions(
                    tile_expert[0:1, bass.ds(s, E_LAG + n)], engines=[mybir.EngineType.PE], min_val=0,
                    max_val=EXPERTS - 1, skip_runtime_bounds_check_because="counts of thresholds among EXPERTS - 1")[1]

            def expert_step(s, k, have, taken):
                par = k % 2
                w_down, _, w_g, w_up = experts[0:E_LAG + 1]
                del experts[0]
                o = 1 - par

                def gate_product():
                    pe.wait_ge(e_gtlo, s)
                    w = bass.ds(w_g * FF + UA_W, FF)
                    pe.matmul(bank[2][:, :], gt[:, o, :], wg_hi[:, w], start=True, stop=False)
                    pe.matmul(bank[2][:, :], gt[:, o, :], wg_lo[:, w], start=False, stop=True).then_inc(e_g, 1)

                if have(0):
                    pe.wait_ge(e_rows[k], 16 * (taken(0, ROWBUFS) + 1))
                    transpose(bank[4][:, 0:P], rows[:, k, 0:P])
                    transpose(bank[4][:, P:D], rows[:, k, P:D]).then_inc(e_th, 1)
                if have(3):
                    pe.wait_ge(e_alo, s - 2)
                    if have(4):
                        pe.wait_ge(e_ys, s - 3)
                    for c in range(FC):
                        w = bass.ds(w_down * (FC * D) + c * D, D)
                        ins = three(bank[7][:, 0:D], act_hi[:, c, :], act_lo[:, c, :], wd_hi[:, w], wd_lo[:, w],
                                    c == 0, c == FC - 1)
                    ins.then_inc(e_y, 1)
                if have(2):
                    pe.wait_ge(e_act, s - 1)
                    for c in range(FC):
                        ins = transpose(bank[3][:, c * P:(c + 1) * P], hidden[:, par, c * P:(c + 1) * P])
                    ins.then_inc(e_ta, 1)
                if have(1):
                    pe.wait_ge(e_ghs, s)
                    if have(0):
                        pe.wait_ge(e_lo, s + 1)
                    transpose(bank[4][:, D:D + P], gh[:, o, :, :].rearrange("p a r -> p (a r)")).then_inc(e_tg, 1)
                if have(0):
                    if not have(1):
                        pe.wait_ge(e_lo, s + 1)
                    for c in range(2):
                        for m in range(HC):
                            if have(1) and c == 1 and m == HC - 1:
                                gate_product()
                            w = bass.ds(w_up * (HC * 2 * HALF) + (m * 2 + c) * HALF, HALF)
                            ins = three(up_banks(par)[:, c, 0:HALF], h_hi[:, par, m, :], h_lo[:, par, m, :],
                                        wg_hi[:, w], wg_lo[:, w], m == 0, m == HC - 1)
                    ins.then_inc(e_up, 1)
                elif have(1):
                    gate_product()

            expert_steps(pe, expert_step, E_LAG, load_experts)

        @block.vector
        def _(dve):
            for n, (t_, v) in enumerate(((eps_col, EPS), (ones_col, 1.0))):
                dve.memset(t_[:], v).then_inc(zero_set, 1)
            for i in range(2):
                dve.memset(xhat[:, i, D:D + 1], 1.0).then_inc(zero_set, 1)

            count = {}

            def then(ins, s):
                count[s.name] = count.get(s.name, 0) + 1
                ins.then_inc(s, 1)
                dve.wait_ge(s, count[s.name])

            def modulation_columns():
                dve.wait_ge(mod_prod, 1)
                v = bank[6][:, 0:2 * HC * BATCH].rearrange("p (q b) -> p q b", b=BATCH)
                dve.tensor_copy(sc_cols[:, 0:HC, :], v[:, 0:HC, :]).then_inc(mod_cols, 1)
                dve.tensor_scalar(sc_cols[:, HC:2 * HC, :], v[:, HC:2 * HC, :], 1.0, None, ALU.add).then_inc(mod_cols, 1)

            def biases():
                dve.wait_ge(qkv_in, 3 * 16)
                dve.wait_ge(bias_prod, 2)
                dve.tensor_tensor(bq_all[:], bank[5][:, 0:HC * BATCH].rearrange("p (j b) -> p j b", b=BATCH),
                                  bq_c[:].unsqueeze(2).to_broadcast([P, HC, BATCH]), ALU.add).then_inc(bias_set, 1)
                dve.tensor_tensor(bkv_rows[:], bank[7][0:BATCH, :], brow[:], ALU.add).then_inc(bias_set, 1)

            def split_low(n, buf):
                dve.wait_ge(wghi_done, n + 1)
                chunk = bass.ds(n * G_CHUNK, G_CHUNK)
                dve.tensor_tensor(wg_lo[:, chunk], stage_g[:, buf, :], wg_hi[:, chunk].bitcast(F32),
                                  ALU.subtract).then_inc(wglo_done, 1)

            def first_pass(b, k, have):
                t = b * TB + k
                i, o = k % 2, 1 - k % 2
                if have(0):
                    dve.wait_ge(x1_in[k % X1BUFS], 16 * (TB // X1BUFS * b + k // X1BUFS + 1))
                    dve.bn_stats(bn[:, i, :], x1_bufs[k % X1BUFS][:, 0, :]).then_inc(bn_done, 1)
                if have(1) and (k - 1) % G_EVERY == 0:
                    split_low(*chunk_of(b, k - 1))
                if have(0):
                    dve.wait_ge(bn_done, t + 1)
                if have(2):
                    dve.wait_ge(rstd_done, t - 1)
                    dve.scalar_tensor_tensor(out=nmr1[:, bass.ds(t - 2, 1)], in0=mv[:, (k - 2) % MVBUFS, 0:1], scalar=-1.0,
                                             in1=rstd1[:, bass.ds(t - 2, 1)], op0=ALU.mult, op1=ALU.mult)\
                       .then_inc(nmr_done, 1)
                if have(0):
                    dve.bn_aggr(mv[:, k % MVBUFS, :], bn[:, i, :]).then_inc(mv_done, 1)
                if have(1):
                    dve.wait_ge(std_done, t)
                    dve.reciprocal(rstd1[:, bass.ds(t - 1, 1)], std[:, o:o + 1]).then_inc(rstd_done, 1)

            token_steps(dve, first_pass, 2, 2, {9: modulation_columns, 15: biases})

            for b in range(1, BATCH, 2):
                dve.wait_ge(gram_done, TB * (b + 1))
                for out_, in_ in gram_copies(b):
                    dve.tensor_copy(out_, in_)
                for out_, in_, scale in gram_scalings(b):
                    ins = dve.tensor_scalar(out_, in_, scale, None, ALU.mult)
                ins.then_inc(att_ev["gram_v"], 1)
            for n in range(4):
                dve.wait_ge(mod_prod, n + 2)
                dve.tensor_copy(mod_sb[:, n * D:(n + 1) * D], bank[n][0:BATCH, 0:D]).then_inc(mod_rows, 1)
            dve.wait_ge(bkv_in, 16 * BATCH)
            for b in range(BATCH):
                dve.wait_ge(att_pe["p1"], b + 1)
                dve.wait_ge(p1_bias, b + 1)
                for i in range(HC):
                    ins = dve.scalar_tensor_tensor(out=p1[:, b, i, :], in0=bank[b][:, i * D:(i + 1) * D],
                                                   scalar=sc_cols[:, HC + i, b:b + 1], in1=p1[:, b, i, :],
                                                   op0=ALU.mult, op1=ALU.add)
                ins.then_inc(att_ev["p1"], 1)
                dve.wait_ge(att_pe["rv"], b + 1)
                dve.scalar_tensor_tensor(out=rv_row[0:1, b, :], in0=bkv[0:1, b, D:2 * D], scalar=float(SEQ),
                                         in1=bank[4 + b][0:1, 0:D], op0=ALU.mult, op1=ALU.add)\
                   .then_inc(att_ev["rv"], 1)
                for n in range(G_FIRST + G_LATER * b, G_FIRST + G_LATER * (b + 1)):
                    split_low(n, n % GBUFS)
            for b in range(BATCH):
                dve.wait_ge(att_pe["kv"], b + 1)
                dve.tensor_tensor(kv[:, b, :, :], bank[4 + b][:, 0:D].rearrange("p (j q) -> p j q", j=HC),
                                  headmask[:].unsqueeze(1).to_broadcast([P, HC, P]), ALU.mult)\
                   .then_inc(att_ev["kv"], 1)
            dve.wait_ge(mod_out, 16)
            for b in range(BATCH):
                dve.wait_ge(att_pe["anc"], b + 1)
                dve.tensor_copy(a_nc[:, b, :, :], bank[4 + b][:, :].rearrange("p (i d) -> p i d", i=HC))\
                   .then_inc(att_ev["anc"], 1)
            for b in range(BATCH):
                for n in range(G_FIRST + G_LATER * (BATCH + b), G_FIRST + G_LATER * (BATCH + b + 1)):
                    split_low(n, n % GBUFS)
                dve.wait_ge(att_pe["prod"], b + 1)
                for i in range(HC):
                    ins = dve.scalar_tensor_tensor(out=p1[:, b, i, :], in0=bank[b][:, i * D:(i + 1) * D],
                                                   scalar=sc_cols[:, HC + i, b:b + 1], in1=a_nc[:, b, i, :],
                                                   op0=ALU.mult, op1=ALU.mult)
                ins.then_inc(att_ev["prod"], 1)

            dve.wait_ge(att_ev["cols"], BATCH)
            a0, axs, sq = cols[:, :, 0:2], cols[:, :, 2:4], cols[:, :, 4:6]
            mean, mu, var, dev, dev2, std_, scale, shift = (stat[:, n, :, :] for n in range(8))

            def spread(col):
                return gn_c[:, col, :].unsqueeze(1).to_broadcast([P, BATCH, HC])

            def heads(n):
                return bank[n][:, 0:BATCH * HC].rearrange("p (b j) -> p b j", b=BATCH)

            dve.wait_ge(attw_in, 4 * 16)
            then(dve.tensor_scalar(mean, axs, 1.0 / SEQ, None, ALU.mult), stat_step)
            then(dve.scalar_tensor_tensor(out=mu, in0=axs, scalar=1.0 / SEQ, in1=a0, op0=ALU.mult, op1=ALU.add), stat_step)
            assert count[stat_step.name] == STAT_MU
            then(dve.tensor_tensor(dev, mean, mean, ALU.mult), stat_step)
            then(dve.scalar_tensor_tensor(out=var, in0=sq, scalar=1.0 / SEQ, in1=dev, op0=ALU.mult, op1=ALU.subtract),
                 stat_step)
            dve.wait_ge(stat_pe, 1)
            then(dve.tensor_tensor(dev, mu, heads(0), ALU.subtract), stat_step)
            then(dve.tensor_tensor(mean, a0, heads(0), ALU.subtract), stat_step)
            then(dve.tensor_tensor(dev, dev, dev, ALU.mult), stat_step)
            then(dve.scalar_tensor_tensor(out=dev2, in0=var, scalar=0.0, in1=dev, op0=ALU.max, op1=ALU.add), stat_step)
            assert count[stat_step.name] == STAT_SQ
            dve.wait_ge(stat_std, 1)
            then(dve.reciprocal(scale, std_), stat_step)
            then(dve.tensor_tensor(scale, scale, spread(0), ALU.mult), stat_step)
            assert count[stat_step.name] == STAT_SCALE
            then(dve.tensor_tensor(shift, mean, scale, ALU.mult), stat_step)
            then(dve.tensor_tensor(shift, shift, spread(1), ALU.add), stat_step)
            assert count[stat_step.name] == STAT_SHIFT
            dve.wait_ge(ga_in, 16)
            for b in range(BATCH):
                dve.wait_ge(att_pe["c"], b + 1)
                for i in range(HC):
                    ins = dve.scalar_tensor_tensor(out=c_mat[:, b, i, :], in0=bank[b][:, i * D:(i + 1) * D],
                                                   scalar=sc_cols[:, HC + i, b:b + 1], in1=ga_bc[:, b, :],
                                                   op0=ALU.mult, op1=ALU.mult)
                ins.then_inc(att_ev["c"], 1)
                dve.wait_ge(att_pe["c0"], b + 1)
                dve.tensor_tensor(c0_bc[:, b, :], bank[4 + b][:, 0:D], outb_bc[:], ALU.add).then_inc(att_ev["c0a"], 1)
                dve.wait_ge(att_ev["c0a"], b + 1)
                dve.tensor_tensor(c0_bc[:, b, :], c0_bc[:, b, :], ga_bc[:, b, :], ALU.mult).then_inc(att_ev["c0"], 1)

            def second_pass(b, k, have):
                t = b * TB + k
                i, o = k % 2, 1 - k % 2
                if have(3):
                    dve.wait_ge(d_bn, t - 2)
                if have(5):
                    dve.wait_ge(d_hi, t - 4)
                    dve.tensor_tensor(hd_lo[:, o, :, :], bank[2][:, 0:D].rearrange("p (i q) -> p i q", i=HC),
                                      hd_hi[:, o, :, :].bitcast(F32), ALU.subtract).then_inc(d_lo, 1)
                if have(3):
                    dve.bn_aggr(mv2[:, o, :], bn2[:, o, :]).then_inc(d_mv, 1)
                if have(6):
                    dve.wait_ge(d_sq, t - 5)
                    dve.tensor_reduce(ssum[:, bass.ds(t - 6, 1), :].rearrange("p t e -> p (t e)"),
                                      bank[3 + i][:, :].rearrange("p (e r) -> p e r", e=EXPERTS),
                                      AX_X, ALU.add).then_inc(d_sum, 1)
                if have(3):
                    dve.wait_ge(d_std, t - 2)
                    dve.reciprocal(rstd2[:, o:o + 1], std2[:, o:o + 1]).then_inc(d_rstd, 1)
                if have(2):
                    dve.wait_ge(d_c, t - 1)
                    dve.wait_ge(d_xc, t - 1)
                    if have(4):
                        dve.wait_ge(x2_out[i], 16 * (TB // 2 * b + (k - 2) // 2))
                    dve.tensor_tensor(x2buf[:, i, :], bank[1][:, 0:D], xbuf[:, (k - 2) % XBUFS, :], ALU.add)\
                       .then_inc(d_x2, 1)
                if have(3):
                    dve.wait_ge(d_rstd, t - 2)
                    if have(5):
                        dve.wait_ge(h2_out[o], 16 * (TB // 2 * b + (k - 3) // 2))
                        dve.wait_ge(d_th, t - 4)
                    dve.tensor_scalar(h2[:, o, :], x2buf[:, o, :], mv2[:, o, 0:1], rstd2[:, o:o + 1],
                                      ALU.subtract, ALU.mult).then_inc(d_xn, 1)
                if have(2):
                    dve.wait_ge(d_x2, t - 1)
                    dve.bn_stats(bn2[:, i, :], x2buf[:, i, :]).then_inc(d_bn, 1)
                if have(0):
                    dve.wait_ge(d_whi, t + 1)
                    chunk = bass.ds(t * D_CHUNK, D_CHUNK)
                    dve.tensor_tensor(wd_lo[:, chunk], stage_d[:, i, :], wd_hi[:, chunk].bitcast(F32), ALU.subtract)\
                       .then_inc(d_wlo, 1)

            def best(first, last):
                for t in range(first, last):
                    ins = dve.max(top[:, t, :], ssum[:, t, :])
                ins.then_inc(top_done, 1)

            def best_index(first, last):
                for t in range(first, last):
                    ins = dve.max_index(topi[:, t, :], top[:, t, :], ssum[:, t, :])
                ins.then_inc(top_done, 1)

            def best_early():
                dve.wait_ge(scores_done, 1)
                best(0, EARLY // 2)

            def best_early_index():
                dve.wait_ge(top_done, 1)
                best_index(0, EARLY // 2)

            def best_middle():
                best(EARLY // 2, EARLY)

            def best_middle_index():
                dve.wait_ge(top_done, 3)
                best_index(EARLY // 2, EARLY)

            token_steps(dve, second_pass, 6, 1, {TILES + 1: best_early, TILES + 2: best_early_index,
                                                 TILES + 3: best_middle, TILES + 4: best_middle_index})

            dve.wait_ge(scores_done, 2)
            best(EARLY, TILES)
            dve.wait_ge(top_done, 5)
            best_index(EARLY, TILES)
            dve.wait_ge(top_done, 6)
            for i in range(2):
                dve.wait_ge(x2_out[i], 16 * (TILES // 2))
                dve.wait_ge(h2_out[i], 16 * (TILES // 2))
            dve.wait_ge(d_h2, TILES)
            dve.tensor_tensor(weight[:, 0, :], top[:, :, 1], top[:, :, 0], ALU.subtract).then_inc(diff_done, 1)
            dve.memset(zeros[:], 0.0)
            then(dve.tensor_copy(topf[:], topi[:, :, 0:TOPK].rearrange("p t c -> p c t")), route_step)
            dve.wait_ge(route_pool, ROUTE_CONSTS)
            for c in range(TOPK):
                ins = dve.tensor_tensor(pick[:, c, :, :], iota_row[:, 0:EXPERTS].unsqueeze(1).to_broadcast([P, TILES, EXPERTS]),
                                        topf[:, c, :].unsqueeze(2).to_broadcast([P, TILES, EXPERTS]), ALU.is_equal)
            then(ins, route_step)
            dve.tensor_tensor(both[:], pick[:, 0, :, :], pick[:, 1, :, :], ALU.add).then_inc(pick_done, 1)
            dve.wait_ge(exp_done, 1)
            then(dve.tensor_scalar(weight[:, 0, :], weight[:, 1, :], 1.0, None, ALU.add), route_step)
            then(dve.reciprocal(weight[:, 0, :], weight[:, 0, :]), route_step)
            then(dve.tensor_tensor(weight[:, 1, :], weight[:, 1, :], weight[:, 0, :], ALU.mult), route_step)
            for c in range(TOPK):
                ins = dve.tensor_copy(values[:, c * TILES:(c + 1) * TILES], value[:, 0:TILES])
            then(ins, route_step)
            dve.wait_ge(count_pe, 1)
            then(dve.tensor_copy(total[:], bank[6][:, 0:TILES * EXPERTS].rearrange("p (t e) -> p e t", e=EXPERTS)), route_step)
            flat = total[:].rearrange("p e t -> p (e t)")
            then(dve.tensor_tensor_scan(cum[:].rearrange("p e t -> p (e t)"), flat, zeros[:], 0.0, ALU.add, ALU.add),
                 route_step)
            start, number, tiles_f, ends, shift_e = (small[:, n, :] for n in range(5))
            dve.memset(small[:, 0, 0:1], 0.0)
            then(dve.tensor_copy(small[:, 0, 1:EXPERTS], cum[:, 0:EXPERTS - 1, TILES - 1]), route_step)
            then(dve.tensor_tensor(number, cum[:, :, TILES - 1], start, ALU.subtract), route_step)
            then(dve.tensor_scalar(small_i[:, 0, :], number, float(P - 1), None, ALU.add), route_step)
            then(dve.tensor_scalar(small_i[:, 1, :], small_i[:, 0, :], LOG_P, None, ALU.logical_shift_right), route_step)
            then(dve.tensor_copy(tiles_f, small_i[:, 1, :]), route_step)
            then(dve.tensor_tensor_scan(ends, tiles_f, zeros[:, 0:EXPERTS], 0.0, ALU.add, ALU.add), route_step)
            then(dve.tensor_tensor(shift_e, ends, tiles_f, ALU.subtract), route_step)
            then(dve.scalar_tensor_tensor(out=shift_e, in0=shift_e, scalar=float(P), in1=start, op0=ALU.mult,
                                          op1=ALU.subtract), route_step)
            then(dve.tensor_tensor(cum[:], cum[:], total[:], ALU.subtract), route_step)
            then(dve.tensor_tensor(cum[:], cum[:], shift_e.unsqueeze(2).to_broadcast([P, EXPERTS, TILES]), ALU.add), route_step)
            then(dve.tensor_tensor(slot_m[:], bank[5][:, 0:TILES * EXPERTS].rearrange("p (t e) -> p t e", e=EXPERTS),
                                   cum[:].rearrange("p e t -> p t e"), ALU.add), route_step)
            for c in range(TOPK):
                ins = dve.tensor_tensor(slot_k[:, c, :, :], pick[:, c, :, :], slot_m[:], ALU.mult)
            then(ins, route_step)
            then(dve.tensor_reduce(slot[:], slot_k[:].rearrange("p c t e -> p (c t) e"), AX_X, ALU.add), route_step)
            then(dve.tensor_copy(slot_i[:, 0, :], slot[:]), route_step)
            dve.tensor_scalar(slot_i[:, 1, :], slot_i[:, 0, :], P - 1, None, ALU.bitwise_and)
            then(dve.tensor_scalar(slot_i[:, 2, :], slot_i[:, 0, :], LOG_P, None, ALU.logical_shift_right), route_step)
            then(dve.tensor_copy(slot_f[:], slot_i[:, 1:3, :]), route_step)

            def table_onehots(g, buf, first, last):
                if not first:
                    dve.wait_ge(table_pe, g - TABLE_BUFS + 1)
                for part, width, out_, done in ((1, ETILES, in_col, cols_done), (0, P, in_row, rows_done)):
                    shape = [P, GROUP, width]
                    dve.tensor_tensor(out_[:, buf, :, :], iota_row[:, 0:width].unsqueeze(1).to_broadcast(shape),
                                      slot_f[:, part, bass.ds(g * GROUP, GROUP)].unsqueeze(2).to_broadcast(shape),
                                      ALU.is_equal).then_inc(done, 1)

            table_steps(dve, table_onehots)

            ef = expert_f[0:1, :]
            then(dve.memset(tile_expert[0:1, :], 0), route_step)
            then(dve.tensor_scalar(ef, iota_row[0:1, 0:ETILES], small[0:1, 3, 0:1], None, ALU.is_ge), route_step)
            for e in range(1, EXPERTS - 1):
                then(dve.scalar_tensor_tensor(out=ef, in0=iota_row[0:1, 0:ETILES], scalar=small[0:1, 3, e:e + 1], in1=ef,
                                              op0=ALU.is_ge, op1=ALU.add), route_step)
            then(dve.tensor_copy(tile_expert[0:1, E_LAG:E_LAG + ETILES], ef), route_step)
            dve.wait_ge(table_pe, GROUPS)
            dve.tensor_scalar(token[:], bank[7][:, 0:ETILES], -1.0, 0.0, ALU.add, ALU.max).then_inc(route_done, 1)
            then(dve.tensor_scalar(pad, bank[7][:, 0:ETILES], 0.0, value[:, TILES:TILES + 1],
                                   ALU.is_equal, ALU.mult), route_step)
            dve.scalar_tensor_tensor(out=dest[:], in0=bank[7][:, 0:ETILES], scalar=-1.0, in1=pad,
                                     op0=ALU.add, op1=ALU.add).then_inc(route_done, 1)
            dve.tensor_copy(slot_w[:], bank[7][:, ETILES:2 * ETILES]).then_inc(route_done, 1)

            def expert_step(s, k, have, taken):
                par = k % 2
                o = 1 - par
                if have(1):
                    dve.wait_ge(e_up, s)
                    dve.tensor_copy(gh[:, o, :, :].rearrange("p a (c r) -> p a c r", c=2),
                                    up_banks(o)[:, :, FF // 2:HALF].unsqueeze(1).to_broadcast([P, 2, 2, RANK // 2]))\
                       .then_inc(e_ghs, 1)
                if have(2):
                    dve.wait_ge(e_silu, s - 1)
                    dve.tensor_tensor(hidden[:, par, :].rearrange("p (c f) -> p c f", c=2), up_banks(par)[:, :, 0:FF // 2],
                                      silu[:].rearrange("p (c f) -> p c f", c=2), ALU.mult).then_inc(e_act, 1)
                if have(0):
                    dve.wait_ge(e_hi, s + 1)
                    dve.tensor_tensor(h_lo[:, par, :, :], bank[4][:, 0:D].rearrange("p (i q) -> p i q", i=HC),
                                      h_hi[:, par, :, :].bitcast(F32), ALU.subtract).then_inc(e_lo, 1)
                if have(3):
                    dve.wait_ge(e_y, s - 2)
                    dve.wait_ge(e_gate, s - 2)
                    if have(5):
                        dve.wait_ge(e_out[o], 16 * taken(3, 2))
                    dve.tensor_tensor(y[:, o, :], bank[7][:, 0:D], gate[:, o, :], ALU.mult).then_inc(e_ys, 1)
                if have(1):
                    dve.wait_ge(e_gthi, s)
                    half = slice(RANK, 2 * RANK)
                    dve.tensor_tensor(gt[half, o, :], bank[4][half, D:D + P], gt[half, o, :].bitcast(F32), ALU.subtract)\
                       .then_inc(e_gtlo, 1)
                if have(2):
                    dve.wait_ge(e_ahi, s - 1)
                    dve.tensor_tensor(act_lo[:], bank[3][:, :].rearrange("p (c q) -> p c q", c=FC),
                                      act_hi[:].bitcast(F32), ALU.subtract).then_inc(e_alo, 1)

            expert_steps(dve, expert_step, E_LAG)

        @block.gpsimd
        def _(pool):
            n = 0
            for t_, v in ((ident, 0.0), (headmask, 1.0), (headavg, 1.0 / HEAD)):
                pool.memset(t_[:], v).then_inc(const_set, 1)
                n += 1
            pool.wait_ge(const_set, n)
            pool.affine_select(out=ident[:], in_=ident[:], compare_op=ALU.not_equal, fill=1.0, base=0,
                               pattern=[[-1, P]], channel_multiplier=1).then_inc(const_set, 1)
            for t_ in (headmask, headavg):
                v = t_[:].rearrange("p (g r) -> p g r", r=HEAD)
                pool.affine_select(out=v, in_=v, compare_op=ALU.is_ge, fill=0.0, base=0,
                                   pattern=[[-HEAD, P // HEAD], [0, HEAD]], channel_multiplier=1).then_inc(const_set, 1)
            pool.wait_ge(const_set, n + 3)
            for t_ in (headmask, headavg):
                v = t_[:].rearrange("p (g r) -> p g r", r=HEAD)
                pool.affine_select(out=v, in_=v, compare_op=ALU.is_ge, fill=0.0, base=HEAD - 1,
                                   pattern=[[HEAD, P // HEAD], [0, HEAD]], channel_multiplier=-1).then_inc(const_set, 1)
            assert n + 5 == POOL_CONSTS

            pool.wait_ge(bias_set, 2)
            for b in range(BATCH):
                pool.dma_start(bkv[0:1, b, :], bkv_rows[b:b + 1, :]).then_inc(bkv_in, 16)
            pool.dma_start(bv_dram, bkv_rows[:, D:2 * D]).then_inc(bv_out, 16)
            pool.wait_ge(bv_out, 16)
            pool.dma_start(bv_bc[:], bv_dram.partition_broadcast(P)).then_inc(bv_in, 16)
            pool.wait_ge(bv_in, 16)
            for b in range(BATCH):
                pool.wait_ge(att_ev["gram_v" if b % 2 else "gram_a"], b // 2 + 1)
                for i in range(HC):
                    ins = pool.tensor_scalar(p1[:, b, i, :], bv_bc[:, b, :], xs_raw[:, b, i:i + 1],
                                             sc_cols[:, HC + i, b:b + 1], ALU.mult, ALU.mult)
                ins.then_inc(p1_bias, 1)
            pool.wait_ge(mod_rows, 4)
            row_cb = mod_sb[:, 2 * D:3 * D]
            gates = mod_sb[:, :].rearrange("b (r d) -> b r d", r=4)[:, 0:4:3, :]
            pool.tensor_scalar(row_cb, row_cb, 1.0, None, ALU.add).then_inc(mod_step, 1)
            pool.tensor_scalar(mod_sign[:], gates, 0.0, 2.0, ALU.is_ge, ALU.mult).then_inc(mod_step, 1)
            pool.wait_ge(mod_step, 2)
            pool.tensor_scalar(mod_sign[:], mod_sign[:], -1.0, None, ALU.add).then_inc(mod_step, 1)
            pool.wait_ge(mod_step, 3)
            pool.tensor_tensor(mod_abs[:], mod_sign[:], gates, ALU.mult).then_inc(mod_step, 1)
            pool.wait_ge(mod_step, 4)
            pool.tensor_scalar(mod_abs[:], mod_abs[:], GATE_MIN, None, ALU.max).then_inc(mod_step, 1)
            pool.wait_ge(mod_step, 5)
            pool.tensor_tensor(gates, mod_sign[:], mod_abs[:], ALU.mult).then_inc(mod_step, 1)
            pool.wait_ge(mod_step, 6)
            pool.dma_start(mod_dram.rearrange("b r d -> b (r d)"), mod_sb[:]).then_inc(mod_out, 16)
            pool.wait_ge(mod_out, 16)
            pool.dma_start(ga_bc[:], mod_dram[:, 0, :].partition_broadcast(P)).then_inc(ga_in, 16)

            for b in range(BATCH):
                pool.wait_ge(att_ev["prod"], b + 1)
                pool.tensor_tensor(p1[:, b, 0, :], p1[:, b, 0, :], p1[:, b, 1, :], ALU.add).then_inc(prod_sum, 1)
            pool.wait_ge(stat_step, STAT_SHIFT)
            for b in range(BATCH):
                for j in range(HC):
                    ins = pool.tensor_scalar(p1[:, b, j, 0:P], ident[:], 0.0, stat[:, 7, b, j:j + 1], ALU.mult, ALU.add)
                ins.then_inc(att_ev["ones"], 1)

            pool.wait_ge(att_ev["c0"], BATCH)

            def second_pass(b, k, have):
                t = b * TB + k
                i, o = k % 2, 1 - k % 2
                if have(4):
                    bo, _ = back(b, k, 4)
                    hk = h2[:, i:i + 1, :]
                    pool.wait_ge(d_h2m, t - 3)
                    pool.sem_inc(pool_past, 1)
                    pool.tensor_tensor(hk, hk, sb_bc[:, bass.ds(bo, 1), :], ALU.add).then_inc(d_h2, 1)
                if have(1):
                    bo, ko = back(b, k, 1)
                    xk = xbuf[:, ko % XBUFS:ko % XBUFS + 1, :]
                    pool.wait_ge(d_xhat, t)
                    pool.sem_inc(pool_past, 1)
                    pool.tensor_tensor(xk, xk, c0_bc[:, bass.ds(bo, 1), :], ALU.add).then_inc(d_xc, 1)
                if have(3):
                    if not have(4):
                        pool.wait_ge(sb_in, 16)
                        pool.wait_ge(cb_in, 16)
                    bo, _ = back(b, k, 3)
                    hk = h2[:, o:o + 1, :]
                    pool.wait_ge(d_xn, t - 2)
                    pool.sem_inc(pool_past, 1)
                    pool.tensor_tensor(hk, hk, cb_bc[:, bass.ds(bo, 1), :], ALU.mult).then_inc(d_h2m, 1)

            token_steps(pool, second_pass, 4)

            for i in range(2):
                pool.wait_ge(x2_out[i], 16 * (TILES // 2))
                pool.wait_ge(h2_out[i], 16 * (TILES // 2))
            pool.wait_ge(d_sum, TILES)
            pool.wait_ge(d_wlo, TILES)
            pool.memset(upper[:], 1.0).then_inc(route_pool, 1)
            pool.memset(ones_m[:], 1.0).then_inc(route_pool, 1)
            pool.iota(iota_row[:], pattern=[[1, P]], base=0, channel_multiplier=0, allow_small_or_imprecise_dtypes=True)\
                .then_inc(route_pool, 1)
            pool.wait_ge(route_pool, 3)
            pool.affine_select(out=upper[:], in_=upper[:], compare_op=ALU.is_gt, fill=0.0, base=0,
                               pattern=[[1, P]], channel_multiplier=-1).then_inc(route_pool, 1)
            pool.iota(value[:, 0:TILES].rearrange("p (b k) -> p b k", b=BATCH), pattern=[[SEQ, BATCH], [1, TB]], base=1,
                      channel_multiplier=TB, allow_small_or_imprecise_dtypes=True).then_inc(route_pool, 1)
            pool.iota(value[:, TILES:TILES + 1], pattern=[[0, 1]], base=TOKENS + 1, channel_multiplier=1,
                      allow_small_or_imprecise_dtypes=True).then_inc(route_pool, 1)

            def table_weights(g, buf, first, last):
                pool.wait_ge(cols_done, g + 1)
                pool.sem_inc(pool_past, 1)
                w = weight[:].rearrange("p c t -> p (c t)")[:, bass.ds(g * GROUP, GROUP)]
                pool.tensor_tensor(col_values[:, buf, :, 1, :], in_col[:, buf, :, :],
                                   w.unsqueeze(2).to_broadcast([P, GROUP, ETILES]), ALU.mult)\
                    .then_inc(col_weight_done, 1)

            table_steps(pool, table_weights)

            pool.wait_ge(route_done, 1)
            pool.wait_ge(gb_out, 16 * BATCH)
            pool.wait_ge(pad_out, 16)

            def expert_step(s, k, have, taken):
                par = k % 2
                if have(0):
                    if have(ROWBUFS):
                        pool.wait_ge(e_gate, s - ROWBUFS + 1)
                        pool.wait_ge(e_th, s - ROWBUFS + 1)
                    ix = tok_ix[:, k:k + 1]
                    pool.tensor_copy(ix, token[:, bass.ds(s, 1)]).then_inc(e_tix, 1)
                    pool.wait_ge(e_tix, s + 1)
                    pool.sem_inc(pool_past, 1)
                    pool.indirect_dma_start(rows[:, k, :], None, h2_dram, bass.IndirectOffsetOnAxis(ap=ix, axis=0))\
                        .then_inc(e_rows[k], 16)
                if have(OUT_LAG):
                    o = 1 - par
                    pool.wait_ge(e_ys, s - OUT_LAG + 1)
                    if have(OUT_LAG + 1):
                        pool.wait_ge(e_out[par], 16 * (taken(OUT_LAG + 1, 2) + 1))
                    if not have(OUT_LAG + 1):
                        pool.wait_ge(route_done, 2)
                    ix = dst_ix[:, o:o + 1]
                    pool.tensor_copy(ix, dest[:, bass.ds(s - OUT_LAG, 1)]).then_inc(e_dix, 1)
                    pool.wait_ge(e_dix, s - OUT_LAG + 1)
                    pool.sem_inc(pool_past, 1)
                    pool.indirect_dma_start(out, bass.IndirectOffsetOnAxis(ap=ix, axis=0), y[:, o, :], None,
                                            compute_op=ALU.add).then_inc(e_out[o], 16)

            expert_steps(pool, expert_step, OUT_LAG)


def kernel(**inputs):
    import numpy as np
    import concourse.bacc as bacc
    from concourse.bass_utils import run_bass_kernel_spmd

    a = {n.removeprefix("L0_"): np.asarray(v) for n, v in inputs.items()}

    def halves(m):
        return np.ascontiguousarray(m.reshape(-1, P, m.shape[-1]).transpose(1, 0, 2))

    w_a = a["ffn_W_A"].transpose(2, 0, 1).reshape(HC, P, EXPERTS, 2, RANK // 2).transpose(1, 2, 0, 3, 4)
    w_b = a["ffn_W_B"].transpose(2, 0, 1).reshape(RANK, -1)
    w_up = a["ffn_W_up"].transpose(2, 0, 1).reshape(HC, P, EXPERTS, 2, FF // 2).transpose(1, 2, 0, 3, 4)
    w_ua = np.concatenate([w_up, w_a], axis=4).reshape(P, -1)
    w_down = a["ffn_W_down"].transpose(2, 0, 1).reshape(FC, P, EXPERTS, D).transpose(1, 2, 0, 3).reshape(P, -1)
    arrays = {
        "x": a["attn_x"],
        "c_t": halves(a["c"].T),
        "wmod": halves(a["wmod"]),
        "wqkv_t": halves(a["attn_Wqkv_w"].T),
        "wq": halves(a["attn_Wqkv_w"][0:D]),
        "bq_cols": a["attn_Wqkv_b"][0:D].reshape(HC, P).T,
        "bkv_row": a["attn_Wqkv_b"][D:].reshape(1, 2 * D),
        "gn_cols": np.stack([a["attn_gn_w"].reshape(HC, P).T, a["attn_gn_b"].reshape(HC, P).T], axis=1),
        "wo_t": halves(a["attn_out_w"].T),
        "out_b": a["attn_out_b"],
        "wg": np.concatenate([w_ua, np.concatenate([w_b, w_b], axis=0)], axis=1),
        "wd": w_down,
    }
    nc = bacc.Bacc("TRN2", target_bir_lowering=False, num_devices=1)
    args = {}
    for name, v in arrays.items():
        arrays[name] = v = np.ascontiguousarray(v)
        args[name] = nc.dram_tensor(f"in_{name}", v.shape, mybir.dt.from_np(v.dtype), kind="ExternalInput").ap()
    args["out"] = nc.dram_tensor("out_0", (TOKENS + P, D), F32, kind="ExternalOutput").ap()
    build(nc, **args)
    r = run_bass_kernel_spmd(nc, [{f"in_{n}": v for n, v in arrays.items()}], core_ids=[0])
    return r.results[0]["out_0"][0:TOKENS].reshape(BATCH, SEQ, D)
```
